# Optimizing a Trainium2 kernel written in Bass

```python
import numpy as np
import jax
import jax.numpy as jnp

def _softmax(x, axis=-1):
    return jax.nn.softmax(x, axis=axis)

def _gelu(x):
    return jax.nn.gelu(x, approximate=True)

def _silu(x):
    return jax.nn.silu(x)

def _sigmoid(x):
    return jax.nn.sigmoid(x)

def _layernorm(x, axis=-1, eps=1e-05):
    m = jnp.mean(x, axis=axis, keepdims=True)
    v = jnp.var(x, axis=axis, keepdims=True)
    return (x - m) / jnp.sqrt(v + eps)

def _scatter_add(tgt, idx, src, axis=0):
    return tgt.at[idx].add(src)

def _segment_sum(src, seg, n):
    return jax.ops.segment_sum(src, seg, n)
kernel_name = 'mk_gps_d2_gnn_r32_60f088'

def setup_inputs(seed: int=0):
    np.random.seed(seed)
    _w = jnp.asarray

    def _rec_inputs():
        import jax
        import jax.numpy as jnp
        _gk = jax.random.key(seed)
        x = -0.0003713 + 1 * jax.random.normal(jax.random.fold_in(_gk, 1), (3125, 256), jnp.float32)
        src = jax.random.randint(jax.random.fold_in(_gk, 2), (50000,), 0, 3125, jnp.int32)
        dst = jnp.minimum((3125 * jax.random.uniform(jax.random.fold_in(_gk, 3), (50000,)) ** 2.0).astype(jnp.int32), 99999)
        _o = jnp.argsort(dst, stable=True)
        src = src[_o]
        dst = dst[_o]
        edge_type_6 = jax.random.randint(jax.random.fold_in(_gk, 13), (50000,), 0, 6, jnp.int32)
        edge_weight = jax.random.uniform(jax.random.fold_in(_gk, 14), (50000,), jnp.float32, 0.0, 0.999999)
        return (x, src, dst, edge_type_6, edge_weight)
    x, src, dst, edge_type_6, edge_weight = _rec_inputs()

    def _L0_gnn_setup():
        import jax, jax.numpy as jnp
        import numpy as np
        N_NODES = 50000
        N_EDGES = 25000
        IN_DIM = 256
        NUM_HEADS = 4
        HEAD_DIM = 64
        EPS = 1e-05

        def _layernorm(h, g, b):
            mu = h.mean(axis=-1, keepdims=True)
            var = ((h - mu) ** 2).mean(axis=-1, keepdims=True)
            return (h - mu) * jax.lax.rsqrt(var + EPS) * g + b
        key = jax.random.key(seed)
        ks = jax.random.split(key, 5)
        x = jax.random.normal(ks[0], (N_NODES, IN_DIM), dtype=jnp.float32)
        rows = jax.random.randint(ks[1], (N_EDGES,), 0, N_NODES, dtype=jnp.int32)
        cols = jax.random.randint(ks[2], (N_EDGES,), 0, N_NODES, dtype=jnp.int32)
        vals = jax.random.uniform(ks[3], (N_EDGES,), dtype=jnp.float32)
        W = jax.random.normal(ks[4], (NUM_HEADS, IN_DIM, HEAD_DIM), dtype=jnp.float32) / np.sqrt(IN_DIM)
        bias = jnp.zeros((NUM_HEADS, HEAD_DIM), dtype=jnp.float32)
        ln1_g = jnp.ones((NUM_HEADS, HEAD_DIM), dtype=jnp.float32)
        ln1_b = jnp.zeros((NUM_HEADS, HEAD_DIM), dtype=jnp.float32)
        ln2_g = jnp.ones((IN_DIM,), dtype=jnp.float32)
        ln2_b = jnp.zeros((IN_DIM,), dtype=jnp.float32)
        return {'x': x, 'rows': rows, 'cols': cols, 'vals': vals, 'W': W, 'bias': bias, 'ln1_g': ln1_g, 'ln1_b': ln1_b, 'ln2_g': ln2_g, 'ln2_b': ln2_b}
    _L0_gnn_all = _L0_gnn_setup()
    _L0_gnn_in = {k: v for k, v in _L0_gnn_all.items() if k in ('W', 'bias', 'ln1_g', 'ln1_b', 'ln2_g', 'ln2_b')}
    del _L0_gnn_all

    def _L0_mix_setup():
        import jax, jax.numpy as jnp
        import numpy as np
        HEADS = 8
        DIM_HEAD = 32
        SCALE = DIM_HEAD ** (-0.5)
        EPS = 1e-05

        def _layernorm_gamma(x, gamma):
            mu = jnp.mean(x, axis=-1, keepdims=True)
            var = jnp.var(x, axis=-1, keepdims=True)
            return (x - mu) * jax.lax.rsqrt(var + EPS) * gamma
        key = jax.random.key(seed)
        k1, k2, k3 = jax.random.split(key, 3)
        B, N, D = (8, 512, 256)
        hidden = HEADS * DIM_HEAD
        x = jax.random.normal(k1, (B, N, D), dtype=jnp.float32)
        Wqkv = jax.random.normal(k2, (D, 3 * hidden), dtype=jnp.float32) * D ** (-0.5)
        Wout = jax.random.normal(k3, (hidden, D), dtype=jnp.float32) * hidden ** (-0.5)
        gamma = jnp.ones((D,), dtype=jnp.float32)
        return {'x': x, 'Wqkv': Wqkv, 'Wout': Wout, 'gamma': gamma}
    _L0_mix_all = _L0_mix_setup()
    _L0_mix_in = {k: v for k, v in _L0_mix_all.items() if k in ('Wqkv', 'Wout', 'gamma')}
    del _L0_mix_all

    def _L0_ffn_setup():
        import jax, jax.numpy as jnp
        import numpy as np
        BN_EPS = 0.001

        def _bn(h, g, b, m, v):
            return g * (h - m) * jax.lax.rsqrt(v + BN_EPS) + b
        key = jax.random.key(seed)
        ks = jax.random.split(key, 8)
        B, F, Df = (256, 64, 256)
        E, H, D = (8, 256, 256)
        s1 = 1.0 / np.sqrt(Df)
        s2 = 1.0 / np.sqrt(H)
        return {'x': jax.random.normal(ks[0], (B, F, Df), jnp.float32), 'Wr': jax.random.normal(ks[1], (Df, E), jnp.float32) * s1, 'br': jnp.zeros((E,), jnp.float32), 'W1': jax.random.normal(ks[2], (E, Df, H), jnp.float32) * s1, 'b1': jnp.zeros((E, H), jnp.float32), 'g1': jnp.ones((E, H), jnp.float32), 'be1': jnp.zeros((E, H), jnp.float32), 'm1': jnp.zeros((E, H), jnp.float32), 'v1': jnp.ones((E, H), jnp.float32), 'W2': jax.random.normal(ks[3], (E, H, H), jnp.float32) * s2, 'b2': jnp.zeros((E, H), jnp.float32), 'g2': jnp.ones((E, H), jnp.float32), 'be2': jnp.zeros((E, H), jnp.float32), 'm2': jnp.zeros((E, H), jnp.float32), 'v2': jnp.ones((E, H), jnp.float32), 'Wo': jax.random.normal(ks[4], (E, H, D), jnp.float32) * s2, 'bo': jnp.zeros((E, D), jnp.float32)}
    _L0_ffn_all = _L0_ffn_setup()
    _L0_ffn_in = {k: v for k, v in _L0_ffn_all.items() if k in ('Wr', 'br', 'W1', 'b1', 'g1', 'be1', 'm1', 'v1', 'W2', 'b2', 'g2', 'be2', 'm2', 'v2', 'Wo', 'bo')}
    del _L0_ffn_all

    def _L1_gnn_setup():
        import jax, jax.numpy as jnp
        import numpy as np
        N_NODES = 50000
        N_EDGES = 12500
        D_IN = 256
        D_OUT = 256
        N_REL = 6
        N_HEADS = 4
        key = jax.random.key(seed)
        ks = jax.random.split(key, 12)
        s_in = 1.0 / np.sqrt(D_IN)
        s_out = 1.0 / np.sqrt(D_OUT)
        return {'x': jax.random.normal(ks[0], (N_NODES, D_IN), dtype=jnp.float32), 'edge_index': jax.random.randint(ks[1], (2, N_EDGES), 0, N_NODES, dtype=jnp.int64), 'edge_types': jax.random.randint(ks[2], (N_EDGES,), 0, N_REL, dtype=jnp.int64), 'W': jax.random.uniform(ks[3], (N_REL, D_IN, D_OUT), jnp.float32, -s_in, s_in), 'b': jax.random.uniform(ks[4], (N_REL, D_OUT), jnp.float32, -s_in, s_in), 'in_proj_w': jax.random.uniform(ks[5], (3 * D_OUT, D_OUT), jnp.float32, -s_out, s_out), 'in_proj_b': jnp.zeros((3 * D_OUT,), jnp.float32), 'attn_out_w': jax.random.uniform(ks[6], (D_OUT, D_OUT), jnp.float32, -s_out, s_out), 'attn_out_b': jnp.zeros((D_OUT,), jnp.float32), 'proj_w': jax.random.uniform(ks[7], (D_OUT, D_OUT), jnp.float32, -s_out, s_out), 'proj_b': jax.random.uniform(ks[8], (D_OUT,), jnp.float32, -s_out, s_out)}
    _L1_gnn_all = _L1_gnn_setup()
    _L1_gnn_in = {k: v for k, v in _L1_gnn_all.items() if k in ('W', 'b', 'in_proj_w', 'in_proj_b', 'attn_out_w', 'attn_out_b', 'proj_w', 'proj_b')}
    del _L1_gnn_all

    def _L1_mix_setup():
        import jax, jax.numpy as jnp
        import numpy as np
        B, N, C = (8, 256, 256)
        H, D, S = (8, 32, 32)
        HID = 4 * C

        def layernorm(x, w, b, eps=1e-05):
            mu = jnp.mean(x, axis=-1, keepdims=True)
            var = jnp.mean(jnp.square(x - mu), axis=-1, keepdims=True)
            return (x - mu) * jax.lax.rsqrt(var + eps) * w + b

        def linear_no_attn(x, Wx, bx, Wq, Wk, Wv, Wo, bo):
            x_mid = x @ Wx.T + bx
            x_mid = x_mid.reshape(x.shape[0], x.shape[1], H, D).transpose(0, 2, 1, 3)
            q = jax.nn.softmax(x_mid @ Wq.T, axis=-1)
            k = jax.nn.softmax(x_mid @ Wk.T, axis=-2)
            v = x_mid @ Wv.T
            kv = jnp.einsum('bhns,bhnd->bhsd', k, v)
            qkv = jnp.einsum('bhns,bhsd->bhnd', q, kv)
            qkv = qkv.transpose(0, 2, 1, 3).reshape(x.shape[0], x.shape[1], H * D)
            return qkv @ Wo.T + bo
        key = jax.random.key(seed)
        ks = jax.random.split(key, 16)
        s = lambda fan: 1.0 / np.sqrt(fan)
        return {'fx': jax.random.normal(ks[0], (B, N, C), jnp.float32), 'ln1_w': jnp.ones((C,), jnp.float32), 'ln1_b': jnp.zeros((C,), jnp.float32), 'Wx': jax.random.uniform(ks[1], (C, C), jnp.float32, -s(C), s(C)), 'bx': jax.random.uniform(ks[2], (C,), jnp.float32, -s(C), s(C)), 'Wq': jax.random.uniform(ks[3], (S, D), jnp.float32, -s(D), s(D)), 'Wk': jax.random.uniform(ks[4], (S, D), jnp.float32, -s(D), s(D)), 'Wv': jax.random.uniform(ks[5], (D, D), jnp.float32, -s(D), s(D)), 'Wo': jax.random.uniform(ks[6], (C, C), jnp.float32, -s(C), s(C)), 'bo': jax.random.uniform(ks[7], (C,), jnp.float32, -s(C), s(C)), 'ln2_w': jnp.ones((C,), jnp.float32), 'ln2_b': jnp.zeros((C,), jnp.float32), 'W1': jax.random.uniform(ks[8], (HID, C), jnp.float32, -s(C), s(C)), 'b1': jax.random.uniform(ks[9], (HID,), jnp.float32, -s(C), s(C)), 'W2': jax.random.uniform(ks[10], (C, HID), jnp.float32, -s(HID), s(HID)), 'b2': jax.random.uniform(ks[11], (C,), jnp.float32, -s(HID), s(HID))}
    _L1_mix_all = _L1_mix_setup()
    _L1_mix_in = {k: v for k, v in _L1_mix_all.items() if k in ('ln1_w', 'ln1_b', 'Wx', 'bx', 'Wq', 'Wk', 'Wv', 'Wo', 'bo', 'ln2_w', 'ln2_b', 'W1', 'b1', 'W2', 'b2')}
    del _L1_mix_all

    def _L1_ffn_setup():
        import jax, jax.numpy as jnp
        import numpy as np
        B, K, D = (512, 16, 256)
        E = 32
        H = int(D * 0.25)
        key = jax.random.key(seed)
        ks = jax.random.split(key, 7)
        d_rs = D ** (-0.5)
        h_rs = H ** (-0.5)
        x = jax.random.normal(ks[0], (B, K, D), dtype=jnp.float32)
        router_w = jax.random.uniform(ks[1], (E, D), jnp.float32, -d_rs, d_rs)
        router_b = jax.random.uniform(ks[2], (E,), jnp.float32, -d_rs, d_rs)
        W1 = jax.random.uniform(ks[3], (E, D, H), jnp.float32, -h_rs, h_rs)
        b1 = jax.random.uniform(ks[4], (E, H), jnp.float32, -h_rs, h_rs)
        W2 = jax.random.uniform(ks[5], (E, H, D), jnp.float32, -d_rs, d_rs)
        b2 = jax.random.uniform(ks[6], (E, D), jnp.float32, -d_rs, d_rs)
        return {'x': x, 'router_w': router_w, 'router_b': router_b, 'W1': W1, 'b1': b1, 'W2': W2, 'b2': b2}
    _L1_ffn_all = _L1_ffn_setup()
    _L1_ffn_in = {k: v for k, v in _L1_ffn_all.items() if k in ('router_w', 'router_b', 'W1', 'b1', 'W2', 'b2')}
    del _L1_ffn_all
    return {'x': x, 'src': src, 'dst': dst, 'edge_type_6': edge_type_6, 'edge_weight': edge_weight, 'L0_gnn_W': _L0_gnn_in['W'], 'L0_gnn_bias': _L0_gnn_in['bias'], 'L0_gnn_ln1_g': _L0_gnn_in['ln1_g'], 'L0_gnn_ln1_b': _L0_gnn_in['ln1_b'], 'L0_gnn_ln2_g': _L0_gnn_in['ln2_g'], 'L0_gnn_ln2_b': _L0_gnn_in['ln2_b'], 'L0_mix_Wqkv': _L0_mix_in['Wqkv'], 'L0_mix_Wout': _L0_mix_in['Wout'], 'L0_mix_gamma': _L0_mix_in['gamma'], 'L0_ffn_Wr': _L0_ffn_in['Wr'], 'L0_ffn_br': _L0_ffn_in['br'], 'L0_ffn_W1': _L0_ffn_in['W1'], 'L0_ffn_b1': _L0_ffn_in['b1'], 'L0_ffn_g1': _L0_ffn_in['g1'], 'L0_ffn_be1': _L0_ffn_in['be1'], 'L0_ffn_m1': _L0_ffn_in['m1'], 'L0_ffn_v1': _L0_ffn_in['v1'], 'L0_ffn_W2': _L0_ffn_in['W2'], 'L0_ffn_b2': _L0_ffn_in['b2'], 'L0_ffn_g2': _L0_ffn_in['g2'], 'L0_ffn_be2': _L0_ffn_in['be2'], 'L0_ffn_m2': _L0_ffn_in['m2'], 'L0_ffn_v2': _L0_ffn_in['v2'], 'L0_ffn_Wo': _L0_ffn_in['Wo'], 'L0_ffn_bo': _L0_ffn_in['bo'], 'L1_gnn_W': _L1_gnn_in['W'], 'L1_gnn_b': _L1_gnn_in['b'], 'L1_gnn_in_proj_w': _L1_gnn_in['in_proj_w'], 'L1_gnn_in_proj_b': _L1_gnn_in['in_proj_b'], 'L1_gnn_attn_out_w': _L1_gnn_in['attn_out_w'], 'L1_gnn_attn_out_b': _L1_gnn_in['attn_out_b'], 'L1_gnn_proj_w': _L1_gnn_in['proj_w'], 'L1_gnn_proj_b': _L1_gnn_in['proj_b'], 'L1_mix_ln1_w': _L1_mix_in['ln1_w'], 'L1_mix_ln1_b': _L1_mix_in['ln1_b'], 'L1_mix_Wx': _L1_mix_in['Wx'], 'L1_mix_bx': _L1_mix_in['bx'], 'L1_mix_Wq': _L1_mix_in['Wq'], 'L1_mix_Wk': _L1_mix_in['Wk'], 'L1_mix_Wv': _L1_mix_in['Wv'], 'L1_mix_Wo': _L1_mix_in['Wo'], 'L1_mix_bo': _L1_mix_in['bo'], 'L1_mix_ln2_w': _L1_mix_in['ln2_w'], 'L1_mix_ln2_b': _L1_mix_in['ln2_b'], 'L1_mix_W1': _L1_mix_in['W1'], 'L1_mix_b1': _L1_mix_in['b1'], 'L1_mix_W2': _L1_mix_in['W2'], 'L1_mix_b2': _L1_mix_in['b2'], 'L1_ffn_router_w': _L1_ffn_in['router_w'], 'L1_ffn_router_b': _L1_ffn_in['router_b'], 'L1_ffn_W1': _L1_ffn_in['W1'], 'L1_ffn_b1': _L1_ffn_in['b1'], 'L1_ffn_W2': _L1_ffn_in['W2'], 'L1_ffn_b2': _L1_ffn_in['b2']}

def reference(x, src, dst, edge_type_6, edge_weight, L0_gnn_W, L0_gnn_bias, L0_gnn_ln1_g, L0_gnn_ln1_b, L0_gnn_ln2_g, L0_gnn_ln2_b, L0_mix_Wqkv, L0_mix_Wout, L0_mix_gamma, L0_ffn_Wr, L0_ffn_br, L0_ffn_W1, L0_ffn_b1, L0_ffn_g1, L0_ffn_be1, L0_ffn_m1, L0_ffn_v1, L0_ffn_W2, L0_ffn_b2, L0_ffn_g2, L0_ffn_be2, L0_ffn_m2, L0_ffn_v2, L0_ffn_Wo, L0_ffn_bo, L1_gnn_W, L1_gnn_b, L1_gnn_in_proj_w, L1_gnn_in_proj_b, L1_gnn_attn_out_w, L1_gnn_attn_out_b, L1_gnn_proj_w, L1_gnn_proj_b, L1_mix_ln1_w, L1_mix_ln1_b, L1_mix_Wx, L1_mix_bx, L1_mix_Wq, L1_mix_Wk, L1_mix_Wv, L1_mix_Wo, L1_mix_bo, L1_mix_ln2_w, L1_mix_ln2_b, L1_mix_W1, L1_mix_b1, L1_mix_W2, L1_mix_b2, L1_ffn_router_w, L1_ffn_router_b, L1_ffn_W1, L1_ffn_b1, L1_ffn_W2, L1_ffn_b2):
    import jax
    import jax.numpy as jnp

    def _L0_gnn_ref(x, rows, cols, vals, W, bias, ln1_g, ln1_b, ln2_g, ln2_b):
        import jax, jax.numpy as jnp
        import numpy as np
        N_NODES = 50000
        N_EDGES = 25000
        IN_DIM = 256
        NUM_HEADS = 4
        HEAD_DIM = 64
        EPS = 1e-05

        def _layernorm(h, g, b):
            mu = h.mean(axis=-1, keepdims=True)
            var = ((h - mu) ** 2).mean(axis=-1, keepdims=True)
            return (h - mu) * jax.lax.rsqrt(var + EPS) * g + b
        n = x.shape[0]
        h = jnp.einsum('ni,hio->nho', x, W)
        msg = vals[:, None, None] * h[cols]
        agg = jax.ops.segment_sum(msg, rows, num_segments=n)
        agg = agg + bias[None, :, :]
        agg = _layernorm(agg, ln1_g[None], ln1_b[None])
        hcat = agg.reshape(n, NUM_HEADS * HEAD_DIM)
        return _layernorm(hcat, ln2_g, ln2_b)

    def _L0_mix_ref(x, Wqkv, Wout, gamma):
        import jax, jax.numpy as jnp
        import numpy as np
        HEADS = 8
        DIM_HEAD = 32
        SCALE = DIM_HEAD ** (-0.5)
        EPS = 1e-05

        def _layernorm_gamma(x, gamma):
            mu = jnp.mean(x, axis=-1, keepdims=True)
            var = jnp.var(x, axis=-1, keepdims=True)
            return (x - mu) * jax.lax.rsqrt(var + EPS) * gamma
        B, N, D = x.shape
        qkv = x @ Wqkv
        q, k, v = jnp.split(qkv, 3, axis=-1)

        def to_heads(t):
            return t.reshape(B, N, HEADS, DIM_HEAD).transpose(0, 2, 1, 3)
        q, k, v = map(to_heads, (q, k, v))
        q = jax.nn.softmax(q, axis=-1) * SCALE
        k = jax.nn.softmax(k, axis=2)
        context = jnp.einsum('bhnd,bhne->bhde', k, v)
        out = jnp.einsum('bhde,bhnd->bhne', context, q)
        out = out.transpose(0, 2, 1, 3).reshape(B, N, HEADS * DIM_HEAD)
        out = out @ Wout
        return _layernorm_gamma(out, gamma)

    def _L0_ffn_ref(x, Wr, br, W1, b1, g1, be1, m1, v1, W2, b2, g2, be2, m2, v2, Wo, bo):
        import jax, jax.numpy as jnp
        import numpy as np
        BN_EPS = 0.001

        def _bn(h, g, b, m, v):
            return g * (h - m) * jax.lax.rsqrt(v + BN_EPS) + b
        feat = jnp.mean(x, axis=0)
        w = jax.nn.softmax(feat @ Wr + br, axis=-1)
        h = jnp.einsum('bfd,edh->bfeh', x, W1) + b1
        h = jax.nn.relu(_bn(h, g1, be1, m1, v1))
        h = jnp.einsum('bfeh,ehk->bfek', h, W2) + b2
        h = jax.nn.relu(_bn(h, g2, be2, m2, v2))
        y = jnp.einsum('bfeh,ehd->bfed', h, Wo) + bo
        return jnp.einsum('bfed,fe->bfd', y, w)

    def _L1_gnn_ref(x, edge_index, edge_types, W, b, in_proj_w, in_proj_b, attn_out_w, attn_out_b, proj_w, proj_b):
        import jax, jax.numpy as jnp
        import numpy as np
        N_NODES = 50000
        N_EDGES = 12500
        D_IN = 256
        D_OUT = 256
        N_REL = 6
        N_HEADS = 4
        num_nodes = x.shape[0]
        hd = D_OUT // N_HEADS
        transformed = jnp.einsum('ni,rio->rno', x, W) + b[:, None, :]
        src, dst = (edge_index[0], edge_index[1])
        msgs = transformed[edge_types, src]
        agg = jnp.zeros((N_REL, num_nodes, D_OUT), x.dtype).at[edge_types, dst].add(msgs)
        s = jnp.transpose(agg, (1, 0, 2))
        qkv = s @ in_proj_w.T + in_proj_b
        q, k, v = jnp.split(qkv, 3, axis=-1)
        q = q.reshape(num_nodes, N_REL, N_HEADS, hd)
        k = k.reshape(num_nodes, N_REL, N_HEADS, hd)
        v = v.reshape(num_nodes, N_REL, N_HEADS, hd)
        scores = jnp.einsum('nrhd,nshd->nhrs', q, k) / np.sqrt(hd)
        probs = jax.nn.softmax(scores, axis=-1)
        attn = jnp.einsum('nhrs,nshd->nrhd', probs, v).reshape(num_nodes, N_REL, D_OUT)
        attended = attn @ attn_out_w.T + attn_out_b
        aggregated_output = attended.mean(axis=1)
        out = (aggregated_output + x[:, :D_OUT]) @ proj_w.T + proj_b
        return out

    def _L1_mix_ref(fx, ln1_w, ln1_b, Wx, bx, Wq, Wk, Wv, Wo, bo, ln2_w, ln2_b, W1, b1, W2, b2):
        import jax, jax.numpy as jnp
        import numpy as np
        B, N, C = (8, 256, 256)
        H, D, S = (8, 32, 32)
        HID = 4 * C

        def layernorm(x, w, b, eps=1e-05):
            mu = jnp.mean(x, axis=-1, keepdims=True)
            var = jnp.mean(jnp.square(x - mu), axis=-1, keepdims=True)
            return (x - mu) * jax.lax.rsqrt(var + eps) * w + b

        def linear_no_attn(x, Wx, bx, Wq, Wk, Wv, Wo, bo):
            x_mid = x @ Wx.T + bx
            x_mid = x_mid.reshape(x.shape[0], x.shape[1], H, D).transpose(0, 2, 1, 3)
            q = jax.nn.softmax(x_mid @ Wq.T, axis=-1)
            k = jax.nn.softmax(x_mid @ Wk.T, axis=-2)
            v = x_mid @ Wv.T
            kv = jnp.einsum('bhns,bhnd->bhsd', k, v)
            qkv = jnp.einsum('bhns,bhsd->bhnd', q, kv)
            qkv = qkv.transpose(0, 2, 1, 3).reshape(x.shape[0], x.shape[1], H * D)
            return qkv @ Wo.T + bo
        h = linear_no_attn(layernorm(fx, ln1_w, ln1_b), Wx, bx, Wq, Wk, Wv, Wo, bo) + fx
        y = layernorm(h, ln2_w, ln2_b)
        y = jax.nn.gelu(y @ W1.T + b1, approximate=False)
        y = y @ W2.T + b2
        return y + h

    def _L1_ffn_ref(x, router_w, router_b, W1, b1, W2, b2):
        import jax, jax.numpy as jnp
        import numpy as np
        B, K, D = (512, 16, 256)
        E = 32
        H = int(D * 0.25)
        xf = x.reshape(-1, D)
        logits = xf @ router_w.T + router_b
        idx = jnp.argmax(logits, axis=-1)
        w1t = jnp.take(W1, idx, axis=0)
        h = jnp.einsum('nd,ndh->nh', xf, w1t) + jnp.take(b1, idx, axis=0)
        h = jax.nn.relu(h)
        w2t = jnp.take(W2, idx, axis=0)
        out = jnp.einsum('nh,nhd->nd', h, w2t) + jnp.take(b2, idx, axis=0)
        out = jax.nn.relu(out)
        return out.reshape(x.shape)
    edge_index = jnp.stack([src, dst])
    xn = _layernorm(x, axis=-1)
    x = x + _L0_gnn_ref(xn, src, dst, edge_weight, L0_gnn_W, L0_gnn_bias, L0_gnn_ln1_g, L0_gnn_ln1_b, L0_gnn_ln2_g, L0_gnn_ln2_b) + _L0_mix_ref(xn[None], L0_mix_Wqkv, L0_mix_Wout, L0_mix_gamma)[0]
    x = x + _L0_ffn_ref(_layernorm(x, axis=-1)[None], L0_ffn_Wr, L0_ffn_br, L0_ffn_W1, L0_ffn_b1, L0_ffn_g1, L0_ffn_be1, L0_ffn_m1, L0_ffn_v1, L0_ffn_W2, L0_ffn_b2, L0_ffn_g2, L0_ffn_be2, L0_ffn_m2, L0_ffn_v2, L0_ffn_Wo, L0_ffn_bo)[0]
    xn = _layernorm(x, axis=-1)
    x = x + _L1_gnn_ref(xn, edge_index, edge_type_6, L1_gnn_W, L1_gnn_b, L1_gnn_in_proj_w, L1_gnn_in_proj_b, L1_gnn_attn_out_w, L1_gnn_attn_out_b, L1_gnn_proj_w, L1_gnn_proj_b) + _L1_mix_ref(xn[None], L1_mix_ln1_w, L1_mix_ln1_b, L1_mix_Wx, L1_mix_bx, L1_mix_Wq, L1_mix_Wk, L1_mix_Wv, L1_mix_Wo, L1_mix_bo, L1_mix_ln2_w, L1_mix_ln2_b, L1_mix_W1, L1_mix_b1, L1_mix_W2, L1_mix_b2)[0]
    x = x + _L1_ffn_ref(_layernorm(x, axis=-1)[None], L1_ffn_router_w, L1_ffn_router_b, L1_ffn_W1, L1_ffn_b1, L1_ffn_W2, L1_ffn_b2)[0]
    return x

_drawn_inputs = setup_inputs


def setup_inputs(seed=0):
    import zlib

    import numpy as np

    out = dict(_drawn_inputs(seed))
    spreads = {'L0_gnn_bias': (0.0, 0.1),
     'L0_gnn_ln1_g': (1.0, 0.2),
     'L0_gnn_ln1_b': (0.0, 0.1),
     'L0_gnn_ln2_g': (1.0, 0.2),
     'L0_gnn_ln2_b': (0.0, 0.1),
     'L0_mix_gamma': (1.0, 0.2),
     'L0_ffn_br': (0.0, 0.342),
     'L0_ffn_b1': (0.0, 0.433),
     'L0_ffn_g1': (1.0, 0.2),
     'L0_ffn_be1': (0.0, 0.458),
     'L0_ffn_m1': (0.0, 0.446),
     'L0_ffn_v1': (1.0, 0.6),
     'L0_ffn_b2': (0.0, 0.331),
     'L0_ffn_g2': (1.0, 0.2),
     'L0_ffn_be2': (0.0, 0.34),
     'L0_ffn_m2': (0.0, 0.33),
     'L0_ffn_v2': (1.0, 0.6),
     'L0_ffn_bo': (0.0, 0.1),
     'L1_gnn_in_proj_b': (0.0, 0.525),
     'L1_gnn_attn_out_b': (0.0, 0.306),
     'L1_mix_ln1_w': (1.0, 0.6),
     'L1_mix_ln1_b': (0.0, 0.727),
     'L1_mix_ln2_w': (1.0, 0.6),
     'L1_mix_ln2_b': (0.0, 0.8)}
    factors = {'L1_gnn_b': 4.178,
     'L1_gnn_proj_b': 3.877,
     'L1_mix_bx': 8.0,
     'L1_mix_Wq': 8.0,
     'L1_mix_Wk': 8.0,
     'L1_mix_bo': 3.576,
     'L1_mix_b1': 8.0,
     'L1_mix_b2': 6.172,
     'L1_ffn_router_b': 2.975,
     'L1_ffn_b1': 8.0,
     'L1_ffn_b2': 6.178}
    for name, (base, spread) in spreads.items():
        noise = np.random.default_rng([zlib.crc32(name.encode()), seed]).standard_normal(out[name].shape)
        drawn = base * np.exp(spread * noise) if base else spread * noise
        out[name] = jnp.asarray(drawn.astype(out[name].dtype))
    for name, factor in factors.items():
        out[name] = (out[name] * factor).astype(out[name].dtype)
    return out
```

```python
from contextlib import ExitStack

import numpy as np
import concourse.bass as bass
from concourse import mybir

F32 = mybir.dt.float32
I32 = mybir.dt.int32
U32 = mybir.dt.uint32
ALU = mybir.AluOpType
ACT = mybir.ActivationFunctionType
AX = mybir.AxisListType

NODES = 3125
D = 256
P = 125
TILES = NODES // P
CHUNK = 625
CHUNKS = NODES // CHUNK
HALVES = ((0, 313), (313, 312))
TPC = CHUNK // P
EDGES = 50000
ETILES = EDGES // P
EB = 8
EROWS = 100
EBLK = ETILES // EROWS
REL = 6
HEADS = 4
HD = D // HEADS
MIX_HEADS = 8
MHD = D // MIX_HEADS
MOE = 8
EXP = 32
EH = 64
HID = 1024
EPS = 1e-5
BN_EPS = 1e-3
TABLES = 2
AGG_ROWS = (3328, 18944)
SEGS = (NODES, REL * NODES)
LOOK = 4


def gps_two_layers(nc, A, out):
    ctx = ExitStack()
    with ctx:
        def sb(name, shape, dt=F32):
            return ctx.enter_context(nc.sbuf_tensor(name, shape, dt))

        def sem(name):
            return ctx.enter_context(nc.semaphore(name))

        def dram(name, shape, dt=F32):
            return nc.dram_tensor(name, shape, dt, kind="Internal").ap()

        ps = [ctx.enter_context(nc.psum_tensor(f"bank{i}", [128, 512], F32)) for i in range(8)]

        x_cur = sb("x_cur", [P, TILES * D])
        xn_whole = sb("xn", [128, TILES * D])
        xn = xn_whole[0:P, :]
        xnT = sb("xnT", [128, 2, NODES])
        rows = sb("rows", [P, TILES * D])
        ident = sb("ident", [128, 128])
        earlier = sb("earlier", [P, P])
        lane = sb("lane", [128, 1])
        lane_i = sb("lane_i", [128, 1], I32)
        neghalf = sb("neghalf", [128, 32])
        zeros = sb("zeros", [128, D])
        key_col = [sb(f"key_col{i}", [P, ETILES]) for i in range(2)]
        spare_gap = [sb(f"spare_gap{i}", [P, ETILES]) for i in range(2)]
        gather_col = [sb(f"gather_col{i}", [P, ETILES], I32) for i in range(2)]
        weight_col = sb("weight_col", [P, ETILES])
        ARENA = 23400
        arena = sb("arena", [128, ARENA])

        xn_table = dram("xn_table", [NODES, D])
        rel_table = dram("rel_table", [REL * NODES, D])
        agg = [[dram(f"agg{la}_{k}", [AGG_ROWS[la], D]) for k in range(TABLES)] for la in range(2)]
        key_row = [dram(f"key_row{la}", [EDGES]) for la in range(2)]

        class Counted:

            def __init__(self, handle, base):
                self.sem, self.base = handle, base

        counts = {}

        def counted(name, total):
            if name not in counts:
                counts[name] = [sem(name), 0]
            handle, base = counts[name]
            counts[name][1] += total
            return Counted(handle, base)

        class Carver:

            def __init__(self):
                self.at = 0

            def __call__(self, parts, cols, dt=F32, **split):
                a = arena[0:parts, self.at:self.at + cols]
                self.at += cols
                assert self.at <= ARENA, self.at
                return a if dt == F32 else a.bitcast(dt)

        phase_done = sem("phase_done")
        engines = 5

        def phase_end(e, n):
            e.drain().then_inc(phase_done, 1)
            e.wait_ge(phase_done, engines * n)

        paces = {n: sem(f"pace_{n}") for n in ("act", "pool", "dve", "pe")}

        def own(e, name):
            e.sem_inc(paces[name], 1)

        def tiles(e, body):
            with e.Fori(0, TILES // 2) as k:
                body(2 * k, 0, k)
                body(2 * k + 1, 1, k)
            body(TILES - 1, 0, TILES // 2)

        def tiles_lagged(e, ahead, behind):
            ahead(0, 0, 0)
            with e.Fori(0, TILES // 2) as k:
                ahead(2 * k + 1, 1, k)
                behind(2 * k, 0, k)
                ahead(2 * k + 2, 0, k + 1)
                behind(2 * k + 1, 1, k)
            behind(TILES - 1, 0, TILES // 2)

        def col(ap, i, n=1):
            return ap[:, bass.ds(i, n)]

        def cm(v):
            return v.rearrange("(c p) n -> p c n", p=128)

        def as3(ap, b):
            return ap.rearrange("p (a b) -> p a b", b=b)

        def over(ap, n):
            return ap.unsqueeze(2).broadcast_to([ap.shape[0], ap.shape[1], n])

        def row_of(v, n, parts=128):
            return v.rearrange("(a n) -> a n", a=1).broadcast_to([parts, n])

        class Norm:
            def __init__(s, i, src, dst, affine):
                s.src, s.dst, s.affine = src, dst, affine
                s.stats_ready = counted("ln_stats_ready", 1)
                s.rstd_ready = counted("ln_rstd_ready", 1)
                s.stage_ready = counted("ln_stage_ready", TILES)
                s.turned = counted("ln_turned", TILES + 2)
                s.turned_out = counted("ln_turned_out", TILES + 2)
                s.kept = counted("ln_kept", TILES + 2 if dst is not None else 0)
                c = Carver()
                c.at = ARENA - 1400
                s.st = c(P, TILES * 6)
                s.a, s.b, s.q, s.mean, s.var, s.rstd = [c(P, TILES) for _ in range(6)]
                s.stage = as3(c(P, 2 * D), D)
                s.gcol, s.bcol = c(128, 2), c(128, 2)

            def vector(s, e):
                def stats(t, u, k):
                    e.bn_stats(out=col(s.st, t * 6, 6), in_=col(s.src, t * D, D))
                tiles(e, stats)
                e.drain()
                st = as3(s.st, 6)
                e.tensor_tensor(s.a, st[:, :, 1], st[:, :, 4], ALU.add)
                e.tensor_tensor(s.b, st[:, :, 1], st[:, :, 4], ALU.subtract)
                e.tensor_tensor(s.q, st[:, :, 2], st[:, :, 5], ALU.add)
                e.drain()
                e.tensor_scalar(s.mean, s.a, 0.5, None, ALU.mult)
                e.tensor_tensor(s.b, s.b, s.b, ALU.mult)
                e.tensor_scalar(s.q, s.q, 1.0 / D, EPS, ALU.mult, ALU.add)
                e.drain()
                e.scalar_tensor_tensor(out=s.var, in0=s.b, scalar=0.25, in1=s.q, op0=ALU.mult,
                                       op1=ALU.add).then_inc(s.stats_ready.sem, 1)
                e.wait_ge(s.rstd_ready.sem, s.rstd_ready.base + 1)

                def scale(t, u, k):
                    e.wait_ge(s.turned.sem, s.turned.base + t + 1)
                    if s.dst is not None:
                        e.wait_ge(s.kept.sem, s.kept.base + t + 1)
                    e.tensor_scalar(s.stage[:, u, :], col(s.src, t * D, D), col(s.mean, t), col(s.rstd, t),
                                    ALU.subtract, ALU.mult).then_inc(s.stage_ready.sem, 1)
                tiles(e, scale)

            def gpsimd(s, e):
                e.wait_ge(s.stats_ready.sem, s.stats_ready.base + 1)
                e.tensor_tensor(s.rstd, s.var, neghalf[0:P, 0:TILES], ALU.pow).then_inc(s.rstd_ready.sem, 1)
                if s.dst is None:
                    return
                e.sem_inc(s.kept.sem, 2)

                def keep(t, u, k):
                    e.wait_ge(s.stage_ready.sem, s.stage_ready.base + t + 1)
                    own(e, "pool")
                    e.tensor_copy(col(s.dst, t * D, D), s.stage[:, u, :]).then_inc(s.kept.sem, 1)
                tiles(e, keep)

            def tensor(s, e):
                e.sem_inc(s.turned.sem, 2)

                def turn(t, u, k):
                    e.wait_ge(s.stage_ready.sem, s.stage_ready.base + t + 1)
                    e.wait_ge(s.turned_out.sem, s.turned_out.base + t + 1)
                    e.transpose(ps[u][:, 0:P], s.stage[:, u, 0:128], ident[0:P, 0:P])
                    e.transpose(ps[u][:, P:2 * P], s.stage[:, u, 128:256], ident[0:P, 0:P]).then_inc(s.turned.sem, 1)
                tiles(e, turn)

            def scalar(s, e):
                e.sem_inc(s.turned_out.sem, 2)

                def move(t, u, k):
                    e.wait_ge(s.turned.sem, s.turned.base + t + 3)
                    own(e, "act")
                    if s.affine:
                        e.activation(xnT[:, 0, bass.ds(t * P, P)], ps[u][:, 0:P], ACT.Identity,
                                     bias=s.bcol[:, 0:1], scale=s.gcol[:, 0:1])
                        e.activation(xnT[:, 1, bass.ds(t * P, P)], ps[u][:, P:2 * P], ACT.Identity,
                                     bias=s.bcol[:, 1:2], scale=s.gcol[:, 1:2]).then_inc(s.turned_out.sem, 1)
                    else:
                        e.activation(xnT[:, :, bass.ds(t * P, P)], as3(ps[u][:, 0:2 * P], P),
                                     ACT.Copy).then_inc(s.turned_out.sem, 1)
                tiles(e, move)

        class Messages:
            def __init__(s, la, table):
                s.la, s.table = la, table
                s.keys_loaded = counted("msg_keys_loaded", 16 * (ETILES // EB))
                s.picked = counted("msg_picked", ETILES)
                s.merged = counted("msg_merged", ETILES + EB)
                s.sums_out = counted("msg_sums_out", ETILES + 4)
                s.retired = counted("msg_retired", ETILES + 6)
                s.gathered = [counted(f"msg_gathered{u}", 16 * (ETILES // EB)) for u in range(EB)]
                s.scattered = [counted(f"msg_scattered{k}", 32 + 16 * (ETILES // TABLES)) for k in range(TABLES)]
                c = Carver()
                s.keys = c(128, EB * P)
                s.got = as3(c(P, EB * D), D)
                s.pick = as3(c(P, EB * P), P)
                s.sums = as3(c(P, EB * D), D)
                s.same = c(P, P)
                s.junk = c(P, P)
                s.count = c(P, 1)
                s.move = c(P, 1)
                s.gather_index = c(P, EB, I32)
                s.scatter_index = c(P, EB, I32)

            def sync(s, e):
                def load(i):
                    e.dma_start(s.keys, key_row[s.la][bass.ds(i * EB * P, EB * P)]
                                .rearrange("(a n) -> a n", a=1).broadcast_to([128, EB * P])
                                ).then_inc(s.keys_loaded.sem, 16)
                load(0)
                with e.Fori(1, ETILES // EB) as i:
                    e.wait_ge(s.picked.sem, s.picked.base + i * EB)
                    load(i)

            def vector(s, e):
                e.sem_inc(s.retired.sem, 6)
                with e.Fori(0, ETILES // EB) as i:
                    for u in range(EB):
                        n = i * EB + u
                        if u == 0:
                            e.wait_ge(s.keys_loaded.sem, s.keys_loaded.base + 16 * (i + 1))
                        e.wait_ge(s.merged.sem, s.merged.base + n + 1)
                        keys = s.keys[0:P, u * P:(u + 1) * P]
                        e.tensor_scalar(s.same, keys, col(key_col[s.la], n), None, ALU.is_equal)
                        if s.la == 0:
                            e.tensor_scalar(s.pick[:, u, :], keys, col(key_col[0], n), col(weight_col, n),
                                            ALU.is_equal, ALU.mult)
                        else:
                            e.tensor_scalar(s.pick[:, u, :], keys, col(key_col[1], n), None, ALU.is_equal)
                        e.drain()
                        e.wait_ge(s.retired.sem, s.retired.base + n + 1)
                        e.tensor_tensor_reduce(out=s.junk, in0=s.same, in1=earlier[:, :], scale=1.0, scalar=0.0,
                                               op0=ALU.mult, op1=ALU.add, accum_out=s.count)
                        e.tensor_copy(s.gather_index[:, u:u + 1], col(gather_col[s.la], n))
                        e.drain()
                        e.tensor_scalar(s.move, s.count, 1.0, col(spare_gap[s.la], n), ALU.min, ALU.mult)
                        e.drain()
                        e.tensor_tensor(s.scatter_index[:, u:u + 1], s.move, col(key_col[s.la], n), ALU.add)
                        e.drain().then_inc(s.picked.sem, 1)

            def gpsimd(s, e):
                for k in range(TABLES):
                    half = AGG_ROWS[s.la] // 2
                    for h in range(2):
                        e.dma_start(agg[s.la][k][h * half:(h + 1) * half, :].rearrange("(p a) d -> p a d", p=128),
                                    zeros[:, :].unsqueeze(1).broadcast_to([128, half // 128, D])
                                    ).then_inc(s.scattered[k].sem, 16)

                def gather(n, u):
                    e.wait_ge(s.picked.sem, s.picked.base + n + 1)
                    own(e, "pool")
                    e.indirect_dma_start(out=s.got[:, u, :], out_offset=None, in_=s.table[:, :],
                                         in_offset=bass.IndirectOffsetOnAxis(ap=s.gather_index[:, u:u + 1], axis=0)
                                         ).then_inc(s.gathered[u].sem, 16)

                def scatter(n, u, i):
                    e.wait_ge(s.sums_out.sem, s.sums_out.base + n + 5)
                    e.wait_ge(s.scattered[u % TABLES].sem, s.scattered[u % TABLES].base + 32 + 16 * (i * (EB // TABLES) + u // TABLES))
                    e.sem_inc(s.retired.sem, 1)
                    e.indirect_dma_start(out=agg[s.la][u % TABLES][:, :], in_=s.sums[:, u, :], in_offset=None,
                                         out_offset=bass.IndirectOffsetOnAxis(ap=s.scatter_index[:, u:u + 1], axis=0),
                                         compute_op=ALU.add).then_inc(s.scattered[u % TABLES].sem, 16)

                def turn(i, last):
                    for u in range(EB):
                        scatter(i * EB + u, u, i)
                        if not (last and u >= EB - LOOK):
                            gather(i * EB + u + LOOK, (u + LOOK) % EB)
                for n in range(LOOK):
                    gather(n, n)
                with e.Fori(0, ETILES // EB - 1) as i:
                    turn(i, False)
                turn(ETILES // EB - 1, True)
                for k in range(TABLES):
                    e.wait_ge(s.scattered[k].sem, s.scattered[k].base + 32 + 16 * (ETILES // TABLES))

            def tensor(s, e):
                e.sem_inc(s.merged.sem, EB)
                with e.Fori(0, ETILES // EB) as i:
                    for u in range(EB):
                        n = i * EB + u
                        e.wait_ge(s.picked.sem, s.picked.base + n + 1)
                        e.wait_ge(s.gathered[u].sem, s.gathered[u].base + 16 * (i + 1))
                        e.wait_ge(s.sums_out.sem, s.sums_out.base + n + 1)
                        e.matmul(ps[u % 4][0:P, 0:D], s.pick[:, u, :], s.got[:, u, :],
                                 start=True, stop=True).then_inc(s.merged.sem, 1)

            def scalar(s, e):
                e.sem_inc(s.sums_out.sem, 4)
                with e.Fori(0, ETILES // EB) as i:
                    for u in range(EB):
                        n = i * EB + u
                        e.wait_ge(s.merged.sem, s.merged.base + n + EB + 1)
                        e.wait_ge(s.retired.sem, s.retired.base + n + 1)
                        e.activation(s.sums[:, u, :], ps[u % 4][0:P, 0:D], ACT.Copy).then_inc(s.sums_out.sem, 1)

        class Project:

            def __init__(s, name, weights, at=0):
                s.staged = counted("prj_staged", TILES)
                s.turned = counted("prj_turned", TILES + 2)
                s.moved = counted("prj_moved", TILES + 2)
                s.product = counted("prj_product", TILES + 2)
                s.used = counted("prj_used", TILES + 2)
                s.w = weights
                c = Carver()
                c.at = at
                s.stage = as3(c(P, 2 * D), D)
                s.lt = c(128, 2 * 2 * P).rearrange("p (u c n) -> p u c n", u=2, c=2)
                s.end = c.at

            def fill_from_rows(s, e, src):
                def fill(t, u, k):
                    e.wait_ge(s.turned.sem, s.turned.base + t + 1)
                    own(e, "pool")
                    e.tensor_copy(s.stage[:, u, :], col(src, t * D, D)).then_inc(s.staged.sem, 1)
                return fill

            def tensor(s, e):
                e.sem_inc(s.turned.sem, 2)
                e.sem_inc(s.product.sem, 2)

                def turn(t, u, k):
                    e.wait_ge(s.staged.sem, s.staged.base + t + 1)
                    e.wait_ge(s.moved.sem, s.moved.base + t + 1)
                    e.transpose(ps[u][:, 0:P], s.stage[:, u, 0:128], ident[0:P, 0:P])
                    e.transpose(ps[u][:, P:2 * P], s.stage[:, u, 128:256], ident[0:P, 0:P]).then_inc(s.turned.sem, 1)

                def multiply(t, u, k):
                    e.wait_ge(s.moved.sem, s.moved.base + t + 3)
                    e.wait_ge(s.used.sem, s.used.base + t + 1)
                    for c in range(2):
                        mm = e.matmul(ps[2 + u][0:P, 0:D], s.lt[:, u, c, :], s.w[:, c, :],
                                      start=(c == 0), stop=(c == 1))
                    mm.then_inc(s.product.sem, 1)
                tiles_lagged(e, turn, multiply)

            def scalar(s, e):
                e.sem_inc(s.moved.sem, 2)

                def move(t, u, k):
                    e.wait_ge(s.turned.sem, s.turned.base + t + 3)
                    e.wait_ge(s.product.sem, s.product.base + t + 1)
                    e.activation(s.lt[:, u, :, :], as3(ps[u][:, 0:2 * P], P), ACT.Copy).then_inc(s.moved.sem, 1)
                tiles(e, move)

            def out(s, u):
                return ps[2 + u][0:P, 0:D]

        class Attend:
            def __init__(s, la, scale, wqkv, bias, w_out):
                s.la, s.scale, s.wqkv, s.bias, s.w_out = la, scale, wqkv, bias, w_out
                s.k_product = counted("mix_k_product", 4 * CHUNKS)
                s.k_reduced = counted("mix_k_reduced", 4 * CHUNKS + 4)
                s.k_max = counted("mix_k_max", 1)
                s.k_row = counted("mix_k_row", 1)
                s.shift = counted("mix_shift", 1)
                s.lt_ready = counted("mix_lt_ready", TILES)
                s.qkv = counted("mix_qkv", TILES + 2)
                s.qkv_out = counted("mix_qkv_out", TILES + 2)
                s.q_shifted = counted("mix_q_shifted", TILES)
                s.k_exp = counted("mix_k_exp", TILES)
                s.q_exp = counted("mix_q_exp", TILES)
                s.ctx_sum = counted("mix_ctx_sum", TILES + 2)
                s.ctx_closed = counted("mix_ctx_closed", 1)
                s.blocks = counted("mix_blocks", 1)
                s.blocks_turned = counted("mix_blocks_turned", 1)
                s.blocks_out = counted("mix_blocks_out", 1)
                s.folded = counted("mix_folded", 1)
                c = Carver()
                c.at = 4200
                s.lt = c(128, 4 * P).rearrange("p (u c n) -> p u c n", u=2, c=2)
                s.part = c(128, 4)
                s.part_new = c(128, 4)
                s.kmax = c(128, 2)
                s.shift_row = c(P, D)
                s.tmp = c(P, D)
                s.ks = as3(c(P, 2 * D), D)
                s.ke = as3(c(P, 2 * D), D)
                s.qb = as3(c(P, 2 * D), D)
                s.qe = as3(c(P, 2 * D), D)
                s.v1 = as3(c(P, 2 * (D + 1)), D + 1)
                s.q8 = as3(c(P, 2 * MIX_HEADS), MIX_HEADS)
                s.zero = c(P, D + 1)
                s.rs = c(128, 2)
                s.bd = as3(c(128, 2 * D), D)
                s.bdT = as3(c(128, 2 * 128), 128)
                s.m = as3(c(128, 2 * D), D)
                s.end = c.at

            def tensor(s, e):
                with e.Fori(0, CHUNKS) as c:
                    for oc in range(2):
                        for h, (off, n) in enumerate(HALVES):
                            j = 2 * oc + h
                            e.wait_ge(s.k_reduced.sem, s.k_reduced.base + 4 * c + j + 1)
                            for k in range(2):
                                mm = e.matmul(ps[j][:, 0:n], s.wqkv[:, k, D + oc * 128:D + (oc + 1) * 128],
                                              xnT[:, k, bass.ds(c * CHUNK + off, n)], start=(k == 0), stop=(k == 1))
                            mm.then_inc(s.k_product.sem, 1)
                e.wait_ge(s.k_max.sem, s.k_max.base + 1)
                for oc in range(2):
                    mm = e.matmul(ps[4][0:P, oc * 128:(oc + 1) * 128], s.kmax[:, oc:oc + 1].broadcast_to([128, P]),
                                  ident[:, :], start=True, stop=True, skip_group_check=True)
                mm.then_inc(s.k_row.sem, 1)
                e.wait_ge(s.shift.sem, s.shift.base + 1)
                for c in range(2):
                    e.matmul(ps[6 + c][:, 0:D + 1], s.zero[:, 0:128], s.zero, start=True, stop=False)
                e.sem_inc(s.qkv.sem, 2)
                e.sem_inc(s.ctx_sum.sem, 2)

                def project(t, u, k):
                    e.wait_ge(s.lt_ready.sem, s.lt_ready.base + t + 1)
                    e.wait_ge(s.qkv_out.sem, s.qkv_out.base + t + 1)
                    for c in range(2):
                        e.matmul(ps[u][0:P, 0:512], s.lt[:, u, c, :], s.wqkv[:, c, 0:512],
                                 start=(c == 0), stop=(c == 1))
                    for c in range(2):
                        mm = e.matmul(ps[2 + u][0:P, 0:D], s.lt[:, u, c, :], s.wqkv[:, c, 512:768],
                                      start=(c == 0), stop=(c == 1))
                    mm.then_inc(s.qkv.sem, 1)

                def context(t, u, k):
                    e.wait_ge(s.k_exp.sem, s.k_exp.base + t + 1)
                    for c in range(2):
                        mm = e.matmul(ps[6 + c][:, 0:D + 1], s.ke[:, u, c * 128:(c + 1) * 128], s.v1[:, u, :],
                                      start=False, stop=False)
                    mm.then_inc(s.ctx_sum.sem, 1)
                tiles_lagged(e, project, context)
                for c in range(2):
                    mm = e.matmul(ps[6 + c][:, 0:D + 1], s.zero[:, 0:128], s.zero, start=False, stop=True)
                mm.then_inc(s.ctx_closed.sem, 1)
                e.wait_ge(s.blocks.sem, s.blocks.base + 1)
                for c in range(2):
                    mm = e.transpose(ps[4][:, c * 128:(c + 1) * 128], s.bd[:, c, c * 128:(c + 1) * 128], ident[:, :])
                mm.then_inc(s.blocks_turned.sem, 1)
                e.wait_ge(s.blocks_out.sem, s.blocks_out.base + 1)
                for c in range(2):
                    mm = e.matmul(ps[5][:, c * D:(c + 1) * D], s.bdT[:, c, :], s.w_out[:, c, :],
                                  start=True, stop=True, skip_group_check=True)
                mm.then_inc(s.folded.sem, 1)

            def gpsimd(s, e):
                def fill(t, u, k):
                    e.wait_ge(s.qkv.sem, s.qkv.base + t + 1)
                    own(e, "pool")
                    e.tensor_copy(s.lt[:, u, :, :], xnT[:, :, bass.ds(t * P, P)]).then_inc(s.lt_ready.sem, 1)
                tiles(e, fill)

            def scalar(s, e):
                e.preload_act_table(ACT.Exp)

                def exps(t, u, k):
                    e.wait_ge(s.qkv_out.sem, s.qkv_out.base + t + 3)
                    e.wait_ge(s.ctx_sum.sem, s.ctx_sum.base + t + 1)
                    e.activation(s.ke[:, u, :], s.ks[:, u, :], ACT.Exp).then_inc(s.k_exp.sem, 1)
                    e.wait_ge(s.q_shifted.sem, s.q_shifted.base + t + 1)
                    e.activation(s.qe[:, u, :], s.qb[:, u, :], ACT.Exp).then_inc(s.q_exp.sem, 1)
                tiles(e, exps)

            def vector(s, e):
                e.sem_inc(s.k_reduced.sem, 4)
                e.memset(s.part, -3.0e38)
                e.memset(s.zero, 0.0)
                e.memset(s.bd[:, :, :], 0.0)
                e.memset(s.v1[:, :, D:D + 1], 1.0)
                with e.Fori(0, CHUNKS) as c:
                    for j in range(4):
                        n = HALVES[j % 2][1]
                        e.wait_ge(s.k_product.sem, s.k_product.base + 4 * c + j + 1)
                        e.tensor_reduce(s.part_new[:, j:j + 1], ps[j][:, 0:n], AX.X, ALU.max).then_inc(s.k_reduced.sem, 1)
                    e.drain()
                    e.tensor_tensor(s.part, s.part, s.part_new, ALU.max)
                    e.drain()
                p2 = as3(s.part, 2)
                e.tensor_tensor(s.kmax, p2[:, :, 0], p2[:, :, 1], ALU.max)
                e.drain().then_inc(s.k_max.sem, 1)
                e.wait_ge(s.k_row.sem, s.k_row.base + 1)
                e.tensor_tensor(s.tmp, ps[4][0:P, 0:D], s.bias[:, D:2 * D], ALU.add)
                e.drain()
                e.tensor_tensor(s.shift_row, s.bias[:, D:2 * D], s.tmp, ALU.subtract)
                e.drain().then_inc(s.shift.sem, 1)
                e.sem_inc(s.qkv_out.sem, 2)

                def spread(t, u, k):
                    e.wait_ge(s.qkv.sem, s.qkv.base + t + 3)
                    e.wait_ge(s.ctx_sum.sem, s.ctx_sum.base + t + 1)
                    e.tensor_tensor(s.ks[:, u, :], ps[u][0:P, D:2 * D], s.shift_row, ALU.add)
                    e.tensor_tensor(s.v1[:, u, 0:D], ps[2 + u][0:P, 0:D], s.bias[:, 2 * D:3 * D], ALU.add)
                    e.tensor_tensor(s.qb[:, u, :], ps[u][0:P, 0:D], s.bias[:, 0:D], ALU.add)
                    e.drain().then_inc(s.qkv_out.sem, 1)
                    q3 = as3(s.qb[:, u, :], MHD)
                    e.tensor_reduce(s.q8[:, u, :], q3, AX.X, ALU.max)
                    e.drain()
                    e.tensor_tensor(q3, q3, over(s.q8[:, u, :], MHD), ALU.subtract)
                    e.drain().then_inc(s.q_shifted.sem, 1)

                def finish(t, u, k):
                    e.wait_ge(s.q_exp.sem, s.q_exp.base + t + 1)
                    q3 = as3(s.qe[:, u, :], MHD)
                    e.tensor_reduce(s.q8[:, u, :], q3, AX.X, ALU.add)
                    e.drain()
                    e.reciprocal(s.q8[:, u, :], s.q8[:, u, :])
                    e.drain()
                    e.tensor_tensor(as3(col(rows, t * D, D), MHD), q3, over(s.q8[:, u, :], MHD), ALU.mult)
                    e.drain()
                tiles_lagged(e, spread, finish)
                e.wait_ge(s.ctx_closed.sem, s.ctx_closed.base + 1)
                for c in range(2):
                    e.reciprocal(s.rs[:, c:c + 1], ps[6 + c][:, D:D + 1])
                e.drain()
                for h in range(MIX_HEADS):
                    c, p0 = h // 4, (h % 4) * MHD
                    e.tensor_scalar(s.bd[p0:p0 + MHD, c, h * MHD:(h + 1) * MHD],
                                    ps[6 + c][p0:p0 + MHD, h * MHD:(h + 1) * MHD],
                                    s.rs[p0:p0 + MHD, c:c + 1], s.scale, ALU.mult, ALU.mult)
                e.drain().then_inc(s.blocks.sem, 1)
                e.wait_ge(s.blocks_turned.sem, s.blocks_turned.base + 1)
                e.tensor_copy(s.bdT[:, :, :], as3(ps[4][:, 0:256], 128))
                e.drain().then_inc(s.blocks_out.sem, 1)
                e.wait_ge(s.folded.sem, s.folded.base + 1)
                e.tensor_copy(s.m[:, :, :], as3(ps[5][:, 0:512], D))

        edge_loaded, edge_ready, edge_turned, consts_ready = (sem(n) for n in (
            "edge_loaded", "edge_ready", "edge_turned", "consts_ready"))
        x_loaded, rows_written, table_written, out_written = (sem(n) for n in (
            "x_loaded", "rows_written", "table_written", "out_written"))
        c = Carver()
        raw_i = [c(EROWS, EBLK * P, I32) for _ in range(3)]
        raw_w = c(EROWS, EBLK * P)
        src_f, dst_f, typ_f, key1_f, gat1_f = [c(EROWS, EBLK * P) for _ in range(5)]
        ones_c = c(128, 128)

        ln = [Norm(0, x_cur, xn, False), Norm(1, x_cur, None, False), Norm(2, x_cur, xn, False),
              Norm(3, xn, None, True), Norm(4, rows, None, True), Norm(5, x_cur, None, False)]

        c = Carver()
        w_qkv0 = as3(c(128, 2 * 768), 768)
        w_out0 = as3(c(128, 2 * D), D)
        bias0 = c(P, 768)
        gamma0 = c(P, D)
        mix0_loaded = sem("mix0_loaded")
        bias0_cleared = sem("bias0_cleared")
        att0 = Attend(0, MHD ** -0.5, w_qkv0, bias0, w_out0)
        prj0 = Project("prj0", att0.m, att0.end)
        c = Carver()
        c.at = prj0.end
        cs_st = as3(c(P, 12), 6)
        cs_mv = as3(c(P, 4), 2)
        cs_ve = c(P, 2)
        cs_rs = c(P, 2)
        cs_o = as3(c(P, 2 * D), D)
        var0, rstd0 = sem("mix0_var"), sem("mix0_rstd")

        msg = [Messages(0, xn_table), Messages(1, rel_table)]

        prjg = Project("prjg", None, 0)
        c = Carver()
        c.at = prjg.end
        w_gnn0 = as3(c(128, 2 * D), D)
        prjg.w = w_gnn0
        gnn_rows = as3(c(P, 5 * D), D)
        ag0 = c(P, 4 * D).rearrange("p (u k d) -> p u k d", u=2, k=2)
        g_y = as3(c(P, 2 * D), D)
        g_st = c(P, 2 * 24).rearrange("p (u h s) -> p u h s", u=2, s=6)
        g_mv = c(P, 2 * 8).rearrange("p (u h s) -> p u h s", u=2, s=2)
        g_ve = as3(c(P, 8), 4)
        g_rs = as3(c(P, 8), 4)
        gnn0_loaded = sem("gnn0_loaded")
        agg0_loaded = [sem(f"agg0_loaded{u}") for u in range(2)]
        agg0_free = sem("agg0_free")
        gvar, grstd = sem("gnn0_var"), sem("gnn0_rstd")

        c = Carver()
        w_e = c(128, 2 * 3 * 2 * D).rearrange("p (u w c d) -> p u w c d", u=2, w=3, c=2)
        bnp = c(128, 10 * 16).rearrange("p (a b) -> p a b", b=16)
        bns = as3(c(128, 4 * 16), 16)
        bnt = c(128, 16)
        w_r = as3(c(128, 2 * MOE), MOE)
        br_row = c(P, MOE)
        bo_sb = c(MOE, D)
        gate = c(P, TILES * MOE)
        gt_l = as3(c(P, 2 * MOE), MOE)
        gt_s = c(P, 2)
        gT = as3(c(MOE, 2 * P), P)
        ltg = c(128, 4 * P).rearrange("p (u c n) -> p u c n", u=2, c=2)
        h1 = as3(c(128, 2 * CHUNK), CHUNK)
        h2 = as3(c(128, 2 * CHUNK), CHUNK)
        ffn0_loaded = sem("ffn0_loaded")
        gsem = {x: sem(f"gate_{x}") for x in ("lt_ready", "logits", "shifted", "exp", "ready", "turned", "copied", "bias", "bias_used")}
        bn_var, bn_rstd, bn_ready = sem("bn_var"), sem("bn_rstd"), sem("bn_ready")
        we_loaded = [sem(f"expert_loaded{u}") for u in range(2)]
        we_used, unit_done, unit_out, y_done, y_out = (sem(f"moe_{n}") for n in (
            "weights_used", "unit_done", "unit_out", "y_done", "y_out"))

        c = Carver()
        w_rel = as3(c(128, 2 * REL * D), REL * D)
        b_rel = c(P, REL * D)
        lt_rel = c(128, 4 * P).rearrange("p (u c n) -> p u c n", u=2, c=2)
        rel_out = as3(c(P, 2 * REL * D), REL * D)
        rel_dma = [sem(f"rel_dma{u}") for u in range(2)]
        rel_lt, rel_mm, rel_moved = sem("rel_lt"), sem("rel_mm"), sem("rel_moved")

        RD = REL * D
        c = Carver()
        w_in = as3(c(128, 2 * 768), 768)
        b_in = c(P, 768)
        ag1 = c(P, 4 * RD).rearrange("p (u k d) -> p u k d", u=2, k=2)
        agsum = c(P, RD)
        aT = as3(c(128, 12 * P), P)
        Q = as3(c(P, RD), D)
        K = as3(c(P, RD), D)
        V = as3(c(P, RD), D)
        prod = c(P, RD)
        pprod = c(P, RD)
        scores = c(P, REL * REL * HEADS)
        sc24 = c(P, REL * HEADS)
        pbar = c(P, REL * HEADS)
        vsum = c(P, D)
        rel_agg_loaded = [sem(f"rel_agg_loaded{u}") for u in range(2)]
        asem = {x: sem(f"relatt_{x}") for x in ("w", "agg_free", "summed", "turned", "moved", "qkv", "qkv_out", "q_ready",
                                                "pool_prod", "pool_prod_used", "shifted", "exp")}

        prj1 = Project("prj1", None, 0)
        prj2 = Project("prj2", None, prj1.end)
        c = Carver()
        c.at = prj2.end
        w_ao = as3(c(128, 2 * D), D)
        w_pr = as3(c(128, 2 * D), D)
        prj1.w, prj2.w = w_ao, w_pr
        b_ao = c(P, D)
        b_pr = c(P, D)
        prj_tmp = as3(c(P, 2 * D), D)
        prj_loaded = sem("prj_loaded")

        c = Carver()
        w_qkv1 = as3(c(128, 2 * 768), 768)
        bias1 = c(P, 768)
        w_out1 = as3(c(128, 2 * D), D)
        b_o1 = c(P, D)
        assert c.at <= 4200
        att1 = Attend(1, 1.0, w_qkv1, bias1, w_out1)
        prj3 = Project("prj3", att1.m, att1.end)
        c = Carver()
        c.at = prj3.end
        w_x = as3(c(128, 2 * D), D)
        b_x = c(128, 2)
        blk = c(128, 3 * 128)
        p3_tmp = as3(c(P, 2 * D), D)
        mix1_loaded, blk_cleared, blk_loaded, fold_mm, fold_out, bias_mm = (sem(f"mix1_{n}") for n in (
            "loaded", "blk_cleared", "blk_loaded", "fold_mm", "fold_out", "bias_mm"))

        c = Carver()
        w_m1 = as3(c(128, 2 * HID), HID)
        w_m2 = as3(c(128, 8 * D), D)
        b_m1 = c(128, 8)
        b_m2 = c(P, D)
        m_h = as3(c(128, 8 * CHUNK), CHUNK)
        m_o = as3(c(P, 2 * D), D)
        mlp_loaded, m1_mm, m1_out, m2_mm, m2_out = (sem(f"mlp_{n}") for n in ("loaded", "m1_mm", "m1_out", "m2_mm", "m2_out"))

        c = Carver()
        w_1 = as3(c(128, 2 * EXP * EH), EXP * EH)
        w_2 = as3(c(128, 16 * D), D)
        b_1 = c(128, 16)
        w_ro = as3(c(128, 2 * EXP), EXP)
        b_ro = c(P, EXP)
        b_2 = c(EXP, D)
        e_col = c(128, 16)
        e_col_i = c(128, 16, I32)
        iota32 = c(P, EXP)
        iota32_i = c(P, EXP, I32)
        lt_ro = c(128, 4 * P).rearrange("p (u c n) -> p u c n", u=2, c=2)
        ro_l = as3(c(P, 2 * EXP), EXP)
        ro_m = as3(c(P, 2 * 8), 8)
        ro_i = as3(c(P, 2 * 8, U32), 8)
        ro_f = c(P, 2)
        ro_h = as3(c(P, 2 * EXP), EXP)
        e_h = as3(c(128, 16 * CHUNK), CHUNK)
        ffn1_loaded = sem("ffn1_loaded")
        rsem = {x: sem(f"route_{x}") for x in ("consts", "cols", "lt_ready", "logits", "ready", "turned", "copied")}
        x_mm, x_relu, x_masked, x_y, x_yout = (sem(f"moe1_{n}") for n in ("unit", "relu", "masked", "y", "y_out"))
        e_hot = c(EXP, CHUNK)
        idxT = xn_whole[:, 0:NODES]
        ohT = rows[0:EXP, 0:NODES]

        block = ctx.enter_context(nc.Block())

        @block.sync
        def _(sp):
            sp.dma_start(as3(x_cur[:, :], D), A["x"].rearrange("(t p) d -> p t d", p=P)).then_inc(x_loaded, 16)
            for r, n in enumerate(("src", "dst", "edge_type_6")):
                sp.dma_start(as3(raw_i[r], P), A[n].rearrange("(a q j) -> q a j", q=EROWS, j=P)).then_inc(edge_loaded, 16)
            sp.dma_start(as3(raw_w, P), A["edge_weight"].rearrange("(a q j) -> q a j", q=EROWS, j=P)).then_inc(edge_loaded, 16)
            sp.wait_ge(edge_ready, 1)
            for la, k in enumerate((src_f, key1_f)):
                sp.dma_start(key_row[la].rearrange("(a q j) -> q a j", q=EROWS, j=P), as3(k, P)).then_inc(rows_written, 16)
            sp.wait_ge(rows_written, 32)
            phase_end(sp, 1)
            phase_end(sp, 2)
            sp.dma_start(xn_table.rearrange("(t p) d -> p t d", p=P), as3(xn[:, :], D)).then_inc(table_written, 16)
            sp.dma_start(w_qkv0[:, :, :], cm(A["L0_mix_Wqkv"])).then_inc(mix0_loaded, 16)
            sp.dma_start(w_out0[:, :, :], cm(A["L0_mix_Wout"])).then_inc(mix0_loaded, 16)
            sp.dma_start(gamma0, row_of(A["L0_mix_gamma"], D, P)).then_inc(mix0_loaded, 16)
            sp.wait_ge(table_written, 16)
            sp.wait_ge(mix0_loaded, 48)
            phase_end(sp, 3)
            phase_end(sp, 4)
            phase_end(sp, 5)
            msg[0].sync(sp)
            phase_end(sp, 6)
            sp.dma_start(w_gnn0[:, :, :], cm(A["gnn0_W"])).then_inc(gnn0_loaded, 16)
            for i, n in enumerate(("L0_gnn_bias", "L0_gnn_ln1_g", "L0_gnn_ln1_b", "L0_gnn_ln2_g", "L0_gnn_ln2_b")):
                sp.dma_start(gnn_rows[:, i, :], row_of(A[n], D, P)).then_inc(gnn0_loaded, 16)

            def load_agg(t, u, k):
                sp.wait_ge(agg0_free, t + 1)
                for tb in range(TABLES):
                    sp.dma_start(ag0[:, u, tb, :], agg[0][tb][bass.ds(t * P, P), :]).then_inc(agg0_loaded[u], 16)
            tiles(sp, load_agg)
            sp.wait_ge(gnn0_loaded, 96)
            phase_end(sp, 7)
            phase_end(sp, 8)
            for i, n in enumerate(("L0_ffn_b1", "L0_ffn_g1", "L0_ffn_be1", "L0_ffn_m1", "L0_ffn_v1",
                                   "L0_ffn_b2", "L0_ffn_g2", "L0_ffn_be2", "L0_ffn_m2", "L0_ffn_v2")):
                sp.dma_start(bnp[:, i, :], A[n]).then_inc(ffn0_loaded, 16)
            sp.dma_start(w_r[:, :, :], cm(A["L0_ffn_Wr"])).then_inc(ffn0_loaded, 16)
            sp.dma_start(br_row, row_of(A["L0_ffn_br"], MOE, P)).then_inc(ffn0_loaded, 16)
            sp.dma_start(bo_sb, A["L0_ffn_bo"]).then_inc(ffn0_loaded, 16)
            sp.wait_ge(ffn0_loaded, 13 * 16)
            phase_end(sp, 9)
            with sp.Fori(0, MOE // 2) as k:
                for u in range(2):
                    sp.wait_ge(we_used, 2 * k + u + 1)
                    for i, n in enumerate(("L0_ffn_W1", "L0_ffn_W2", "L0_ffn_Wo")):
                        sp.dma_start(w_e[:, u, i, :, :], A[n][bass.ds((2 * k + u) * D, D), :]
                                     .rearrange("(c p) n -> p c n", p=128)).then_inc(we_loaded[u], 16)
            phase_end(sp, 10)
            phase_end(sp, 11)
            sp.dma_start(w_rel[:, :, :], cm(A["gnn1_W"])).then_inc(rel_dma[0], 16)
            sp.dma_start(b_rel, row_of(A["L1_gnn_b"], RD, P)).then_inc(rel_dma[1], 16)

            def store_rel(t, u, k):
                sp.wait_ge(rel_moved, t + 3)
                sp.dma_start(rel_table.rearrange("(r n) d -> n r d", r=REL)[bass.ds(t * P, P), :, :],
                             as3(rel_out[:, u, :], D)).then_inc(rel_dma[u], 16)
            tiles(sp, store_rel)
            sp.wait_ge(rel_dma[0], 16 + 16 * 13)
            sp.wait_ge(rel_dma[1], 16 + 16 * 12)
            phase_end(sp, 12)
            msg[1].sync(sp)
            phase_end(sp, 13)
            sp.dma_start(w_in[:, :, :], cm(A["gnn1_in_T"])).then_inc(asem["w"], 16)
            sp.dma_start(b_in, row_of(A["L1_gnn_in_proj_b"], 768, P)).then_inc(asem["w"], 16)

            def load_rel(t, u, k):
                sp.wait_ge(asem["agg_free"], t + 1)
                for tb in range(TABLES):
                    sp.dma_start(as3(ag1[:, u, tb, :], D), agg[1][tb][0:REL * NODES, :]
                                 .rearrange("(r n) d -> n r d", r=REL)[bass.ds(t * P, P), :, :]
                                 ).then_inc(rel_agg_loaded[u], 16)
            tiles(sp, load_rel)
            sp.wait_ge(asem["w"], 32)
            phase_end(sp, 14)
            sp.dma_start(w_ao[:, :, :], cm(A["gnn1_ao_T"])).then_inc(prj_loaded, 16)
            sp.dma_start(w_pr[:, :, :], cm(A["gnn1_pr_T"])).then_inc(prj_loaded, 16)
            sp.dma_start(b_ao, row_of(A["L1_gnn_attn_out_b"], D, P)).then_inc(prj_loaded, 16)
            sp.dma_start(b_pr, row_of(A["L1_gnn_proj_b"], D, P)).then_inc(prj_loaded, 16)
            sp.wait_ge(prj_loaded, 64)
            phase_end(sp, 15)
            phase_end(sp, 16)
            phase_end(sp, 17)
            sp.dma_start(ln[3].gcol, A["mix1_ln1_w"]).then_inc(mix1_loaded, 16)
            sp.dma_start(ln[3].bcol, A["mix1_ln1_b"]).then_inc(mix1_loaded, 16)
            sp.dma_start(w_x[:, :, :], cm(A["L1_mix_Wx"])).then_inc(mix1_loaded, 16)
            sp.dma_start(b_x, A["mix1_bx"]).then_inc(mix1_loaded, 16)
            sp.dma_start(w_out1[:, :, :], cm(A["mix1_Wo_T"])).then_inc(mix1_loaded, 16)
            sp.dma_start(b_o1, row_of(A["L1_mix_bo"], D, P)).then_inc(mix1_loaded, 16)
            sp.wait_ge(blk_cleared, 1)
            for i, n in enumerate(("mix1_Wq_T", "mix1_Wk_T", "mix1_Wv_T")):
                for h in range(4):
                    sp.dma_start(blk[h * MHD:(h + 1) * MHD, i * 128 + h * MHD:i * 128 + (h + 1) * MHD],
                                 A[n]).then_inc(blk_loaded, 16)
            sp.wait_ge(mix1_loaded, 96)
            sp.wait_ge(blk_loaded, 16 * 12)
            phase_end(sp, 18)
            phase_end(sp, 19)
            phase_end(sp, 20)
            phase_end(sp, 21)
            sp.dma_start(ln[4].gcol, A["mix1_ln2_w"]).then_inc(mlp_loaded, 16)
            sp.dma_start(ln[4].bcol, A["mix1_ln2_b"]).then_inc(mlp_loaded, 16)
            sp.dma_start(w_m1[:, :, :], cm(A["mix1_W1_T"])).then_inc(mlp_loaded, 16)
            sp.dma_start(w_m2[:, :, :], A["mix1_W2_T"].rearrange("(c p) n -> p c n", p=128)).then_inc(mlp_loaded, 16)
            sp.dma_start(b_m1, A["mix1_b1"]).then_inc(mlp_loaded, 16)
            sp.dma_start(b_m2, row_of(A["L1_mix_b2"], D, P)).then_inc(mlp_loaded, 16)
            sp.wait_ge(mlp_loaded, 96)
            phase_end(sp, 22)
            phase_end(sp, 23)
            phase_end(sp, 24)
            phase_end(sp, 25)
            for d_, n in ((w_1, cm(A["ffn1_W1"])), (w_2, A["ffn1_W2"].rearrange("(c p) n -> p c n", p=128)), (w_ro, cm(A["ffn1_router_T"]))):
                sp.dma_start(d_[:, :, :], n).then_inc(ffn1_loaded, 16)
            sp.dma_start(b_1, A["ffn1_b1"]).then_inc(ffn1_loaded, 16)
            sp.dma_start(b_ro, row_of(A["L1_ffn_router_b"], EXP, P)).then_inc(ffn1_loaded, 16)
            sp.dma_start(b_2, A["L1_ffn_b2"]).then_inc(ffn1_loaded, 16)
            sp.wait_ge(ffn1_loaded, 96)
            phase_end(sp, 26)
            phase_end(sp, 27)
            sp.dma_start(out.rearrange("(t p) d -> p t d", p=P), as3(x_cur[:, :], D)).then_inc(out_written, 16)
            sp.wait_ge(out_written, 16)

        @block.gpsimd
        def _(pool):
            pool.memset(ones_c, 1.0)
            pool.memset(zeros[:, :], 0.0)
            pool.memset(neghalf[:, :], -0.5)
            pool.iota(lane_i[:, :], [[0, 1]], base=0, channel_multiplier=1)
            pool.drain()
            pool.affine_select(out=ident[:, :], in_=ones_c, compare_op=ALU.is_equal, fill=0.0, base=0,
                               pattern=[[-1, 128]], channel_multiplier=1)
            pool.affine_select(out=earlier[:, :], in_=ones_c[0:P, 0:P], compare_op=ALU.is_gt, fill=0.0, base=0,
                               pattern=[[-1, P]], channel_multiplier=1)
            pool.tensor_copy(lane[:, :], lane_i[:, :])
            pool.drain().then_inc(consts_ready, 1)
            phase_end(pool, 1)
            ln[0].gpsimd(pool)
            phase_end(pool, 2)
            pool.memset(bias0, 0.0)
            phase_end(pool, 3)
            att0.gpsimd(pool)
            phase_end(pool, 4)
            fill = prj0.fill_from_rows(pool, rows[:, :])

            def root0(t, u, k):
                pool.wait_ge(var0, t + 1)
                pool.tensor_tensor(cs_rs[:, u:u + 1], cs_ve[:, u:u + 1], neghalf[0:P, 0:1], ALU.pow).then_inc(rstd0, 1)
            tiles_lagged(pool, fill, root0)
            phase_end(pool, 5)
            msg[0].gpsimd(pool)
            phase_end(pool, 6)
            pool.sem_inc(agg0_free, 2)

            def add_tables(t, u, k):
                pool.wait_ge(agg0_loaded[u], 32 * (k + 1))
                pool.wait_ge(prjg.turned.sem, prjg.turned.base + t + 1)
                pool.tensor_tensor(prjg.stage[:, u, :], ag0[:, u, 0, :], ag0[:, u, 1, :], ALU.add).then_inc(prjg.staged.sem, 1)
                pool.wait_ge(prjg.staged.sem, prjg.staged.base + t + 1)
                pool.sem_inc(agg0_free, 1)

            def rootg(t, u, k):
                pool.wait_ge(gvar, 2 * t + 1)
                pool.tensor_tensor(g_rs[:, u, :], g_ve[:, u, :], neghalf[0:P, 0:4], ALU.pow).then_inc(grstd, 1)
                pool.wait_ge(gvar, 2 * t + 2)
                pool.tensor_tensor(g_rs[:, u, 0:1], g_ve[:, u, 0:1], neghalf[0:P, 0:1], ALU.pow).then_inc(grstd, 1)
            tiles_lagged(pool, add_tables, rootg)
            phase_end(pool, 7)
            ln[1].gpsimd(pool)
            phase_end(pool, 8)
            pool.wait_ge(bn_var, 1)
            for i in (0, 2):
                pool.tensor_tensor(bns[:, i, :], bns[:, i, :], neghalf[:, 0:16], ALU.pow)
            pool.drain().then_inc(bn_rstd, 1)

            def fillg(t, u, k):
                pool.wait_ge(gsem["logits"], t + 1)
                own(pool, "pool")
                pool.tensor_copy(ltg[:, u, :, :], xnT[:, :, bass.ds(t * P, P)]).then_inc(gsem["lt_ready"], 1)
            tiles(pool, fillg)
            phase_end(pool, 9)
            phase_end(pool, 10)
            ln[2].gpsimd(pool)
            phase_end(pool, 11)

            def fill_rel(t, u, k):
                pool.wait_ge(rel_mm, t + 1)
                own(pool, "pool")
                pool.tensor_copy(lt_rel[:, u, :, :], xnT[:, :, bass.ds(t * P, P)]).then_inc(rel_lt, 1)
            tiles(pool, fill_rel)
            phase_end(pool, 12)
            msg[1].gpsimd(pool)
            phase_end(pool, 13)
            pool.sem_inc(asem["agg_free"], 2)

            def rel_sum(t, u, k):
                pool.wait_ge(rel_agg_loaded[u], 32 * (k + 1))
                pool.wait_ge(asem["turned"], t + 1)
                pool.tensor_tensor(agsum, ag1[:, u, 0, :], ag1[:, u, 1, :], ALU.add).then_inc(asem["summed"], 1)
                pool.wait_ge(asem["summed"], t + 1)
                pool.sem_inc(asem["agg_free"], 1)

            def rel_prod(t, u, k):
                pool.wait_ge(asem["q_ready"], t + 1)
                for i in range(2):
                    pool.wait_ge(asem["pool_prod_used"], 2 * t + i + 1)
                    pool.tensor_tensor(as3(pprod, D), Q[:, 4 + i:5 + i, :].broadcast_to([P, REL, D]), K[:, :, :],
                                       ALU.mult).then_inc(asem["pool_prod"], 1)
            tiles_lagged(pool, rel_sum, rel_prod)
            phase_end(pool, 14)
            tiles(pool, prj1.fill_from_rows(pool, rows[:, :]))
            phase_end(pool, 15)
            tiles(pool, prj2.fill_from_rows(pool, rows[:, :]))
            phase_end(pool, 16)
            phase_end(pool, 17)
            pool.memset(blk, 0.0)
            pool.drain().then_inc(blk_cleared, 1)
            phase_end(pool, 18)
            ln[3].gpsimd(pool)
            phase_end(pool, 19)
            att1.gpsimd(pool)
            phase_end(pool, 20)
            tiles(pool, prj3.fill_from_rows(pool, rows[:, :]))
            phase_end(pool, 21)
            phase_end(pool, 22)
            ln[4].gpsimd(pool)
            phase_end(pool, 23)
            phase_end(pool, 24)
            ln[5].gpsimd(pool)
            phase_end(pool, 25)
            pool.iota(e_col_i, [[2, 16]], base=0, channel_multiplier=0)
            pool.iota(iota32_i, [[1, EXP]], base=0, channel_multiplier=0)
            pool.drain().then_inc(rsem["consts"], 1)

            def fill_ro(t, u, k):
                pool.wait_ge(rsem["logits"], t + 1)
                own(pool, "pool")
                pool.tensor_copy(lt_ro[:, u, :, :], xnT[:, :, bass.ds(t * P, P)]).then_inc(rsem["lt_ready"], 1)
            tiles(pool, fill_ro)
            phase_end(pool, 26)
            phase_end(pool, 27)

        @block.scalar
        def _(act):
            act.preload_act_table(ACT.Exp)
            phase_end(act, 1)
            ln[0].scalar(act)
            phase_end(act, 2)
            phase_end(act, 3)
            att0.scalar(act)
            phase_end(act, 4)
            prj0.scalar(act)
            phase_end(act, 5)
            msg[0].scalar(act)
            phase_end(act, 6)
            prjg.scalar(act)
            phase_end(act, 7)
            ln[1].scalar(act)
            phase_end(act, 8)
            act.sem_inc(gsem["exp"], 2)

            def gate_exp(t, u, k):
                act.wait_ge(gsem["shifted"], t + 1)
                act.activation(gt_l[:, u, :], gt_l[:, u, :], ACT.Exp).then_inc(gsem["exp"], 1)
                act.wait_ge(gsem["turned"], t + 1)
                act.activation(gT[:, u, :], ps[2 + u][0:MOE, 0:P], ACT.Copy).then_inc(gsem["copied"], 1)
            tiles(act, gate_exp)
            phase_end(act, 9)
            act.sem_inc(unit_out, 8)
            with act.Fori(0, MOE // 2) as k:
                for u in range(2):
                    with act.Fori(0, CHUNKS) as c_:
                        ex = 2 * k + u
                        g = ex * CHUNKS + c_
                        for layer in range(2):
                            dst = (h1, h2)[layer]
                            for j in range(4):
                                h, oc = j // 2, j % 2
                                off, n = HALVES[h]
                                act.wait_ge(unit_done, g * 8 + 4 * layer + j + 1)
                                own(act, "act")
                                act.activation(dst[:, oc, off:off + n], ps[j][:, 0:n], ACT.Relu,
                                               scale=bns[:, 2 * layer, bass.ds(ex * 2 + oc, 1)],
                                               bias=bns[:, 2 * layer + 1, bass.ds(ex * 2 + oc, 1)]).then_inc(unit_out, 1)
            phase_end(act, 10)
            ln[2].scalar(act)
            phase_end(act, 11)
            phase_end(act, 12)
            msg[1].scalar(act)
            phase_end(act, 13)
            act.sem_inc(asem["moved"], 1)

            def rel_move(t, u, k):
                act.wait_ge(asem["turned"], t + 2)
                act.wait_ge(asem["qkv"], REL * t + 1)
                for b in range(3):
                    a = act.activation(aT[:, 4 * b:4 * b + 4, :], as3(ps[b][:, 0:4 * P], P), ACT.Copy)
                a.then_inc(asem["moved"], 1)
                act.wait_ge(asem["shifted"], t + 1)
                act.activation(scores, scores, ACT.Exp, scale=HD ** -0.5).then_inc(asem["exp"], 1)
            tiles(act, rel_move)
            phase_end(act, 14)
            prj1.scalar(act)
            phase_end(act, 15)
            prj2.scalar(act)
            phase_end(act, 16)
            phase_end(act, 17)
            phase_end(act, 18)
            ln[3].scalar(act)
            phase_end(act, 19)
            att1.scalar(act)
            phase_end(act, 20)
            prj3.scalar(act)
            phase_end(act, 21)
            phase_end(act, 22)
            ln[4].scalar(act)
            phase_end(act, 23)
            act.preload_act_table(ACT.Gelu)
            act.sem_inc(m1_out, 4)
            with act.Fori(0, CHUNKS) as c_:
                for j in range(16):
                    h, oc = j // 8, j % 8
                    off, n = HALVES[h]
                    act.wait_ge(m1_mm, c_ * 16 + j + 1)
                    act.activation(m_h[:, oc, off:off + n], ps[j % 4][:, 0:n], ACT.Gelu,
                                   bias=b_m1[:, oc:oc + 1]).then_inc(m1_out, 1)
            act.preload_act_table(ACT.Exp)
            phase_end(act, 24)
            ln[5].scalar(act)
            phase_end(act, 25)

            def ro_copy(t, u, k):
                act.wait_ge(rsem["turned"], t + 1)
                own(act, "act")
                act.activation(ohT[:, bass.ds(t * P, P)], ps[2 + u][0:EXP, 0:P], ACT.Copy)
                act.activation(idxT[:, bass.ds(t * P, P)], ps[4 + u][:, 0:P], ACT.Copy).then_inc(rsem["copied"], 1)
            act.sem_inc(rsem["copied"], 2)
            tiles(act, ro_copy)
            phase_end(act, 26)
            act.sem_inc(x_relu, 4)
            with act.Fori(0, CHUNKS) as c_:
                for j in range(32):
                    h, pc = j // 16, j % 16
                    off, n = HALVES[h]
                    act.wait_ge(x_mm, c_ * 32 + j + 1)
                    act.activation(e_h[:, pc, off:off + n], ps[j % 4][:, 0:n], ACT.Relu,
                                   bias=b_1[:, pc:pc + 1]).then_inc(x_relu, 1)
            phase_end(act, 27)

        @block.tensor
        def _(pe):
            pe.wait_ge(edge_ready, 1)
            pe.wait_ge(consts_ready, 1)
            for i, a in enumerate((src_f, dst_f, key1_f, gat1_f, raw_w)):
                for b in range(EBLK):
                    mm = pe.transpose(ps[i][0:P, b * EROWS:(b + 1) * EROWS], as3(a, P)[:, b, :], ident[0:EROWS, 0:EROWS])
            mm.then_inc(edge_turned, 1)
            phase_end(pe, 1)
            ln[0].tensor(pe)
            phase_end(pe, 2)
            phase_end(pe, 3)
            att0.tensor(pe)
            phase_end(pe, 4)
            prj0.tensor(pe)
            phase_end(pe, 5)
            msg[0].tensor(pe)
            phase_end(pe, 6)
            prjg.tensor(pe)
            phase_end(pe, 7)
            ln[1].tensor(pe)
            phase_end(pe, 8)
            pe.wait_ge(bn_ready, 1)
            pe.sem_inc(gsem["logits"], 2)

            def logits(t, u, k):
                pe.wait_ge(gsem["lt_ready"], t + 1)
                pe.wait_ge(gsem["exp"], t + 1)
                for c_ in range(2):
                    mm = pe.matmul(ps[u][0:P, 0:MOE], ltg[:, u, c_, :], w_r[:, c_, :], start=(c_ == 0), stop=(c_ == 1))
                mm.then_inc(gsem["logits"], 1)

            def gate_bias(t, u, k):
                pe.wait_ge(gsem["ready"], t + 1)
                pe.transpose(ps[2 + u][0:MOE, 0:P], gt_l[:, u, :], ident[0:P, 0:P]).then_inc(gsem["turned"], 1)
                pe.wait_ge(gsem["copied"], t + 1)
                pe.wait_ge(gsem["bias_used"], t + 1)
                pe.matmul(ps[4 + u][0:P, 0:D], gT[:, u, :], bo_sb, start=True, stop=True).then_inc(gsem["bias"], 1)
            tiles_lagged(pe, logits, gate_bias)
            phase_end(pe, 9)
            pe.sem_inc(we_used, 2)
            with pe.Fori(0, MOE // 2) as k:
                for u in range(2):
                    pe.wait_ge(we_loaded[u], 48 * (k + 1))
                    own(pe, "pe")
                    with pe.Fori(0, CHUNKS) as c_:
                        g = (2 * k + u) * CHUNKS + c_
                        for layer in range(2):
                            for j in range(4):
                                h, oc = j // 2, j % 2
                                off, n = HALVES[h]
                                if layer == 0:
                                    pe.wait_ge(unit_out, 8 * g + j + 5)
                                else:
                                    pe.wait_ge(unit_out, 8 * g + 8 + (2 if j < 2 else 4))
                                for c2 in range(2):
                                    rhs = xnT[:, c2, bass.ds(c_ * CHUNK + off, n)] if layer == 0 else h1[:, c2, off:off + n]
                                    mm = pe.matmul(ps[j][:, 0:n], w_e[:, u, layer, c2, oc * 128:(oc + 1) * 128], rhs,
                                                   start=(c2 == 0), stop=(c2 == 1))
                                mm.then_inc(unit_done, 1)
                        for i in range(TPC):
                            pe.wait_ge(unit_out, 8 * g + 8 + (6 if (i + 1) * P <= HALVES[0][1] else 8))
                            pe.wait_ge(y_out, 5 * g + (5 if i == 0 else 6 if i == 4 else i + 1))
                            for c2 in range(2):
                                mm = pe.matmul(ps[4 + i % 4][0:P, 0:D], h2[:, c2, i * P:(i + 1) * P], w_e[:, u, 2, c2, :],
                                               start=(c2 == 0), stop=(c2 == 1))
                            mm.then_inc(y_done, 1)
                    pe.drain().then_inc(we_used, 1)
            phase_end(pe, 10)
            ln[2].tensor(pe)
            phase_end(pe, 11)
            pe.wait_ge(rel_dma[0], 16)
            pe.sem_inc(rel_mm, 2)

            def rel_rows(t, u, k):
                pe.wait_ge(rel_lt, t + 1)
                pe.wait_ge(rel_moved, t + 1)
                for b in range(3):
                    for c_ in range(2):
                        mm = pe.matmul(ps[3 * u + b][0:P, :], lt_rel[:, u, c_, :], w_rel[:, c_, b * 512:(b + 1) * 512],
                                       start=(c_ == 0), stop=(c_ == 1))
                mm.then_inc(rel_mm, 1)
            tiles(pe, rel_rows)
            phase_end(pe, 12)
            msg[1].tensor(pe)
            phase_end(pe, 13)
            pe.wait_ge(asem["w"], 32)
            pe.sem_inc(asem["turned"], 1)
            pe.sem_inc(asem["qkv"], 1)

            def rel_turn(t, u, k):
                pe.wait_ge(asem["summed"], t + 1)
                pe.wait_ge(asem["moved"], t + 1)
                for r in range(REL):
                    for c_ in range(2):
                        i = 2 * r + c_
                        mm = pe.transpose(ps[i // 4][:, (i % 4) * P:(i % 4 + 1) * P],
                                          agsum[:, r * D + c_ * 128:r * D + (c_ + 1) * 128], ident[0:P, 0:P])
                mm.then_inc(asem["turned"], 1)

            def rel_qkv(t, u, k):
                pe.wait_ge(asem["moved"], t + 2)
                for r in range(REL):
                    pe.wait_ge(asem["qkv_out"], REL * t + r + 1)
                    b = 3 + 2 * (r % 2)
                    for c_ in range(2):
                        pe.matmul(ps[b][0:P, 0:512], aT[:, 2 * r + c_, :], w_in[:, c_, 0:512],
                                  start=(c_ == 0), stop=(c_ == 1))
                    for c_ in range(2):
                        mm = pe.matmul(ps[b + 1][0:P, 0:D], aT[:, 2 * r + c_, :], w_in[:, c_, 512:768],
                                       start=(c_ == 0), stop=(c_ == 1))
                    mm.then_inc(asem["qkv"], 1)
            def rel_both(t, u, k):
                rel_turn(t, u, k)
                rel_qkv(t, u, k)
            tiles(pe, rel_both)
            phase_end(pe, 14)
            prj1.tensor(pe)
            phase_end(pe, 15)
            prj2.tensor(pe)
            phase_end(pe, 16)
            phase_end(pe, 17)
            pe.wait_ge(mix1_loaded, 96)
            pe.wait_ge(blk_loaded, 16 * 12)
            for oc in range(2):
                for ic in range(2):
                    mm = pe.matmul(ps[2 * oc + ic][:, 0:384], w_x[:, oc, ic * 128:(ic + 1) * 128], blk,
                                   start=True, stop=True)
                mm = pe.matmul(ps[4 + oc][0:P, 0:384], b_x[:, oc:oc + 1].broadcast_to([128, P]), blk, start=True, stop=True)
            mm.then_inc(fold_mm, 1)
            phase_end(pe, 18)
            ln[3].tensor(pe)
            phase_end(pe, 19)
            att1.tensor(pe)
            phase_end(pe, 20)
            prj3.tensor(pe)
            phase_end(pe, 21)
            phase_end(pe, 22)
            ln[4].tensor(pe)
            phase_end(pe, 23)
            with pe.Fori(0, CHUNKS) as c_:
                for j in range(16):
                    h, oc = j // 8, j % 8
                    off, n = HALVES[h]
                    pe.wait_ge(m1_out, c_ * 16 + j + 1)
                    for c2 in range(2):
                        mm = pe.matmul(ps[j % 4][:, 0:n], w_m1[:, c2, oc * 128:(oc + 1) * 128],
                                       xnT[:, c2, bass.ds(c_ * CHUNK + off, n)], start=(c2 == 0), stop=(c2 == 1))
                    mm.then_inc(m1_mm, 1)
                for i in range(TPC):
                    pe.wait_ge(m1_out, c_ * 16 + 4 + (8 if (i + 1) * P <= HALVES[0][1] else 16))
                    pe.wait_ge(m2_out, 5 * c_ + (5 if i == 0 else 6 if i == 4 else i + 1))
                    for c2 in range(8):
                        mm = pe.matmul(ps[4 + i % 4][0:P, 0:D], m_h[:, c2, i * P:(i + 1) * P], w_m2[:, c2, :],
                                       start=(c2 == 0), stop=(c2 == 7))
                    mm.then_inc(m2_mm, 1)
            phase_end(pe, 24)
            ln[5].tensor(pe)
            phase_end(pe, 25)
            pe.wait_ge(ffn1_loaded, 96)
            pe.sem_inc(rsem["logits"], 2)

            def ro_logits(t, u, k):
                pe.wait_ge(rsem["lt_ready"], t + 1)
                pe.wait_ge(rsem["ready"], t + 1)
                for c_ in range(2):
                    mm = pe.matmul(ps[u][0:P, 0:EXP], lt_ro[:, u, c_, :], w_ro[:, c_, :], start=(c_ == 0), stop=(c_ == 1))
                mm.then_inc(rsem["logits"], 1)

            def ro_turn(t, u, k):
                pe.wait_ge(rsem["ready"], t + 3)
                pe.wait_ge(rsem["copied"], t + 1)
                pe.transpose(ps[2 + u][0:EXP, 0:P], ro_h[:, u, :], ident[0:P, 0:P])
                pe.matmul(ps[4 + u][:, 0:P], ro_f[:, u:u + 1].broadcast_to([P, 128]), ident[0:P, 0:P],
                          start=True, stop=True).then_inc(rsem["turned"], 1)
            tiles_lagged(pe, ro_logits, ro_turn)
            phase_end(pe, 26)
            with pe.Fori(0, CHUNKS) as c_:
                for j in range(32):
                    h, pc = j // 16, j % 16
                    off, n = HALVES[h]
                    pe.wait_ge(x_relu, c_ * 32 + j + 1)
                    for c2 in range(2):
                        mm = pe.matmul(ps[j % 4][:, 0:n], w_1[:, c2, pc * 128:(pc + 1) * 128],
                                       xnT[:, c2, bass.ds(c_ * CHUNK + off, n)], start=(c2 == 0), stop=(c2 == 1))
                    mm.then_inc(x_mm, 1)
                for i in range(TPC):
                    pe.wait_ge(x_masked, c_ * 32 + (16 if (i + 1) * P <= HALVES[0][1] else 32))
                    pe.wait_ge(x_yout, 5 * c_ + (5 if i == 0 else 6 if i == 4 else i + 1))
                    for c2 in range(16):
                        pe.matmul(ps[4 + i % 4][0:P, 0:D], e_h[:, c2, i * P:(i + 1) * P], w_2[:, c2, :],
                                  start=(c2 == 0), stop=False)
                    pe.matmul(ps[4 + i % 4][0:P, 0:D], e_hot[:, i * P:(i + 1) * P], b_2, start=False, stop=True
                              ).then_inc(x_y, 1)
            phase_end(pe, 27)

        @block.vector
        def _(v):
            v.wait_ge(edge_loaded, 64)
            for a, b in ((src_f, raw_i[0]), (dst_f, raw_i[1]), (typ_f, raw_i[2])):
                v.tensor_copy(a, b)
            v.drain()
            v.scalar_tensor_tensor(out=key1_f, in0=typ_f, scalar=float(NODES), in1=dst_f, op0=ALU.mult, op1=ALU.add)
            v.scalar_tensor_tensor(out=gat1_f, in0=typ_f, scalar=float(NODES), in1=src_f, op0=ALU.mult, op1=ALU.add)
            v.drain().then_inc(edge_ready, 1)
            v.wait_ge(edge_turned, 1)
            v.tensor_copy(key_col[0][:, :], ps[0][0:P, 0:ETILES])
            v.tensor_copy(gather_col[0][:, :], ps[1][0:P, 0:ETILES])
            v.tensor_copy(key_col[1][:, :], ps[2][0:P, 0:ETILES])
            v.tensor_copy(gather_col[1][:, :], ps[3][0:P, 0:ETILES])
            v.tensor_copy(weight_col[:, :], ps[4][0:P, 0:ETILES])
            v.drain()
            for la in range(2):
                v.tensor_scalar(spare_gap[la][:, :], key_col[la][:, :], -1.0, float(SEGS[la]), ALU.mult, ALU.add)
            v.drain()
            for la in range(2):
                v.tensor_scalar(spare_gap[la][:, :], spare_gap[la][:, :], lane[0:P, 0:1], None, ALU.add)
            v.wait_ge(x_loaded, 16)
            phase_end(v, 1)
            ln[0].vector(v)
            phase_end(v, 2)
            phase_end(v, 3)
            att0.vector(v)
            phase_end(v, 4)
            v.sem_inc(prj0.used.sem, 2)

            def add_mix0(t, u, k):
                v.wait_ge(prj0.product.sem, prj0.product.base + t + 3)
                v.bn_stats(out=cs_st[:, u, :], in_=prj0.out(u))
                v.drain()
                v.bn_aggr(out=cs_mv[:, u, :], in_=cs_st[:, u, :])
                v.drain()
                v.tensor_scalar(cs_ve[:, u:u + 1], cs_mv[:, u, 1:2], EPS, None, ALU.add).then_inc(var0, 1)
                v.wait_ge(rstd0, t + 1)
                v.tensor_scalar(cs_o[:, u, :], prj0.out(u), cs_mv[:, u, 0:1], cs_rs[:, u:u + 1], ALU.subtract, ALU.mult)
                v.drain().then_inc(prj0.used.sem, 1)
                v.tensor_tensor(cs_o[:, u, :], cs_o[:, u, :], gamma0, ALU.mult)
                v.drain()
                v.tensor_tensor(col(x_cur, t * D, D), col(x_cur, t * D, D), cs_o[:, u, :], ALU.add)
            tiles(v, add_mix0)
            phase_end(v, 5)
            msg[0].vector(v)
            phase_end(v, 6)
            v.wait_ge(gnn0_loaded, 96)
            v.sem_inc(prjg.used.sem, 2)

            def add_gnn0(t, u, k):
                y = g_y[:, u, :]
                v.wait_ge(prjg.product.sem, prjg.product.base + t + 3)
                v.tensor_tensor(y, prjg.out(u), gnn_rows[:, 0, :], ALU.add)
                v.drain().then_inc(prjg.used.sem, 1)
                for h in range(HEADS):
                    v.bn_stats(out=g_st[:, u, h, :], in_=y[:, h * HD:(h + 1) * HD])
                v.drain()
                for h in range(HEADS):
                    v.bn_aggr(out=g_mv[:, u, h, :], in_=g_st[:, u, h, :])
                v.drain()
                v.tensor_scalar(g_ve[:, u, :], g_mv[:, u, :, 1], EPS, None, ALU.add).then_inc(gvar, 1)
                v.wait_ge(grstd, 2 * t + 1)
                for h in range(HEADS):
                    yh = y[:, h * HD:(h + 1) * HD]
                    v.tensor_scalar(yh, yh, g_mv[:, u, h, 0:1], g_rs[:, u, h:h + 1], ALU.subtract, ALU.mult)
                v.drain()
                v.tensor_tensor(y, y, gnn_rows[:, 1, :], ALU.mult)
                v.drain()
                v.tensor_tensor(y, y, gnn_rows[:, 2, :], ALU.add)
                v.drain()
                v.bn_stats(out=g_st[:, u, 0, :], in_=y)
                v.drain()
                v.bn_aggr(out=g_mv[:, u, 0, :], in_=g_st[:, u, 0, :])
                v.drain()
                v.tensor_scalar(g_ve[:, u, 0:1], g_mv[:, u, 0, 1:2], EPS, None, ALU.add).then_inc(gvar, 1)
                v.wait_ge(grstd, 2 * t + 2)
                v.tensor_scalar(y, y, g_mv[:, u, 0, 0:1], g_rs[:, u, 0:1], ALU.subtract, ALU.mult)
                v.drain()
                v.tensor_tensor(y, y, gnn_rows[:, 3, :], ALU.mult)
                v.drain()
                v.tensor_tensor(y, y, gnn_rows[:, 4, :], ALU.add)
                v.drain()
                v.tensor_tensor(col(x_cur, t * D, D), col(x_cur, t * D, D), y, ALU.add)
            tiles(v, add_gnn0)
            phase_end(v, 7)
            ln[1].vector(v)
            phase_end(v, 8)
            v.wait_ge(ffn0_loaded, 13 * 16)
            for i in (0, 1):
                v.tensor_scalar(bns[:, 2 * i, :], bnp[:, 5 * i + 4, :], BN_EPS, None, ALU.add)
            v.drain().then_inc(bn_var, 1)
            v.wait_ge(bn_rstd, 1)
            for i in (0, 1):
                b_, g_, be_, m_, _ = (bnp[:, 5 * i + q, :] for q in range(5))
                v.tensor_tensor(bns[:, 2 * i, :], bns[:, 2 * i, :], g_, ALU.mult)
                v.tensor_tensor(bns[:, 2 * i + 1, :], b_, m_, ALU.subtract)
                v.drain()
                v.tensor_tensor(bns[:, 2 * i + 1, :], bns[:, 2 * i + 1, :], bns[:, 2 * i, :], ALU.mult)
                v.drain()
                v.tensor_tensor(bns[:, 2 * i + 1, :], bns[:, 2 * i + 1, :], be_, ALU.add)
            v.drain().then_inc(bn_ready, 1)
            v.sem_inc(gsem["bias_used"], 2)

            def gates(t, u, k):
                l = gt_l[:, u, :]
                v.wait_ge(gsem["logits"], t + 3)
                v.wait_ge(gsem["bias_used"], t + 1)
                v.tensor_tensor(l, ps[u][0:P, 0:MOE], br_row, ALU.add)
                v.drain()
                v.tensor_reduce(gt_s[:, u:u + 1], l, AX.X, ALU.max)
                v.drain()
                v.tensor_scalar(l, l, gt_s[:, u:u + 1], None, ALU.subtract)
                v.drain().then_inc(gsem["shifted"], 1)
                v.wait_ge(gsem["exp"], t + 3)
                v.tensor_reduce(gt_s[:, u:u + 1], l, AX.X, ALU.add)
                v.drain()
                v.reciprocal(gt_s[:, u:u + 1], gt_s[:, u:u + 1])
                v.drain()
                v.tensor_scalar(l, l, gt_s[:, u:u + 1], None, ALU.mult)
                v.drain().then_inc(gsem["ready"], 1)
                v.tensor_scalar(col(gate, t * MOE, MOE), l, 1.0, None, ALU.mult)
                v.wait_ge(gsem["bias"], t + 1)
                v.tensor_tensor(col(x_cur, t * D, D), col(x_cur, t * D, D), ps[4 + u][0:P, 0:D], ALU.add)
                v.drain().then_inc(gsem["bias_used"], 1)
            tiles(v, gates)
            phase_end(v, 9)
            v.sem_inc(y_out, 5)
            with v.Fori(0, MOE // 2) as k:
                for u in range(2):
                    with v.Fori(0, CHUNKS) as c_:
                        ex = 2 * k + u
                        for i in range(TPC):
                            t = c_ * TPC + i
                            v.wait_ge(y_done, 5 * (ex * CHUNKS + c_) + i + 1)
                            own(v, "dve")
                            v.scalar_tensor_tensor(out=col(x_cur, t * D, D), in0=ps[4 + i % 4][0:P, 0:D],
                                                   scalar=col(gate, t * MOE + ex), in1=col(x_cur, t * D, D),
                                                   op0=ALU.mult, op1=ALU.add).then_inc(y_out, 1)
                        v.drain()
            phase_end(v, 10)
            ln[2].vector(v)
            phase_end(v, 11)
            v.wait_ge(rel_dma[1], 16)
            v.sem_inc(rel_moved, 2)

            def rel_bias(t, u, k):
                v.wait_ge(rel_mm, t + 3)
                v.wait_ge(rel_dma[u], 16 * (k + 1))
                for b in range(3):
                    v.tensor_tensor(rel_out[:, u, b * 512:(b + 1) * 512], ps[3 * u + b][0:P, :],
                                    b_rel[:, b * 512:(b + 1) * 512], ALU.add)
                v.drain().then_inc(rel_moved, 1)
            tiles(v, rel_bias)
            phase_end(v, 12)
            msg[1].vector(v)
            phase_end(v, 13)
            v.wait_ge(asem["w"], 32)
            v.sem_inc(asem["qkv_out"], 2)
            v.sem_inc(asem["pool_prod_used"], 1)
            s3 = scores.rearrange("p (r s h) -> p r s h", r=REL, s=REL)
            s_in = scores.rearrange("p (r s h) -> p r h s", r=REL, s=REL)
            rh = sc24.rearrange("p (r h) -> p r h", r=REL)

            def rel_attend(t, u, k):
                for r in range(REL):
                    b = 3 + 2 * (r % 2)
                    v.wait_ge(asem["qkv"], REL * t + r + 2)
                    v.tensor_tensor(Q[:, r, :], ps[b][0:P, 0:D], b_in[:, 0:D], ALU.add)
                    v.tensor_tensor(K[:, r, :], ps[b][0:P, D:2 * D], b_in[:, D:2 * D], ALU.add)
                    v.tensor_tensor(V[:, r, :], ps[b + 1][0:P, 0:D], b_in[:, 2 * D:3 * D], ALU.add)
                    v.drain().then_inc(asem["qkv_out"], 1)
                v.sem_inc(asem["q_ready"], 1)
                for r in range(4):
                    v.tensor_tensor(as3(prod, D), Q[:, r:r + 1, :].broadcast_to([P, REL, D]), K[:, :, :], ALU.mult)
                    v.drain()
                    v.tensor_reduce(scores[:, r * 24:(r + 1) * 24], as3(prod, HD), AX.X, ALU.add)
                    v.drain()
                    if r % 2:
                        i = r // 2
                        v.wait_ge(asem["pool_prod"], 2 * t + i + 1)
                        v.tensor_reduce(scores[:, (4 + i) * 24:(5 + i) * 24], as3(pprod, HD), AX.X, ALU.add)
                        v.drain().then_inc(asem["pool_prod_used"], 1)
                for r in range(REL):
                    v.tensor_reduce(rh[:, r, :], s_in[:, r, :, :], AX.X, ALU.max)
                v.drain()
                for r in range(REL):
                    v.tensor_tensor(s3[:, r, :, :], s3[:, r, :, :], rh[:, r:r + 1, :].broadcast_to([P, REL, HEADS]), ALU.subtract)
                v.drain().then_inc(asem["shifted"], 1)
                v.wait_ge(asem["exp"], t + 1)
                for r in range(REL):
                    v.tensor_reduce(rh[:, r, :], s_in[:, r, :, :], AX.X, ALU.add)
                v.drain()
                v.tensor_scalar(sc24, sc24, float(REL), None, ALU.mult)
                v.drain()
                v.reciprocal(sc24, sc24)
                v.drain()
                for r in range(REL):
                    v.tensor_tensor(s3[:, r, :, :], s3[:, r, :, :], rh[:, r:r + 1, :].broadcast_to([P, REL, HEADS]), ALU.mult)
                v.drain()
                v.tensor_reduce(pbar, scores.rearrange("p (r a) -> p a r", r=REL), AX.X, ALU.add)
                v.drain()
                v.tensor_tensor(as3(prod, HD), V[:, :, :].rearrange("p r (h c) -> p (r h) c", c=HD),
                                over(pbar, HD), ALU.mult)
                v.drain()
                v.tensor_reduce(vsum, prod.rearrange("p (s d) -> p d s", s=REL), AX.X, ALU.add)
                v.drain()
                v.tensor_scalar(col(rows, t * D, D), vsum, 1.0, None, ALU.mult)
                v.drain()
            tiles(v, rel_attend)
            phase_end(v, 14)
            v.wait_ge(prj_loaded, 64)
            v.sem_inc(prj1.used.sem, 2)

            def out1(t, u, k):
                v.wait_ge(prj1.product.sem, prj1.product.base + t + 3)
                v.tensor_tensor(prj_tmp[:, u, :], prj1.out(u), b_ao, ALU.add)
                v.drain().then_inc(prj1.used.sem, 1)
                v.tensor_tensor(col(rows, t * D, D), col(xn, t * D, D), prj_tmp[:, u, :], ALU.add)
            tiles(v, out1)
            phase_end(v, 15)
            v.sem_inc(prj2.used.sem, 2)

            def out2(t, u, k):
                v.wait_ge(prj2.product.sem, prj2.product.base + t + 3)
                v.tensor_tensor(prj_tmp[:, u, :], prj2.out(u), b_pr, ALU.add)
                v.drain().then_inc(prj2.used.sem, 1)
                v.tensor_tensor(col(x_cur, t * D, D), col(x_cur, t * D, D), prj_tmp[:, u, :], ALU.add)
            tiles(v, out2)
            phase_end(v, 16)
            phase_end(v, 17)
            v.wait_ge(fold_mm, 1)
            for oc in range(2):
                for q in range(3):
                    for ic in range(2):
                        v.tensor_copy(w_qkv1[:, ic, q * D + oc * 128:q * D + (oc + 1) * 128],
                                      ps[2 * oc + ic][:, q * 128:(q + 1) * 128])
                    v.tensor_copy(bias1[:, q * D + oc * 128:q * D + (oc + 1) * 128], ps[4 + oc][0:P, q * 128:(q + 1) * 128])
            phase_end(v, 18)
            ln[3].vector(v)
            phase_end(v, 19)
            att1.vector(v)
            phase_end(v, 20)
            v.sem_inc(prj3.used.sem, 2)

            def out3(t, u, k):
                v.wait_ge(prj3.product.sem, prj3.product.base + t + 3)
                v.tensor_tensor(p3_tmp[:, u, :], prj3.out(u), b_o1, ALU.add)
                v.drain().then_inc(prj3.used.sem, 1)
                v.tensor_tensor(col(rows, t * D, D), col(xn, t * D, D), p3_tmp[:, u, :], ALU.add)
            tiles(v, out3)
            phase_end(v, 21)
            phase_end(v, 22)
            ln[4].vector(v)
            phase_end(v, 23)
            v.sem_inc(m2_out, 5)
            with v.Fori(0, CHUNKS) as c_:
                for i in range(TPC):
                    t = c_ * TPC + i
                    v.wait_ge(m2_mm, 5 * c_ + i + 1)
                    v.tensor_tensor(m_o[:, i % 2, :], ps[4 + i % 4][0:P, 0:D], b_m2, ALU.add)
                    v.drain().then_inc(m2_out, 1)
                    v.tensor_tensor(m_o[:, i % 2, :], m_o[:, i % 2, :], col(rows, t * D, D), ALU.add)
                    v.drain()
                    v.tensor_tensor(col(x_cur, t * D, D), col(x_cur, t * D, D), m_o[:, i % 2, :], ALU.add)
                    v.drain()
            phase_end(v, 24)
            ln[5].vector(v)
            phase_end(v, 25)
            v.wait_ge(ffn1_loaded, 96)
            v.wait_ge(rsem["consts"], 1)
            v.tensor_copy(e_col, e_col_i)
            v.tensor_copy(iota32, iota32_i)
            v.drain()
            v.tensor_scalar(e_col[EH:128, :], e_col[EH:128, :], 1.0, None, ALU.add)
            v.sem_inc(rsem["ready"], 2)

            def route(t, u, k):
                v.wait_ge(rsem["logits"], t + 3)
                v.wait_ge(rsem["copied"], t + 1)
                v.tensor_tensor(ro_l[:, u, :], ps[u][0:P, 0:EXP], b_ro, ALU.add)
                v.drain()
                v.max(ro_m[:, u, :], ro_l[:, u, :])
                v.drain()
                v.max_index(ro_i[:, u, :], ro_m[:, u, :], ro_l[:, u, :])
                v.drain()
                v.tensor_copy(ro_f[:, u:u + 1], ro_i[:, u, 0:1])
                v.drain()
                v.tensor_scalar(ro_h[:, u, :], iota32, ro_f[:, u:u + 1], None, ALU.is_equal)
                v.drain().then_inc(rsem["ready"], 1)
            tiles(v, route)
            phase_end(v, 26)
            v.sem_inc(x_yout, 5)
            with v.Fori(0, CHUNKS) as c_:
                v.drain()
                v.tensor_scalar(e_hot, ohT[:, bass.ds(c_ * CHUNK, CHUNK)], 1.0, None, ALU.mult)
                v.drain()
                for j in range(32):
                    h, pc = j // 16, j % 16
                    off, n = HALVES[h]
                    v.wait_ge(x_relu, c_ * 32 + 4 + j + 1)
                    v.scalar_tensor_tensor(out=e_h[:, pc, off:off + n], in0=idxT[:, bass.ds(c_ * CHUNK + off, n)],
                                           scalar=e_col[:, pc:pc + 1], in1=e_h[:, pc, off:off + n],
                                           op0=ALU.is_equal, op1=ALU.mult).then_inc(x_masked, 1)
                for i in range(TPC):
                    t = c_ * TPC + i
                    v.wait_ge(x_y, 5 * c_ + i + 1)
                    own(v, "dve")
                    v.scalar_tensor_tensor(out=col(x_cur, t * D, D), in0=ps[4 + i % 4][0:P, 0:D], scalar=0.0,
                                           in1=col(x_cur, t * D, D), op0=ALU.max, op1=ALU.add).then_inc(x_yout, 1)
            phase_end(v, 27)


def kernel(**inputs):
    import numpy as _np
    import concourse.bacc as _bacc
    from concourse import mybir as _mybir
    from concourse.bass_utils import run_bass_kernel_spmd as _run

    a = {k: _np.ascontiguousarray(v) for k, v in inputs.items()}

    def cols(v):
        return v.reshape(-1, 2, 128).transpose(2, 0, 1).reshape(128, -1)

    lay = {n: a[n] for n in ("x", "src", "dst", "edge_type_6", "edge_weight", "L0_gnn_ln2_g", "L0_gnn_ln2_b",
                             "L0_mix_Wqkv", "L0_mix_Wout", "L0_mix_gamma", "L0_ffn_Wr", "L0_ffn_br", "L0_ffn_bo",
                             "L1_gnn_in_proj_b", "L1_gnn_attn_out_b", "L1_gnn_proj_b", "L1_mix_Wx", "L1_mix_bo",
                             "L1_mix_b2", "L1_ffn_router_b", "L1_ffn_b2")}
    for n in ("L0_gnn_bias", "L0_gnn_ln1_g", "L0_gnn_ln1_b", "L1_gnn_b"):
        lay[n] = a[n].reshape(-1)
    for n in ("b1", "g1", "be1", "m1", "v1", "b2", "g2", "be2", "m2", "v2"):
        lay["L0_ffn_" + n] = cols(a["L0_ffn_" + n])
    for n in ("W1", "W2", "Wo"):
        lay["L0_ffn_" + n] = a["L0_ffn_" + n].reshape(-1, 256)
    lay["gnn0_W"] = a["L0_gnn_W"].transpose(1, 0, 2).reshape(256, 256)
    lay["gnn1_W"] = a["L1_gnn_W"].transpose(1, 0, 2).reshape(256, -1)
    lay["gnn1_in_T"] = a["L1_gnn_in_proj_w"].T
    lay["gnn1_ao_T"] = a["L1_gnn_attn_out_w"].T
    lay["gnn1_pr_T"] = a["L1_gnn_proj_w"].T
    for n in ("ln1_w", "ln1_b", "ln2_w", "ln2_b", "bx"):
        lay["mix1_" + n] = cols(a["L1_mix_" + n])
    lay["mix1_b1"] = a["L1_mix_b1"].reshape(8, 128).T
    for n in ("Wq", "Wk", "Wv", "Wo", "W1", "W2"):
        lay[f"mix1_{n}_T"] = a["L1_mix_" + n].T
    lay["ffn1_W1"] = a["L1_ffn_W1"].transpose(1, 0, 2).reshape(256, -1)
    lay["ffn1_W2"] = a["L1_ffn_W2"].reshape(-1, 256)
    lay["ffn1_b1"] = a["L1_ffn_b1"].reshape(16, 128).T
    lay["ffn1_router_T"] = a["L1_ffn_router_w"].T

    nc = _bacc.Bacc("TRN2", target_bir_lowering=False, num_devices=1)
    arrays, aps = {}, {}
    for n, v in lay.items():
        v = _np.ascontiguousarray(v)
        arrays["in_" + n] = v
        aps[n] = nc.dram_tensor("in_" + n, v.shape, _mybir.dt.from_np(v.dtype), kind="ExternalInput").ap()
    out = nc.dram_tensor("out_rows", (3125, 256), _mybir.dt.float32, kind="ExternalOutput").ap()
    gps_two_layers(nc, aps, out)
    r = _run(nc, [arrays], core_ids=[0])
    return r.results[0]["out_rows"]
```

```python
from contextlib import ExitStack

import numpy as np
import concourse.bass as bass
from concourse import mybir

F32 = mybir.dt.float32
I32 = mybir.dt.int32
U32 = mybir.dt.uint32
ALU = mybir.AluOpType
ACT = mybir.ActivationFunctionType
AX = mybir.AxisListType

NODES = 3125
D = 256
P = 125
TILES = NODES // P
CHUNK = 625
CHUNKS = NODES // CHUNK
HALVES = ((0, 313), (313, 312))
TPC = CHUNK // P
EDGES = 50000
ETILES = EDGES // P
EB = 8
EROWS = 100
EBLK = ETILES // EROWS
REL = 6
HEADS = 4
HD = D // HEADS
MIX_HEADS = 8
MHD = D // MIX_HEADS
MOE = 8
EXP = 32
EH = 64
HID = 1024
EPS = 1e-5
BN_EPS = 1e-3
TABLES = 2
AGG_ROWS = (3328, 18944)
WIDTH = (D, D + 1)
SEGS = (NODES, REL * NODES)
LOOK = 4
TURNS = ETILES // EB


def gps_two_layers(nc, A, out):
    ctx = ExitStack()
    with ctx:
        def sb(name, shape, dt=F32):
            return ctx.enter_context(nc.sbuf_tensor(name, shape, dt))

        def sem(name):
            return ctx.enter_context(nc.semaphore(name))

        def dram(name, shape, dt=F32):
            return nc.dram_tensor(name, shape, dt, kind="Internal").ap()

        ps = [ctx.enter_context(nc.psum_tensor(f"bank{i}", [128, 512], F32)) for i in range(8)]

        x_cur = sb("x_cur", [P, TILES * D])
        xn_whole = sb("xn", [128, TILES * D])
        xn = xn_whole[0:P, :]
        xnT = sb("xnT", [128, 2, NODES])
        rows = sb("rows", [P, TILES * D])
        ident = sb("ident", [128, 128])
        earlier = sb("earlier", [P, P])
        lane = sb("lane", [128, 1])
        lane_i = sb("lane_i", [128, 1], I32)
        neghalf = sb("neghalf", [128, 32])
        edge_cols = sb("edge_cols", [128, 7 * ETILES])
        key0, key1, gap0, gap1, src0, src1, weight_col = (edge_cols[0:P, i * ETILES:(i + 1) * ETILES] for i in range(7))
        key_col, spare_gap = (key0, key1), (gap0, gap1)
        gather_col = (src0.bitcast(I32), src1.bitcast(I32))
        zeros = sb("zeros", [128, D + 1])
        ARENA = 24300
        arena = sb("arena", [128, ARENA])

        xn_table = dram("xn_table", [NODES, D])
        agg = [[dram(f"agg{la}_{k}", [AGG_ROWS[la], WIDTH[la]]) for k in range(TABLES)] for la in range(2)]
        key_row = [dram(f"key_row{la}", [EDGES]) for la in range(2)]

        JOBS_AT = 6400
        NORM_AT = ARENA - 1600

        class Counted:

            def __init__(self, handle, base):
                self.sem, self.base = handle, base

        counts = {}

        def counted(name, total):
            if name not in counts:
                counts[name] = [sem(name), 0]
            handle, base = counts[name]
            counts[name][1] += total
            return Counted(handle, base)

        class Carver:

            def __init__(self):
                self.at = 0

            def __call__(self, parts, cols, dt=F32, **split):
                a = arena[0:parts, self.at:self.at + cols]
                self.at += cols
                assert self.at <= ARENA, self.at
                return a if dt == F32 else a.bitcast(dt)

        phase_done = sem("phase_done")
        engines = 5

        def phase_end(e, n):
            e.drain().then_inc(phase_done, 1)
            e.wait_ge(phase_done, engines * n)

        job_done = sem("job_done")

        def job_end(e, n):
            e.drain().then_inc(job_done, 1)
            e.wait_ge(job_done, 3 * n)

        def weave(e, step, first, turns, pieces):
            with e.Fori(0, turns) as k:
                for u in range(EB):
                    step(e, first + k, u)
                    for piece in pieces.get(u, ()):
                        piece(k)

        paces = {n: sem(f"pace_{n}") for n in ("act", "pool", "dve", "pe")}

        def own(e, name):
            e.sem_inc(paces[name], 1)

        def tiles(e, body, n=2):
            turns = TILES // n
            with e.Fori(0, turns) as k:
                for u in range(n):
                    body(n * k + u, u, k)
            for u in range(TILES % n):
                body(n * turns + u, u, turns)

        def tiles_lagged(e, ahead, behind):
            ahead(0, 0, 0)
            with e.Fori(0, TILES // 2) as k:
                ahead(2 * k + 1, 1, k)
                behind(2 * k, 0, k)
                ahead(2 * k + 2, 0, k + 1)
                behind(2 * k + 1, 1, k)
            behind(TILES - 1, 0, TILES // 2)

        def col(ap, i, n=1):
            return ap[:, bass.ds(i, n)]

        def cm(v):
            return v.rearrange("(c p) n -> p c n", p=128)

        def as3(ap, b):
            return ap.rearrange("p (a b) -> p a b", b=b)

        def over(ap, n):
            return ap.unsqueeze(2).broadcast_to([ap.shape[0], ap.shape[1], n])

        def row_of(v, n, parts=128):
            return v.rearrange("(a n) -> a n", a=1).broadcast_to([parts, n])

        def moments(e, st, half, a, b, q, mean, var):
            n = 2 * half
            e.tensor_tensor(a, st[:, :, 1], st[:, :, 4], ALU.add)
            e.tensor_tensor(b, st[:, :, 1], st[:, :, 4], ALU.subtract)
            e.tensor_tensor(q, st[:, :, 2], st[:, :, 5], ALU.add)
            e.drain()
            e.tensor_scalar(mean, a, 0.5, None, ALU.mult)
            e.tensor_tensor(b, b, b, ALU.mult)
            e.tensor_scalar(q, q, 1.0 / n, EPS, ALU.mult, ALU.add)
            e.drain()
            return e.scalar_tensor_tensor(out=var, in0=b, scalar=0.25, in1=q, op0=ALU.mult, op1=ALU.add)

        class Norm:

            def __init__(s, src, dst, affine, nb=5, turned=True):
                s.src, s.dst, s.affine, s.nb, s.make_turned = src, dst, affine, nb, turned
                s.stats_ready = counted("ln_stats_ready", 1)
                s.rstd_ready = counted("ln_rstd_ready", 1)
                if turned:
                    s.stage_ready = counted("ln_stage_ready", TILES)
                    s.turned = counted("ln_turned", TILES + nb)
                    s.turned_out = counted("ln_turned_out", TILES + nb)
                c = Carver()
                c.at = NORM_AT
                s.st = c(P, TILES * 6)
                s.a, s.b, s.q, s.mean, s.var, s.rstd = [c(P, TILES) for _ in range(6)]
                s.stage = as3(c(P, nb * D), D)
                c.at += 4 * max(0, affine - 1)
                s.gcol, s.bcol = c(128, 2), c(128, 2)

            def stats(s, e):
                def stats_of(t, u, k):
                    e.bn_stats(out=col(s.st, t * 6, 6), in_=col(s.src, t * D, D))
                tiles(e, stats_of, 5)
                e.drain()

            def moments(s, e):
                moments(e, as3(s.st, 6), D // 2, s.a, s.b, s.q, s.mean, s.var).then_inc(s.stats_ready.sem, 1)

            def scale(s, e, t, u):
                e.wait_ge(s.turned.sem, s.turned.base + t + 1)
                e.tensor_scalar(s.stage[:, u, :], col(s.src, t * D, D), col(s.mean, t), col(s.rstd, t),
                                ALU.subtract, ALU.mult).then_inc(s.stage_ready.sem, 1)

            def keep(s, e, t):
                e.tensor_scalar(col(s.dst, t * D, D), col(s.src, t * D, D), col(s.mean, t), col(s.rstd, t),
                                ALU.subtract, ALU.mult)

            def turn(s, e, t, u):
                e.wait_ge(s.stage_ready.sem, s.stage_ready.base + t + 1)
                e.wait_ge(s.turned_out.sem, s.turned_out.base + t + 1)
                e.transpose(ps[u][:, 0:P], s.stage[:, u, 0:128], ident[0:P, 0:P])
                e.transpose(ps[u][:, P:2 * P], s.stage[:, u, 128:256], ident[0:P, 0:P]).then_inc(s.turned.sem, 1)

            def move(s, e, t, u):
                e.wait_ge(s.turned.sem, s.turned.base + t + s.nb + 1)
                own(e, "act")
                if s.affine:
                    e.activation(xnT[:, 0, bass.ds(t * P, P)], ps[u][:, 0:P], ACT.Identity,
                                 bias=s.bcol[:, 0:1], scale=s.gcol[:, 0:1])
                    e.activation(xnT[:, 1, bass.ds(t * P, P)], ps[u][:, P:2 * P], ACT.Identity,
                                 bias=s.bcol[:, 1:2], scale=s.gcol[:, 1:2]).then_inc(s.turned_out.sem, 1)
                else:
                    e.activation(xnT[:, :, bass.ds(t * P, P)], as3(ps[u][:, 0:2 * P], P),
                                 ACT.Copy).then_inc(s.turned_out.sem, 1)

            def vector(s, e):
                s.stats(e)
                s.moments(e)
                e.wait_ge(s.rstd_ready.sem, s.rstd_ready.base + 1)

                def rows_of(t, u, k):
                    if s.make_turned:
                        s.scale(e, t, u)
                    if s.dst is not None:
                        s.keep(e, t)
                tiles(e, rows_of, s.nb)

            def gpsimd(s, e):
                e.wait_ge(s.stats_ready.sem, s.stats_ready.base + 1)
                e.tensor_tensor(s.rstd, s.var, neghalf[0:P, 0:TILES], ALU.pow).then_inc(s.rstd_ready.sem, 1)

            def tensor(s, e):
                e.sem_inc(s.turned.sem, s.nb)
                tiles(e, lambda t, u, k: s.turn(e, t, u), s.nb)

            def scalar(s, e):
                e.sem_inc(s.turned_out.sem, s.nb)
                tiles(e, lambda t, u, k: s.move(e, t, u), s.nb)

            def woven_vector(s, e, step, first):
                e.wait_ge(s.rstd_ready.sem, s.rstd_ready.base + 1)
                weave(e, step, first, TILES // s.nb, {2 * b: [lambda k, b=b: s.scale(e, s.nb * k + b, b)] for b in range(s.nb)})
                s.scale(e, TILES - 1, 0)

            def woven_tensor(s, e, step, first):
                e.sem_inc(s.turned.sem, s.nb)
                weave(e, step, first, TILES // s.nb, {2 * b + 1: [lambda k, b=b: s.turn(e, s.nb * k + b, b)] for b in range(s.nb)})
                s.turn(e, TILES - 1, 0)

            def woven_scalar(s, e, step, first):
                e.sem_inc(s.turned_out.sem, s.nb)
                weave(e, step, first, TILES // s.nb, {2 * b + 1: [lambda k, b=b: s.move(e, s.nb * k + b, b)] for b in range(s.nb)})
                s.move(e, TILES - 1, 0)

        class Messages:

            def __init__(s, la, table):
                s.la, s.table, s.width = la, table, WIDTH[la]
                s.keys_loaded = [counted(f"msg_keys_loaded{h}", 16 * TURNS) for h in range(2)]
                s.picked = counted("msg_picked", ETILES)
                s.merged = counted("msg_merged", ETILES + EB)
                s.sums_out = counted("msg_sums_out", ETILES + 2)
                s.retired = counted("msg_retired", ETILES + 6)
                s.gathered = [counted(f"msg_gathered{u}", 16 * TURNS) for u in range(EB)]
                s.scattered = [counted(f"msg_scattered{k}", 32 + 16 * (ETILES // TABLES)) for k in range(TABLES)]
                c = Carver()
                s.keys = c(128, EB * P)
                s.got = as3(c(P, EB * (D + 1)), D + 1)
                s.pick = as3(c(P, EB * P), P)
                s.sums = as3(c(P, EB * (D + 1)), D + 1)
                s.same = c(P, P)
                s.junk = c(P, P)
                s.count = c(P, 1)
                s.move = c(P, 1)
                s.gather_index = c(P, EB, I32)
                s.scatter_index = c(P, EB, I32)
                assert c.at <= JOBS_AT

            def sync_load(s, e, i, h):
                n = EB // 2 * P
                e.dma_start(s.keys[:, h * n:(h + 1) * n], key_row[s.la][bass.ds(i * EB * P + h * n, n)]
                            .rearrange("(a n) -> a n", a=1).broadcast_to([128, n])
                            ).then_inc(s.keys_loaded[h].sem, 16)

            def sync_turns(s, e, first, last):
                with e.Fori(first, last) as i:
                    for h in range(2):
                        e.wait_ge(s.picked.sem, s.picked.base + (i - 1) * EB + (h + 1) * (EB // 2))
                        s.sync_load(e, i, h)

            def pick_tile(s, e, i, u):
                n = i * EB + u
                if u % (EB // 2) == 0:
                    half = s.keys_loaded[u // (EB // 2)]
                    e.wait_ge(half.sem, half.base + 16 * (i + 1))
                e.wait_ge(s.merged.sem, s.merged.base + n + 1)
                keys = s.keys[0:P, u * P:(u + 1) * P]
                e.tensor_scalar(s.same, keys, col(key_col[s.la], n), None, ALU.is_equal)
                if s.la == 0:
                    e.tensor_scalar(s.pick[:, u, :], keys, col(key_col[0], n), col(weight_col, n),
                                    ALU.is_equal, ALU.mult)
                else:
                    e.tensor_scalar(s.pick[:, u, :], keys, col(key_col[1], n), None, ALU.is_equal)
                e.drain()
                e.wait_ge(s.retired.sem, s.retired.base + n + 1)
                e.tensor_tensor_reduce(out=s.junk, in0=s.same, in1=earlier[:, :], scale=1.0, scalar=0.0,
                                       op0=ALU.mult, op1=ALU.add, accum_out=s.count)
                e.tensor_copy(s.gather_index[:, u:u + 1], col(gather_col[s.la], n))
                e.drain()
                e.tensor_scalar(s.move, s.count, 1.0, col(spare_gap[s.la], n), ALU.min, ALU.mult)
                e.drain()
                e.tensor_tensor(s.scatter_index[:, u:u + 1], s.move, col(key_col[s.la], n), ALU.add)
                e.drain().then_inc(s.picked.sem, 1)

            def vector_start(s, e):
                e.sem_inc(s.retired.sem, 6)
                for u in range(LOOK):
                    s.pick_tile(e, 0, u)

            def vector_step(s, e, i, u):
                s.pick_tile(e, i + (u + LOOK) // EB, (u + LOOK) % EB)

            def vector_end(s, e):
                for u in range(EB - LOOK):
                    s.vector_step(e, TURNS - 1, u)

            def clear(s, e):
                for k in range(TABLES):
                    half = AGG_ROWS[s.la] // 2
                    for h in range(2):
                        e.dma_start(agg[s.la][k][h * half:(h + 1) * half, :].rearrange("(p a) d -> p a d", p=128),
                                    zeros[:, 0:s.width].unsqueeze(1).broadcast_to([128, half // 128, s.width])
                                    ).then_inc(s.scattered[k].sem, 16)

            def gather(s, e, i, u):
                e.wait_ge(s.picked.sem, s.picked.base + i * EB + u + 1)
                own(e, "pool")
                e.indirect_dma_start(out=s.got[:, u, 0:D], out_offset=None, in_=s.table[:, :],
                                     in_offset=bass.IndirectOffsetOnAxis(ap=s.gather_index[:, u:u + 1], axis=0)
                                     ).then_inc(s.gathered[u].sem, 16)

            def scatter(s, e, i, u):
                table = s.scattered[u % TABLES]
                e.wait_ge(s.sums_out.sem, s.sums_out.base + i * EB + u + 3)
                e.wait_ge(table.sem, table.base + 32 + 16 * (i * (EB // TABLES) + u // TABLES))
                e.sem_inc(s.retired.sem, 1)
                e.indirect_dma_start(out=agg[s.la][u % TABLES][:, :], in_=s.sums[:, u, 0:s.width], in_offset=None,
                                     out_offset=bass.IndirectOffsetOnAxis(ap=s.scatter_index[:, u:u + 1], axis=0),
                                     compute_op=ALU.add).then_inc(table.sem, 16)

            def gpsimd_start(s, e):
                e.memset(s.got[:, :, D:D + 1], 1.0)
                e.drain()
                e.wait_ge(table_written, 16 * (s.la + 1))
                for u in range(LOOK):
                    s.gather(e, 0, u)

            def gpsimd_step(s, e, i, u):
                s.scatter(e, i, u)
                s.gather(e, i + (u + LOOK) // EB, (u + LOOK) % EB)

            def gpsimd_end(s, e):
                for u in range(EB):
                    s.scatter(e, TURNS - 1, u)
                    if u < EB - LOOK:
                        s.gather(e, TURNS - 1, u + LOOK)
                for k in range(TABLES):
                    e.wait_ge(s.scattered[k].sem, s.scattered[k].base + 32 + 16 * (ETILES // TABLES))

            def tensor_start(s, e):
                e.sem_inc(s.merged.sem, EB)

            def tensor_step(s, e, i, u):
                n = i * EB + u
                e.wait_ge(s.picked.sem, s.picked.base + n + 1)
                e.wait_ge(s.gathered[u].sem, s.gathered[u].base + 16 * (i + 1))
                e.wait_ge(s.sums_out.sem, s.sums_out.base + n + 1)
                e.matmul(ps[4 + u % 2][0:P, 0:s.width], s.pick[:, u, :], s.got[:, u, 0:s.width],
                         start=True, stop=True).then_inc(s.merged.sem, 1)

            def scalar_start(s, e):
                e.sem_inc(s.sums_out.sem, 2)

            def scalar_step(s, e, i, u):
                n = i * EB + u
                e.wait_ge(s.merged.sem, s.merged.base + n + EB + 1)
                e.wait_ge(s.retired.sem, s.retired.base + n + 1)
                e.activation(s.sums[:, u, 0:s.width], ps[4 + u % 2][0:P, 0:s.width], ACT.Copy).then_inc(s.sums_out.sem, 1)

        class Project:

            def __init__(s, weights, at=0):
                s.staged = counted("prj_staged", TILES)
                s.turned = counted("prj_turned", TILES + 2)
                s.moved = counted("prj_moved", TILES + 2)
                s.product = counted("prj_product", TILES + 2)
                s.used = counted("prj_used", TILES + 2)
                s.w = weights
                c = Carver()
                c.at = at
                s.stage = as3(c(P, 2 * D), D)
                s.lt = c(128, 2 * 2 * P).rearrange("p (u c n) -> p u c n", u=2, c=2)
                s.end = c.at

            def gpsimd(s, e, src):
                def fill(t, u, k):
                    e.wait_ge(s.turned.sem, s.turned.base + t + 1)
                    own(e, "pool")
                    e.tensor_copy(s.stage[:, u, :], col(src, t * D, D)).then_inc(s.staged.sem, 1)
                tiles(e, fill)

            def fill(s, e, t, u):
                e.wait_ge(s.turned.sem, s.turned.base + t + 1)
                own(e, "act")
                e.activation(s.stage[:, u, :], col(rows, t * D, D), ACT.Copy).then_inc(s.staged.sem, 1)

            def turn(s, e, t, u):
                e.wait_ge(s.staged.sem, s.staged.base + t + 1)
                e.wait_ge(s.moved.sem, s.moved.base + t + 1)
                e.transpose(ps[u][:, 0:P], s.stage[:, u, 0:128], ident[0:P, 0:P])
                e.transpose(ps[u][:, P:2 * P], s.stage[:, u, 128:256], ident[0:P, 0:P]).then_inc(s.turned.sem, 1)

            def multiply(s, e, t, u):
                e.wait_ge(s.moved.sem, s.moved.base + t + 3)
                e.wait_ge(s.used.sem, s.used.base + t + 1)
                for c in range(2):
                    mm = e.matmul(ps[2 + u][0:P, 0:D], s.lt[:, u, c, :], s.w[:, c, :],
                                  start=(c == 0), stop=(c == 1))
                mm.then_inc(s.product.sem, 1)

            def move(s, e, t, u):
                e.wait_ge(s.turned.sem, s.turned.base + t + 3)
                e.wait_ge(s.product.sem, s.product.base + t + 1)
                e.activation(s.lt[:, u, :, :], as3(ps[u][:, 0:2 * P], P), ACT.Copy).then_inc(s.moved.sem, 1)

            def tensor(s, e):
                e.sem_inc(s.turned.sem, 2)
                e.sem_inc(s.product.sem, 2)
                tiles_lagged(e, lambda t, u, k: s.turn(e, t, u), lambda t, u, k: s.multiply(e, t, u))

            def scalar(s, e):
                e.sem_inc(s.moved.sem, 2)
                tiles(e, lambda t, u, k: s.move(e, t, u))

            def out(s, u):
                return ps[2 + u][0:P, 0:D]

            def woven_tensor(s, e, step, first):
                e.sem_inc(s.turned.sem, 2)
                e.sem_inc(s.product.sem, 2)
                s.turn(e, 0, 0)
                weave(e, step, first, TILES // 4, {2 * b: [
                    lambda k, b=b: s.turn(e, 4 * k + b + 1, (b + 1) % 2),
                    lambda k, b=b: s.multiply(e, 4 * k + b, b % 2)] for b in range(4)})
                s.multiply(e, TILES - 1, 0)

            def woven_scalar(s, e, step, first):
                e.sem_inc(s.moved.sem, 2)
                s.fill(e, 0, 0)
                s.move(e, 0, 0)
                weave(e, step, first, TILES // 4, {
                    **{2 * b: [lambda k, b=b: s.fill(e, 4 * k + b + 1, (b + 1) % 2)] for b in range(4)},
                    **{2 * b + 1: [lambda k, b=b: s.move(e, 4 * k + b + 1, (b + 1) % 2)] for b in range(4)}})

            def woven_vector(s, e, step, first, use):
                e.sem_inc(s.used.sem, 2)
                weave(e, step, first, TILES // 4, {2 * b + 1: [lambda k, b=b: use(4 * k + b, b % 2)] for b in range(4)})
                use(TILES - 1, 0)

        class Attend:
            def __init__(s, at, scale, wqkv, bias, w_out):
                s.scale, s.wqkv, s.bias, s.w_out = scale, wqkv, bias, w_out
                s.k_product = counted("mix_k_product", 4 * CHUNKS)
                s.k_reduced = counted("mix_k_reduced", 4 * CHUNKS + 4)
                s.k_max = counted("mix_k_max", 1)
                s.k_row = counted("mix_k_row", 1)
                s.shift = counted("mix_shift", 1)
                s.lt_ready = counted("mix_lt_ready", TILES)
                s.qkv = counted("mix_qkv", TILES + 2)
                s.qkv_out = counted("mix_qkv_out", TILES + 2)
                s.q_shifted = counted("mix_q_shifted", TILES)
                s.k_exp = counted("mix_k_exp", TILES)
                s.q_exp = counted("mix_q_exp", TILES)
                s.ctx_sum = counted("mix_ctx_sum", TILES + 2)
                s.ctx_closed = counted("mix_ctx_closed", 1)
                s.blocks = counted("mix_blocks", 1)
                s.blocks_turned = counted("mix_blocks_turned", 1)
                s.blocks_out = counted("mix_blocks_out", 1)
                s.folded = counted("mix_folded", 1)
                c = Carver()
                c.at = at
                s.lt_at = c.at
                s.lt = c(128, 4 * P).rearrange("p (u c n) -> p u c n", u=2, c=2)
                s.part = c(128, 4)
                s.part_new = c(128, 4)
                s.kmax = c(128, 2)
                s.shift_row = c(P, D)
                s.tmp = c(P, D)
                s.ks = as3(c(P, 2 * D), D)
                s.ke = as3(c(P, 2 * D), D)
                s.qb = as3(c(P, 2 * D), D)
                s.qe = as3(c(P, 2 * D), D)
                s.v1 = as3(c(P, 2 * (D + 1)), D + 1)
                s.q8 = as3(c(P, 2 * MIX_HEADS), MIX_HEADS)
                s.zero = c(P, D + 1)
                s.rs = c(128, 2)
                s.bd = as3(c(128, 2 * D), D)
                s.bdT = as3(c(128, 2 * 128), 128)
                s.m_at = c.at
                s.m = as3(c(128, 2 * D), D)
                s.end = c.at

            def woven_tensor(s, e, step, first, maxed):
                def keys_product(c, j):
                    oc, (off, n) = j // 2, HALVES[j % 2]
                    e.wait_ge(s.k_reduced.sem, s.k_reduced.base + 4 * c + j + 1)
                    for k in range(2):
                        mm = e.matmul(ps[j][:, 0:n], s.wqkv[:, k, D + oc * 128:D + (oc + 1) * 128],
                                      xnT[:, k, bass.ds(c * CHUNK + off, n)], start=(k == 0), stop=(k == 1))
                    mm.then_inc(s.k_product.sem, 1)
                if maxed:
                    weave(e, step, first, CHUNKS, {2 * j: [lambda c, j=j: keys_product(c, j)] for j in range(4)})
                    first += CHUNKS
                else:
                    with e.Fori(0, CHUNKS) as c:
                        for j in range(4):
                            keys_product(c, j)
                e.wait_ge(s.k_max.sem, s.k_max.base + 1)
                for oc in range(2):
                    mm = e.matmul(ps[0][0:P, oc * 128:(oc + 1) * 128], s.kmax[:, oc:oc + 1].broadcast_to([128, P]),
                                  ident[:, :], start=True, stop=True, skip_group_check=True)
                mm.then_inc(s.k_row.sem, 1)
                e.wait_ge(s.shift.sem, s.shift.base + 1)
                for c in range(2):
                    e.matmul(ps[6 + c][:, 0:D + 1], s.zero[:, 0:128], s.zero, start=True, stop=False)
                e.sem_inc(s.qkv.sem, 2)
                e.sem_inc(s.ctx_sum.sem, 2)

                def project(t, u, k):
                    e.wait_ge(s.lt_ready.sem, s.lt_ready.base + t + 1)
                    e.wait_ge(s.qkv_out.sem, s.qkv_out.base + t + 1)
                    for c in range(2):
                        e.matmul(ps[u][0:P, 0:512], s.lt[:, u, c, :], s.wqkv[:, c, 0:512],
                                 start=(c == 0), stop=(c == 1))
                    for c in range(2):
                        mm = e.matmul(ps[2 + u][0:P, 0:D], s.lt[:, u, c, :], s.wqkv[:, c, 512:768],
                                      start=(c == 0), stop=(c == 1))
                    mm.then_inc(s.qkv.sem, 1)

                def context(t, u, k):
                    e.wait_ge(s.k_exp.sem, s.k_exp.base + t + 1)
                    for c in range(2):
                        mm = e.matmul(ps[6 + c][:, 0:D + 1], s.ke[:, u, c * 128:(c + 1) * 128], s.v1[:, u, :],
                                      start=False, stop=False)
                    mm.then_inc(s.ctx_sum.sem, 1)
                project(0, 0, 0)
                weave(e, step, first, TILES // 2, {4 * b + 1: [
                    lambda k, b=b: project(2 * k + b + 1, 1 - b, 0), lambda k, b=b: context(2 * k + b, b, 0)] for b in range(2)})
                context(TILES - 1, 0, 0)
                for c in range(2):
                    mm = e.matmul(ps[6 + c][:, 0:D + 1], s.zero[:, 0:128], s.zero, start=False, stop=True)
                mm.then_inc(s.ctx_closed.sem, 1)
                e.wait_ge(s.blocks.sem, s.blocks.base + 1)
                for c in range(2):
                    mm = e.transpose(ps[0][:, c * 128:(c + 1) * 128], s.bd[:, c, c * 128:(c + 1) * 128], ident[:, :])
                mm.then_inc(s.blocks_turned.sem, 1)
                e.wait_ge(s.blocks_out.sem, s.blocks_out.base + 1)
                for c in range(2):
                    mm = e.matmul(ps[1][:, c * D:(c + 1) * D], s.bdT[:, c, :], s.w_out[:, c, :],
                                  start=True, stop=True, skip_group_check=True)
                mm.then_inc(s.folded.sem, 1)

            def woven_scalar(s, e, step, first, maxed):
                if maxed:
                    weave(e, step, first, CHUNKS, {})
                    first += CHUNKS

                def fill(t, u):
                    e.wait_ge(s.qkv.sem, s.qkv.base + t + 1)
                    own(e, "act")
                    e.activation(s.lt[:, u, :, :], xnT[:, :, bass.ds(t * P, P)], ACT.Copy).then_inc(s.lt_ready.sem, 1)

                def exps(t, u):
                    e.wait_ge(s.qkv_out.sem, s.qkv_out.base + t + 3)
                    e.wait_ge(s.ctx_sum.sem, s.ctx_sum.base + t + 1)
                    e.activation(s.ke[:, u, :], s.ks[:, u, :], ACT.Exp).then_inc(s.k_exp.sem, 1)
                    e.wait_ge(s.q_shifted.sem, s.q_shifted.base + t + 1)
                    e.activation(s.qe[:, u, :], s.qb[:, u, :], ACT.Exp).then_inc(s.q_exp.sem, 1)
                fill(0, 0)
                weave(e, step, first, TILES // 2, {4 * b: [
                    lambda k, b=b: fill(2 * k + b + 1, 1 - b), lambda k, b=b: exps(2 * k + b, b)] for b in range(2)})
                exps(TILES - 1, 0)

            def woven_vector(s, e, step, first, maxed):
                e.sem_inc(s.k_reduced.sem, 4)
                e.memset(s.part, -3.0e38)
                e.memset(s.zero, 0.0)
                e.memset(s.bd[:, :, :], 0.0)
                e.memset(s.v1[:, :, D:D + 1], 1.0)

                def keys_max(c, j):
                    n = HALVES[j % 2][1]
                    e.wait_ge(s.k_product.sem, s.k_product.base + 4 * c + j + 1)
                    e.tensor_reduce(s.part_new[:, j:j + 1], ps[j][:, 0:n], AX.X, ALU.max).then_inc(s.k_reduced.sem, 1)
                    if j == 3:
                        e.drain()
                        e.tensor_tensor(s.part, s.part, s.part_new, ALU.max)
                        e.drain()
                if maxed:
                    weave(e, step, first, CHUNKS, {2 * j + 1: [lambda c, j=j: keys_max(c, j)] for j in range(4)})
                    first += CHUNKS
                else:
                    with e.Fori(0, CHUNKS) as c:
                        for j in range(4):
                            keys_max(c, j)
                p2 = as3(s.part, 2)
                e.tensor_tensor(s.kmax, p2[:, :, 0], p2[:, :, 1], ALU.max)
                e.drain().then_inc(s.k_max.sem, 1)
                e.wait_ge(s.k_row.sem, s.k_row.base + 1)
                e.tensor_tensor(s.tmp, ps[0][0:P, 0:D], s.bias[:, D:2 * D], ALU.add)
                e.drain()
                e.tensor_tensor(s.shift_row, s.bias[:, D:2 * D], s.tmp, ALU.subtract)
                e.drain().then_inc(s.shift.sem, 1)
                e.sem_inc(s.qkv_out.sem, 2)

                def spread(t, u, k):
                    e.wait_ge(s.qkv.sem, s.qkv.base + t + 3)
                    e.wait_ge(s.ctx_sum.sem, s.ctx_sum.base + t + 1)
                    e.tensor_tensor(s.ks[:, u, :], ps[u][0:P, D:2 * D], s.shift_row, ALU.add)
                    e.tensor_tensor(s.v1[:, u, 0:D], ps[2 + u][0:P, 0:D], s.bias[:, 2 * D:3 * D], ALU.add)
                    e.tensor_tensor(s.qb[:, u, :], ps[u][0:P, 0:D], s.bias[:, 0:D], ALU.add)
                    e.drain().then_inc(s.qkv_out.sem, 1)
                    q3 = as3(s.qb[:, u, :], MHD)
                    e.tensor_reduce(s.q8[:, u, :], q3, AX.X, ALU.max)
                    e.drain()
                    e.tensor_tensor(q3, q3, over(s.q8[:, u, :], MHD), ALU.subtract)
                    e.drain().then_inc(s.q_shifted.sem, 1)

                def finish(t, u, k):
                    e.wait_ge(s.q_exp.sem, s.q_exp.base + t + 1)
                    q3 = as3(s.qe[:, u, :], MHD)
                    e.tensor_reduce(s.q8[:, u, :], q3, AX.X, ALU.add)
                    e.drain()
                    e.reciprocal(s.q8[:, u, :], s.q8[:, u, :])
                    e.drain()
                    e.tensor_tensor(as3(col(rows, t * D, D), MHD), q3, over(s.q8[:, u, :], MHD), ALU.mult)
                    e.drain()
                spread(0, 0, 0)
                weave(e, step, first, TILES // 2, {
                    2: [lambda k: finish(2 * k, 0, 0)], 3: [lambda k: spread(2 * k + 1, 1, 0)],
                    6: [lambda k: finish(2 * k + 1, 1, 0)], 7: [lambda k: spread(2 * k + 2, 0, 0)]})
                finish(TILES - 1, 0, 0)
                e.wait_ge(s.ctx_closed.sem, s.ctx_closed.base + 1)
                for c in range(2):
                    e.reciprocal(s.rs[:, c:c + 1], ps[6 + c][:, D:D + 1])
                e.drain()
                for h in range(MIX_HEADS):
                    c, p0 = h // 4, (h % 4) * MHD
                    e.tensor_scalar(s.bd[p0:p0 + MHD, c, h * MHD:(h + 1) * MHD],
                                    ps[6 + c][p0:p0 + MHD, h * MHD:(h + 1) * MHD],
                                    s.rs[p0:p0 + MHD, c:c + 1], s.scale, ALU.mult, ALU.mult)
                e.drain().then_inc(s.blocks.sem, 1)
                e.wait_ge(s.blocks_turned.sem, s.blocks_turned.base + 1)
                e.tensor_copy(s.bdT[:, :, :], as3(ps[0][:, 0:256], 128))
                e.drain().then_inc(s.blocks_out.sem, 1)
                e.wait_ge(s.folded.sem, s.folded.base + 1)
                e.tensor_copy(s.m[:, :, :], as3(ps[1][:, 0:512], D))

        edge_loaded, edge_ready, edge_turned, consts_ready = (sem(n) for n in (
            "edge_loaded", "edge_ready", "edge_turned", "consts_ready"))
        x_loaded, rows_written, table_written, out_written = (sem(n) for n in (
            "x_loaded", "rows_written", "table_written", "out_written"))
        c = Carver()
        raw_i = [c(EROWS, EBLK * P, I32) for _ in range(3)]
        raw_w = c(EROWS, EBLK * P)
        src_f, dst_f, typ_f, key1_f = [c(EROWS, EBLK * P) for _ in range(4)]
        ones_c = c(128, 128)

        ln = [Norm(x_cur, xn, 0), Norm(x_cur, None, 0), Norm(x_cur, xn, 0, nb=4, turned=False),
              Norm(xn, None, 1, nb=4), Norm(rows, None, 2, nb=4), Norm(x_cur, None, 0)]

        c = Carver()
        c.at = JOBS_AT
        w_qkv0 = as3(c(128, 2 * 768), 768)
        w_out0 = as3(c(128, 2 * D), D)
        bias0 = c(P, 768)
        gamma0 = c(P, D)
        mix0_loaded = sem("mix0_loaded")
        bias0_cleared = sem("bias0_cleared")
        att0 = Attend(c.at, MHD ** -0.5, w_qkv0, bias0, w_out0)
        prj0 = Project(att0.m, att0.end)
        c.at = prj0.end
        m0_st = c(P, TILES * 6)
        m0_a, m0_b, m0_q, m0_mean, m0_var, m0_rstd = [c(P, TILES) for _ in range(6)]
        m0_stats, m0_root = sem("mix0_stats"), sem("mix0_root")
        assert c.at <= NORM_AT

        msg = [Messages(0, xn_table), Messages(1, xn_table)]

        prjg = Project(None, 0)
        c = Carver()
        c.at = prjg.end
        w_gnn0 = as3(c(128, 2 * D), D)
        prjg.w = w_gnn0
        gnn_rows = as3(c(P, 5 * D), D)
        ag0 = c(P, 4 * D).rearrange("p (u k d) -> p u k d", u=2, k=2)
        NG = TILES * HEADS
        g_st = c(P, NG * 6)
        g_a, g_b, g_q, g_mean, g_var, g_rs = [c(P, NG) for _ in range(6)]
        g_half = c(P, NG)
        DVE_TILES = 17
        gnn0_loaded = sem("gnn0_loaded")
        agg0_loaded = [sem(f"agg0_loaded{u}") for u in range(2)]
        agg0_free = sem("agg0_free")
        gvar, grstd, gparts = sem("gnn0_var"), sem("gnn0_rstd"), sem("gnn0_parts")

        def gnn0_norm(e, which, lo, hi, heads):
            w = D // heads
            y = rows[:, lo * D:hi * D]
            mean, rs = (over(z[:, lo * heads:hi * heads], w) for z in (g_mean, g_rs))
            g, b = (gnn_rows[:, i:i + 1, :].broadcast_to([P, hi - lo, D]) for i in (2 * which - 1, 2 * which))
            e.wait_ge(grstd, which)
            e.tensor_tensor(as3(y, w), as3(y, w), mean, ALU.subtract)
            e.drain()
            e.tensor_tensor(as3(y, w), as3(y, w), rs, ALU.mult)
            e.drain()
            e.tensor_tensor(as3(y, D), as3(y, D), g, ALU.mult)
            e.drain()
            e.tensor_tensor(as3(y, D), as3(y, D), b, ALU.add)
            e.drain()

        c = Carver()
        w_e = c(128, 2 * 3 * 2 * D).rearrange("p (u w c d) -> p u w c d", u=2, w=3, c=2)
        bnp = c(128, 10 * 16).rearrange("p (a b) -> p a b", b=16)
        bns = as3(c(128, 4 * 16), 16)
        bnt = c(128, 16)
        w_r = as3(c(128, 2 * MOE), MOE)
        br_row = c(P, MOE)
        bo_rows = as3(c(P, MOE * D), D)
        gate = c(P, TILES * MOE)
        gate_sum = c(P, TILES)
        ltg = c(128, 4 * P).rearrange("p (u c n) -> p u c n", u=2, c=2)
        h1 = as3(c(128, 2 * CHUNK), CHUNK)
        h2 = as3(c(128, 2 * CHUNK), CHUNK)
        ffn0_loaded = sem("ffn0_loaded")
        gsem = {x: sem(f"gate_{x}") for x in ("lt_ready", "logits", "shifted", "exp")}
        bn_var, bn_rstd, bn_ready = sem("bn_var"), sem("bn_rstd"), sem("bn_ready")
        we_loaded = [sem(f"expert_loaded{u}") for u in range(2)]
        we_used, unit_done, unit_out, y_done, y_out = (sem(f"moe_{n}") for n in (
            "weights_used", "unit_done", "unit_out", "y_done", "y_out"))

        RD = REL * D
        RW = REL * (D + 1)
        QW = 3 * D
        c = Carver()
        xnT_flat = xnT[:, :, :].rearrange("p c n -> p (c n)")
        w_rq = [as3(xnT_flat[:, r * 2 * QW:(r + 1) * 2 * QW] if r < 4 else c(128, 2 * QW), QW) for r in range(REL)]
        b_all = edge_cols[0:REL + 1, 0:QW]
        row_mask = c(REL + 1, REL)
        at = c.at
        w_relT = as3(c(128, 2 * RD), RD)
        w_in = as3(c(128, 2 * QW), QW)
        b_relT = as3(c(128, 2 * REL), REL)
        c.at = at
        ag1 = c(P, 2 * RW).rearrange("p (k r d) -> p k r d", k=2, d=D + 1)
        agsum = as3(c(P, RD), D)
        counts7 = c(P, REL + 1)
        countT = as3(edge_cols[0:REL + 1, QW:QW + REL * P], P)
        aT = as3(c(128, 12 * P), P)
        QK = c(P, 2 * REL * 2 * D).rearrange("p (u r d) -> p u r d", u=2, d=2 * D)
        V = c(P, 2 * RD).rearrange("p (u r d) -> p u r d", u=2, d=D)
        prod = c(P, RD)
        pprod = as3(c(P, 2 * RD), RD)
        scores = c(P, REL * REL * HEADS)
        sc24 = c(P, REL * HEADS)
        pbar = c(P, REL * HEADS)
        vsum = c(P, D)
        POOL_RELS = (2, 3, 4, 5)
        rel_agg_loaded = sem("rel_agg_loaded")
        asem = {x: sem(f"relatt_{x}") for x in ("w", "fold", "fold_out", "consts", "agg_free", "summed", "turned", "moved",
                                                "qkv", "qkv_out", "attended", "pool_prod", "pool_prod_used", "shifted", "exp")}

        c = Carver()
        c.at = JOBS_AT
        w_qkv1 = as3(c(128, 2 * 768), 768)
        bias1 = c(P, 768)
        w_out1 = as3(c(128, 2 * D), D)
        b_o1 = c(P, D)
        att1 = Attend(c.at, 1.0, w_qkv1, bias1, w_out1)
        prj3 = Project(att1.m, att1.end)
        mlp_weights_at = att1.lt_at
        c.at = prj3.end
        w_x = as3(c(128, 2 * D), D)
        b_x = c(128, 2)
        blk = c(128, 3 * 128)
        p3_tmp = as3(c(P, 2 * D), D)
        mlp_hidden_at = c.at
        attended1 = sem("attended1")
        mix1_loaded, blk_cleared, blk_loaded, fold_mm, fold_out, bias_mm = (sem(f"mix1_{n}") for n in (
            "loaded", "blk_cleared", "blk_loaded", "fold_mm", "fold_out", "bias_mm"))

        prj1 = Project(None, 0)
        prj2 = Project(None, prj1.end)
        c = Carver()
        c.at = prj2.end
        w_ao = as3(c(128, 2 * D), D)
        w_pr = as3(c(128, 2 * D), D)
        prj1.w, prj2.w = w_ao, w_pr
        b_ao = c(P, D)
        b_pr = c(P, D)
        prj_tmp = as3(c(P, 2 * D), D)
        prj_loaded = sem("prj_loaded")

        c = Carver()
        c.at = mlp_weights_at
        w_m1 = as3(c(128, 2 * HID), HID)
        w_m2 = as3(c(128, 8 * D), D)
        b_m1 = c(128, 8)
        b_m2 = c(P, D)
        assert c.at <= att1.m_at
        c.at = mlp_hidden_at
        m_h = as3(c(128, 8 * CHUNK), CHUNK)
        m_o = p3_tmp
        assert c.at <= NORM_AT
        mlp_loaded, m1_mm, m1_out, m2_mm, m2_out = (sem(f"mlp_{n}") for n in ("loaded", "m1_mm", "m1_out", "m2_mm", "m2_out"))

        c = Carver()
        w_1 = as3(c(128, 2 * EXP * EH), EXP * EH)
        w_2 = as3(c(128, 16 * D), D)
        b_1 = c(128, 16)
        w_ro = as3(c(128, 2 * EXP), EXP)
        b_ro = c(P, EXP)
        b_2 = c(EXP, D)
        e_col = c(128, 16)
        e_col_i = c(128, 16, I32)
        iota32 = c(P, EXP)
        iota32_i = c(P, EXP, I32)
        lt_ro = c(128, 4 * P).rearrange("p (u c n) -> p u c n", u=2, c=2)
        ro_l = as3(c(P, 2 * EXP), EXP)
        ro_m = as3(c(P, 2 * 8), 8)
        ro_i = as3(c(P, 2 * 8, U32), 8)
        ro_f = c(P, 2)
        ro_h = as3(c(P, 2 * EXP), EXP)
        e_h = as3(c(128, 16 * CHUNK), CHUNK)
        ffn1_loaded = sem("ffn1_loaded")
        rsem = {x: sem(f"route_{x}") for x in ("consts", "cols", "lt_ready", "logits", "ready", "turned", "copied")}
        x_mm, x_relu, x_masked, x_y, x_yout = (sem(f"moe1_{n}") for n in ("unit", "relu", "masked", "y", "y_out"))
        e_hot = c(EXP, CHUNK)
        idxT = xn_whole[:, 0:NODES]
        ohT = rows[0:EXP, 0:NODES]

        PRJ0_AT = CHUNKS + TILES // 2
        NORM0_AT = PRJ0_AT + TILES // 4
        assert NORM0_AT + TILES // 2 < TURNS
        ATT1_AT = TILES // 4
        PRJ3_AT = ATT1_AT + TILES // 2
        LN4_AT = PRJ3_AT + TILES // 4
        MLP_AT = LN4_AT + TILES // 4
        MLP_TURNS = 3
        MLP_END = MLP_AT + MLP_TURNS * CHUNKS
        assert MLP_END < TURNS
        MLP_OUTPUT = {9: 0, 12: 1, 17: 2, 19: 3, 21: 4}
        MLP_PLAN = [(n, (n,) if n < 16 else (), MLP_OUTPUT.get(n)) for n in range(MLP_TURNS * EB)]

        block = ctx.enter_context(nc.Block())

        @block.sync
        def _(sp):
            sp.dma_start(as3(x_cur[:, :], D), A["x"].rearrange("(t p) d -> p t d", p=P)).then_inc(x_loaded, 16)
            for r, n in enumerate(("src", "dst", "edge_type_6")):
                sp.dma_start(as3(raw_i[r], P), A[n].rearrange("(a q j) -> q a j", q=EROWS, j=P)).then_inc(edge_loaded, 16)
            sp.dma_start(as3(raw_w, P), A["edge_weight"].rearrange("(a q j) -> q a j", q=EROWS, j=P)).then_inc(edge_loaded, 16)
            sp.wait_ge(edge_ready, 1)
            for la, k in enumerate((src_f, key1_f)):
                sp.dma_start(key_row[la].rearrange("(a q j) -> q a j", q=EROWS, j=P), as3(k, P)).then_inc(rows_written, 16)
            sp.wait_ge(rows_written, 32)
            phase_end(sp, 1)
            sp.dma_start(w_qkv0[:, :, :], cm(A["L0_mix_Wqkv"])).then_inc(mix0_loaded, 16)
            sp.dma_start(w_out0[:, :, :], cm(A["L0_mix_Wout"])).then_inc(mix0_loaded, 16)
            sp.dma_start(gamma0, row_of(A["L0_mix_gamma"], D, P)).then_inc(mix0_loaded, 16)
            sp.wait_ge(mix0_loaded, 48)
            phase_end(sp, 2)
            sp.dma_start(xn_table.rearrange("(t p) d -> p t d", p=P), as3(xn[:, :], D)).then_inc(table_written, 16)
            for h in range(2):
                msg[0].sync_load(sp, 0, h)
            msg[0].sync_turns(sp, 1, TURNS)
            sp.wait_ge(table_written, 16)
            phase_end(sp, 3)
            sp.dma_start(w_gnn0[:, :, :], cm(A["gnn0_W"])).then_inc(gnn0_loaded, 16)
            for i, n in enumerate(("L0_gnn_bias", "L0_gnn_ln1_g", "L0_gnn_ln1_b", "L0_gnn_ln2_g", "L0_gnn_ln2_b")):
                sp.dma_start(gnn_rows[:, i, :], row_of(A[n], D, P)).then_inc(gnn0_loaded, 16)

            def load_agg(t, u, k):
                sp.wait_ge(agg0_free, t + 1)
                for tb in range(TABLES):
                    sp.dma_start(ag0[:, u, tb, :], agg[0][tb][bass.ds(t * P, P), :]).then_inc(agg0_loaded[u], 16)
            tiles(sp, load_agg)
            sp.wait_ge(gnn0_loaded, 96)
            phase_end(sp, 4)
            phase_end(sp, 5)
            for i, n in enumerate(("L0_ffn_b1", "L0_ffn_g1", "L0_ffn_be1", "L0_ffn_m1", "L0_ffn_v1",
                                   "L0_ffn_b2", "L0_ffn_g2", "L0_ffn_be2", "L0_ffn_m2", "L0_ffn_v2")):
                sp.dma_start(bnp[:, i, :], A[n]).then_inc(ffn0_loaded, 16)
            sp.dma_start(w_r[:, :, :], cm(A["L0_ffn_Wr"])).then_inc(ffn0_loaded, 16)
            sp.dma_start(br_row, row_of(A["L0_ffn_br"], MOE, P)).then_inc(ffn0_loaded, 16)
            sp.dma_start(bo_rows.rearrange("p e d -> p (e d)"), row_of(A["L0_ffn_bo"], MOE * D, P)).then_inc(ffn0_loaded, 16)
            sp.wait_ge(ffn0_loaded, 13 * 16)
            phase_end(sp, 6)
            with sp.Fori(0, MOE // 2) as k:
                for u in range(2):
                    sp.wait_ge(we_used, 2 * k + u + 1)
                    for i, n in enumerate(("L0_ffn_W1", "L0_ffn_W2", "L0_ffn_Wo")):
                        sp.dma_start(w_e[:, u, i, :, :], A[n][bass.ds((2 * k + u) * D, D), :]
                                     .rearrange("(c p) n -> p c n", p=128)).then_inc(we_loaded[u], 16)
            phase_end(sp, 7)
            sp.dma_start(ln[3].gcol, A["mix1_ln1_w"]).then_inc(mix1_loaded, 16)
            sp.dma_start(ln[3].bcol, A["mix1_ln1_b"]).then_inc(mix1_loaded, 16)
            sp.dma_start(ln[4].gcol, A["mix1_ln2_w"]).then_inc(mix1_loaded, 16)
            sp.dma_start(ln[4].bcol, A["mix1_ln2_b"]).then_inc(mix1_loaded, 16)
            sp.dma_start(w_x[:, :, :], cm(A["L1_mix_Wx"])).then_inc(mix1_loaded, 16)
            sp.dma_start(b_x, A["mix1_bx"]).then_inc(mix1_loaded, 16)
            sp.dma_start(w_out1[:, :, :], cm(A["mix1_Wo_T"])).then_inc(mix1_loaded, 16)
            sp.dma_start(b_o1, row_of(A["L1_mix_bo"], D, P)).then_inc(mix1_loaded, 16)
            sp.wait_ge(blk_cleared, 1)
            for i, n in enumerate(("mix1_Wq_T", "mix1_Wk_T", "mix1_Wv_T")):
                for h in range(4):
                    sp.dma_start(blk[h * MHD:(h + 1) * MHD, i * 128 + h * MHD:i * 128 + (h + 1) * MHD],
                                 A[n]).then_inc(blk_loaded, 16)
            sp.wait_ge(mix1_loaded, 128)
            sp.wait_ge(blk_loaded, 16 * 12)
            phase_end(sp, 8)
            sp.dma_start(xn_table.rearrange("(t p) d -> p t d", p=P), as3(xn[:, :], D)).then_inc(table_written, 16)
            phase_end(sp, 9)
            for h in range(2):
                msg[1].sync_load(sp, 0, h)
            msg[1].sync_turns(sp, 1, PRJ3_AT + 1)
            sp.wait_ge(attended1, 1)
            sp.dma_start(w_m1[:, :, :], cm(A["mix1_W1_T"])).then_inc(mlp_loaded, 16)
            sp.dma_start(w_m2[:, :, :], A["mix1_W2_T"].rearrange("(c p) n -> p c n", p=128)).then_inc(mlp_loaded, 16)
            sp.dma_start(b_m1, A["mix1_b1"]).then_inc(mlp_loaded, 16)
            sp.dma_start(b_m2, row_of(A["L1_mix_b2"], D, P)).then_inc(mlp_loaded, 16)
            msg[1].sync_turns(sp, PRJ3_AT + 1, TURNS)
            phase_end(sp, 10)
            sp.dma_start(w_relT[:, :, :], cm(A["gnn1_W_T"])).then_inc(asem["w"], 16)
            sp.dma_start(w_in[:, :, :], cm(A["gnn1_in_T"])).then_inc(asem["w"], 16)
            sp.dma_start(b_relT[:, :, :], cm(A["gnn1_b_T"])).then_inc(asem["w"], 16)
            sp.dma_start(b_all[REL:REL + 1, :], row_of(A["L1_gnn_in_proj_b"], QW, 1)).then_inc(asem["w"], 16)
            sp.wait_ge(asem["w"], 64)
            phase_end(sp, 11)

            def load_rel(t, u, k):
                sp.wait_ge(asem["agg_free"], t + 1)
                for tb in range(TABLES):
                    sp.dma_start(ag1[:, tb, :, :], agg[1][tb][0:REL * NODES, :]
                                 .rearrange("(r n) d -> n r d", r=REL)[bass.ds(t * P, P), :, :]
                                 ).then_inc(rel_agg_loaded, 16)
            tiles(sp, load_rel)
            phase_end(sp, 12)
            sp.dma_start(w_ao[:, :, :], cm(A["gnn1_ao_T"])).then_inc(prj_loaded, 16)
            sp.dma_start(w_pr[:, :, :], cm(A["gnn1_pr_T"])).then_inc(prj_loaded, 16)
            sp.dma_start(b_ao, row_of(A["L1_gnn_attn_out_b"], D, P)).then_inc(prj_loaded, 16)
            sp.dma_start(b_pr, row_of(A["L1_gnn_proj_b"], D, P)).then_inc(prj_loaded, 16)
            sp.wait_ge(prj_loaded, 64)
            phase_end(sp, 13)
            phase_end(sp, 14)
            phase_end(sp, 15)
            for d_, n in ((w_1, cm(A["ffn1_W1"])), (w_2, A["ffn1_W2"].rearrange("(c p) n -> p c n", p=128)), (w_ro, cm(A["ffn1_router_T"]))):
                sp.dma_start(d_[:, :, :], n).then_inc(ffn1_loaded, 16)
            sp.dma_start(b_1, A["ffn1_b1"]).then_inc(ffn1_loaded, 16)
            sp.dma_start(b_ro, row_of(A["L1_ffn_router_b"], EXP, P)).then_inc(ffn1_loaded, 16)
            sp.dma_start(b_2, A["L1_ffn_b2"]).then_inc(ffn1_loaded, 16)
            sp.wait_ge(ffn1_loaded, 96)
            phase_end(sp, 16)
            phase_end(sp, 17)
            sp.dma_start(out.rearrange("(t p) d -> p t d", p=P), as3(x_cur[:, :], D)).then_inc(out_written, 16)
            sp.wait_ge(out_written, 16)

        @block.gpsimd
        def _(pool):
            pool.memset(ones_c, 1.0)
            pool.memset(neghalf[:, :], -0.5)
            pool.memset(zeros[:, :], 0.0)
            pool.iota(lane_i[:, :], [[0, 1]], base=0, channel_multiplier=1)
            pool.drain()
            pool.affine_select(out=ident[:, :], in_=ones_c, compare_op=ALU.is_equal, fill=0.0, base=0,
                               pattern=[[-1, 128]], channel_multiplier=1)
            pool.affine_select(out=earlier[:, :], in_=ones_c[0:P, 0:P], compare_op=ALU.is_gt, fill=0.0, base=0,
                               pattern=[[-1, P]], channel_multiplier=1)
            pool.tensor_copy(lane[:, :], lane_i[:, :])
            pool.drain().then_inc(consts_ready, 1)
            msg[0].clear(pool)
            phase_end(pool, 1)
            ln[0].gpsimd(pool)
            pool.memset(bias0, 0.0)
            phase_end(pool, 2)
            msg[0].gpsimd_start(pool)
            weave(pool, msg[0].gpsimd_step, 0, NORM0_AT, {})
            pool.wait_ge(m0_stats, 1)
            pool.tensor_tensor(m0_rstd, m0_var, neghalf[0:P, 0:TILES], ALU.pow).then_inc(m0_root, 1)
            weave(pool, msg[0].gpsimd_step, NORM0_AT, TURNS - 1 - NORM0_AT, {})
            msg[0].gpsimd_end(pool)
            phase_end(pool, 3)
            pool.memset(g_half, -0.5)
            pool.sem_inc(agg0_free, 2)

            def add_tables(t, u, k):
                pool.wait_ge(agg0_loaded[u], 32 * (k + 1))
                pool.wait_ge(prjg.turned.sem, prjg.turned.base + t + 1)
                pool.tensor_tensor(prjg.stage[:, u, :], ag0[:, u, 0, :], ag0[:, u, 1, :], ALU.add).then_inc(prjg.staged.sem, 1)
                pool.wait_ge(prjg.staged.sem, prjg.staged.base + t + 1)
                pool.sem_inc(agg0_free, 1)

            tiles(pool, add_tables)
            pool.wait_ge(gvar, 1)
            pool.tensor_tensor(g_rs, g_var, g_half, ALU.pow).then_inc(grstd, 1)
            gnn0_norm(pool, 1, DVE_TILES, TILES, HEADS)
            pool.drain().then_inc(gparts, 1)
            pool.wait_ge(gvar, 2)
            pool.tensor_tensor(g_rs[:, 0:TILES], g_var[:, 0:TILES], g_half[:, 0:TILES], ALU.pow).then_inc(grstd, 1)
            gnn0_norm(pool, 2, DVE_TILES, TILES, 1)
            own_x, own_y = x_cur[:, DVE_TILES * D:], rows[:, DVE_TILES * D:]
            pool.tensor_tensor(own_x, own_x, own_y, ALU.add)
            phase_end(pool, 4)
            ln[1].gpsimd(pool)
            phase_end(pool, 5)
            pool.wait_ge(bn_var, 1)
            for i in (0, 2):
                pool.tensor_tensor(bns[:, i, :], bns[:, i, :], neghalf[:, 0:16], ALU.pow)
            pool.drain().then_inc(bn_rstd, 1)
            phase_end(pool, 6)
            msg[1].clear(pool)
            phase_end(pool, 7)
            pool.memset(blk, 0.0)
            pool.drain().then_inc(blk_cleared, 1)
            ln[2].gpsimd(pool)
            phase_end(pool, 8)
            ln[3].gpsimd(pool)
            phase_end(pool, 9)
            msg[1].gpsimd_start(pool)
            weave(pool, msg[1].gpsimd_step, 0, LN4_AT, {})
            ln[4].gpsimd(pool)
            weave(pool, msg[1].gpsimd_step, LN4_AT, TURNS - 1 - LN4_AT, {})
            msg[1].gpsimd_end(pool)
            phase_end(pool, 10)
            phase_end(pool, 11)
            pool.memset(counts7[:, REL:REL + 1], 1.0)
            pool.sem_inc(asem["agg_free"], 1)

            def rel_sum(t, u, k):
                pool.wait_ge(rel_agg_loaded, 32 * (t + 1))
                pool.wait_ge(asem["turned"], t + 1)
                pool.tensor_tensor(agsum[:, :, :], ag1[:, 0, :, 0:D], ag1[:, 1, :, 0:D], ALU.add)
                pool.tensor_tensor(counts7[:, 0:REL].unsqueeze(2), ag1[:, 0, :, D:D + 1], ag1[:, 1, :, D:D + 1], ALU.add)
                pool.drain().then_inc(asem["summed"], 1)
                pool.sem_inc(asem["agg_free"], 1)

            def rel_prod(t, u, k):
                pool.wait_ge(asem["qkv_out"], REL * (t + 3))
                for i, r in enumerate(POOL_RELS):
                    pool.wait_ge(asem["pool_prod_used"], len(POOL_RELS) * t + i + 1)
                    pool.tensor_tensor(as3(pprod[:, i % 2, :], D), QK[:, u, r:r + 1, 0:D].broadcast_to([P, REL, D]),
                                       QK[:, u, :, D:2 * D], ALU.mult).then_inc(asem["pool_prod"], 1)
            tiles_lagged(pool, rel_sum, rel_prod)
            phase_end(pool, 12)
            prj1.gpsimd(pool, rows[:, :])
            phase_end(pool, 13)
            prj2.gpsimd(pool, rows[:, :])
            phase_end(pool, 14)
            ln[5].gpsimd(pool)
            phase_end(pool, 15)
            pool.iota(e_col_i, [[2, 16]], base=0, channel_multiplier=0)
            pool.iota(iota32_i, [[1, EXP]], base=0, channel_multiplier=0)
            pool.drain().then_inc(rsem["consts"], 1)
            phase_end(pool, 16)
            phase_end(pool, 17)

        @block.scalar
        def _(act):
            act.preload_act_table(ACT.Exp)
            phase_end(act, 1)
            ln[0].scalar(act)
            phase_end(act, 2)
            msg[0].scalar_start(act)
            att0.woven_scalar(act, msg[0].scalar_step, 0, True)
            job_end(act, 1)
            prj0.woven_scalar(act, msg[0].scalar_step, PRJ0_AT)
            weave(act, msg[0].scalar_step, NORM0_AT, TURNS - NORM0_AT, {})
            phase_end(act, 3)
            prjg.scalar(act)
            phase_end(act, 4)
            ln[1].scalar(act)
            phase_end(act, 5)
            def fillg(t, u, k):
                act.wait_ge(gsem["logits"], t + 1)
                own(act, "act")
                act.activation(ltg[:, u, :, :], xnT[:, :, bass.ds(t * P, P)], ACT.Copy).then_inc(gsem["lt_ready"], 1)
            tiles(act, fillg)
            act.wait_ge(gsem["shifted"], 1)
            act.activation(gate, gate, ACT.Exp).then_inc(gsem["exp"], 1)
            phase_end(act, 6)
            act.sem_inc(unit_out, 8)
            with act.Fori(0, MOE // 2) as k:
                for u in range(2):
                    with act.Fori(0, CHUNKS) as c_:
                        ex = 2 * k + u
                        g = ex * CHUNKS + c_
                        for layer in range(2):
                            dst = (h1, h2)[layer]
                            for j in range(4):
                                h, oc = j // 2, j % 2
                                off, n = HALVES[h]
                                act.wait_ge(unit_done, g * 8 + 4 * layer + j + 1)
                                own(act, "act")
                                act.activation(dst[:, oc, off:off + n], ps[j][:, 0:n], ACT.Relu,
                                               scale=bns[:, 2 * layer, bass.ds(ex * 2 + oc, 1)],
                                               bias=bns[:, 2 * layer + 1, bass.ds(ex * 2 + oc, 1)]).then_inc(unit_out, 1)
            phase_end(act, 7)
            phase_end(act, 8)
            phase_end(act, 9)
            step = msg[1].scalar_step
            msg[1].scalar_start(act)
            ln[3].woven_scalar(act, step, 0)
            job_end(act, 2)
            att1.woven_scalar(act, step, ATT1_AT, False)
            job_end(act, 3)
            prj3.woven_scalar(act, step, PRJ3_AT)
            job_end(act, 4)
            ln[4].woven_scalar(act, step, LN4_AT)
            act.preload_act_table(ACT.Gelu)
            job_end(act, 5)
            act.wait_ge(mlp_loaded, 64)
            act.sem_inc(m1_out, 4)

            def gelu(c_, j):
                h, oc = j // 8, j % 8
                off, n = HALVES[h]
                act.wait_ge(m1_mm, c_ * 16 + j + 1)
                act.activation(m_h[:, oc, off:off + n], ps[j % 4][:, 0:n], ACT.Gelu,
                               bias=b_m1[:, oc:oc + 1]).then_inc(m1_out, 1)
            with act.Fori(0, CHUNKS) as c_:
                for at, units, _ in MLP_PLAN:
                    step(act, MLP_AT + MLP_TURNS * c_ + at // EB, at % EB)
                    for j in units:
                        gelu(c_, j)
            weave(act, step, MLP_END, TURNS - MLP_END, {})
            act.preload_act_table(ACT.Exp)
            phase_end(act, 10)
            act.sem_inc(asem["fold_out"], 2)
            for r in range(REL):
                for ic in range(2):
                    i = 2 * r + ic
                    act.wait_ge(asem["fold"], i + 1)
                    act.activation(w_rq[r][:, ic, 0:512], ps[2 * (i % 2)][:, :], ACT.Copy)
                    act.activation(w_rq[r][:, ic, 512:QW], ps[2 * (i % 2) + 1][:, 0:D], ACT.Copy).then_inc(asem["fold_out"], 1)
            act.wait_ge(asem["fold"], 2 * REL + 1)
            act.activation(b_all[0:REL, 0:512], ps[4][0:REL, :], ACT.Copy)
            act.activation(b_all[0:REL, 512:QW], ps[5][0:REL, 0:D], ACT.Copy)
            phase_end(act, 11)
            act.sem_inc(asem["qkv_out"], 2 * REL)

            def rel_move(t, u, k):
                act.wait_ge(asem["turned"], t + 2)
                for b in range(3):
                    act.activation(aT[:, 4 * b:4 * b + 4, :], as3(ps[b][:, 0:4 * P], P), ACT.Copy).then_inc(asem["moved"], 1)
                    if b == 0:
                        for r in range(REL):
                            act.activation(countT[:, r, :], ps[7][0:REL + 1, 0:P], ACT.Copy, scale=row_mask[:, r:r + 1])
                act.drain().then_inc(asem["moved"], 1)

            def rel_out(t, u, rs):
                act.wait_ge(asem["attended"], t + 1)
                for r in rs:
                    b = 3 + 2 * (r % 2)
                    act.wait_ge(asem["qkv"], REL * t + r + 1)
                    act.activation(QK[:, u, r, :], ps[b][0:P, :], ACT.Copy)
                    act.activation(V[:, u, r, :], ps[b + 1][0:P, 0:D], ACT.Copy).then_inc(asem["qkv_out"], 1)

            def rel_exp(t):
                act.wait_ge(asem["shifted"], t + 1)
                act.activation(scores, scores, ACT.Exp, scale=HD ** -0.5).then_inc(asem["exp"], 1)

            def rel_step(t, u):
                rel_move(t, u, None)
                rel_out(t, u, range(0, 4))
                rel_exp(t - 1)
                rel_out(t, u, range(4, REL))
            rel_move(0, 0, None)
            rel_out(0, 0, range(REL))
            with act.Fori(0, TILES // 2) as k:
                rel_step(2 * k + 1, 1)
                rel_step(2 * k + 2, 0)
            rel_exp(TILES - 1)
            phase_end(act, 12)
            prj1.scalar(act)
            phase_end(act, 13)
            prj2.scalar(act)
            phase_end(act, 14)
            ln[5].scalar(act)
            phase_end(act, 15)

            def ro_fill(t, u, k):
                act.wait_ge(rsem["logits"], t + 1)
                own(act, "act")
                act.activation(lt_ro[:, u, :, :], xnT[:, :, bass.ds(t * P, P)], ACT.Copy).then_inc(rsem["lt_ready"], 1)

            def ro_copy(t, u, k):
                act.wait_ge(rsem["turned"], t + 1)
                own(act, "act")
                act.activation(ohT[:, bass.ds(t * P, P)], ps[2 + u][0:EXP, 0:P], ACT.Copy)
                act.activation(idxT[:, bass.ds(t * P, P)], ps[4 + u][:, 0:P], ACT.Copy).then_inc(rsem["copied"], 1)
            act.sem_inc(rsem["copied"], 2)
            tiles_lagged(act, ro_fill, ro_copy)
            phase_end(act, 16)
            act.sem_inc(x_relu, 4)
            with act.Fori(0, CHUNKS) as c_:
                for j in range(32):
                    h, pc = j // 16, j % 16
                    off, n = HALVES[h]
                    act.wait_ge(x_mm, c_ * 32 + j + 1)
                    act.activation(e_h[:, pc, off:off + n], ps[j % 4][:, 0:n], ACT.Relu,
                                   bias=b_1[:, pc:pc + 1]).then_inc(x_relu, 1)
            phase_end(act, 17)

        @block.tensor
        def _(pe):
            pe.wait_ge(edge_ready, 1)
            pe.wait_ge(consts_ready, 1)
            for i, a in enumerate((src_f, dst_f, key1_f, raw_w)):
                for b in range(EBLK):
                    mm = pe.transpose(ps[i][0:P, b * EROWS:(b + 1) * EROWS], as3(a, P)[:, b, :], ident[0:EROWS, 0:EROWS])
            mm.then_inc(edge_turned, 1)
            phase_end(pe, 1)
            ln[0].tensor(pe)
            phase_end(pe, 2)
            msg[0].tensor_start(pe)
            att0.woven_tensor(pe, msg[0].tensor_step, 0, True)
            job_end(pe, 1)
            prj0.woven_tensor(pe, msg[0].tensor_step, PRJ0_AT)
            weave(pe, msg[0].tensor_step, NORM0_AT, TURNS - NORM0_AT, {})
            phase_end(pe, 3)
            prjg.tensor(pe)
            phase_end(pe, 4)
            ln[1].tensor(pe)
            phase_end(pe, 5)
            pe.wait_ge(bn_ready, 1)
            pe.sem_inc(gsem["logits"], 2)

            def logits(t, u, k):
                pe.wait_ge(gsem["lt_ready"], t + 1)
                for c_ in range(2):
                    mm = pe.matmul(col(ps[0][0:P, :], t * MOE, MOE), ltg[:, u, c_, :], w_r[:, c_, :],
                                   start=(c_ == 0), stop=(c_ == 1), skip_group_check=True)
                mm.then_inc(gsem["logits"], 1)
            tiles(pe, logits)
            phase_end(pe, 6)
            pe.sem_inc(we_used, 2)
            with pe.Fori(0, MOE // 2) as k:
                for u in range(2):
                    pe.wait_ge(we_loaded[u], 48 * (k + 1))
                    own(pe, "pe")
                    with pe.Fori(0, CHUNKS) as c_:
                        g = (2 * k + u) * CHUNKS + c_
                        for layer in range(2):
                            for j in range(4):
                                h, oc = j // 2, j % 2
                                off, n = HALVES[h]
                                if layer == 0:
                                    pe.wait_ge(unit_out, 8 * g + j + 5)
                                else:
                                    pe.wait_ge(unit_out, 8 * g + 8 + (2 if j < 2 else 4))
                                for c2 in range(2):
                                    rhs = xnT[:, c2, bass.ds(c_ * CHUNK + off, n)] if layer == 0 else h1[:, c2, off:off + n]
                                    mm = pe.matmul(ps[j][:, 0:n], w_e[:, u, layer, c2, oc * 128:(oc + 1) * 128], rhs,
                                                   start=(c2 == 0), stop=(c2 == 1))
                                mm.then_inc(unit_done, 1)
                        for i in range(TPC):
                            pe.wait_ge(unit_out, 8 * g + 8 + (6 if (i + 1) * P <= HALVES[0][1] else 8))
                            pe.wait_ge(y_out, 5 * g + (5 if i == 0 else 6 if i == 4 else i + 1))
                            for c2 in range(2):
                                mm = pe.matmul(ps[4 + i % 4][0:P, 0:D], h2[:, c2, i * P:(i + 1) * P], w_e[:, u, 2, c2, :],
                                               start=(c2 == 0), stop=(c2 == 1))
                            mm.then_inc(y_done, 1)
                    pe.drain().then_inc(we_used, 1)
            phase_end(pe, 7)
            phase_end(pe, 8)
            pe.wait_ge(mix1_loaded, 128)
            pe.wait_ge(blk_loaded, 16 * 12)
            for oc in range(2):
                for ic in range(2):
                    mm = pe.matmul(ps[2 * oc + ic][:, 0:384], w_x[:, oc, ic * 128:(ic + 1) * 128], blk,
                                   start=True, stop=True)
                mm = pe.matmul(ps[4 + oc][0:P, 0:384], b_x[:, oc:oc + 1].broadcast_to([128, P]), blk, start=True, stop=True)
            mm.then_inc(fold_mm, 1)
            phase_end(pe, 9)
            step = msg[1].tensor_step
            msg[1].tensor_start(pe)
            ln[3].woven_tensor(pe, step, 0)
            job_end(pe, 2)
            att1.woven_tensor(pe, step, ATT1_AT, False)
            job_end(pe, 3)
            pe.sem_inc(attended1, 1)
            prj3.woven_tensor(pe, step, PRJ3_AT)
            job_end(pe, 4)
            ln[4].woven_tensor(pe, step, LN4_AT)
            job_end(pe, 5)
            pe.wait_ge(mlp_loaded, 64)

            def hidden(c_, j):
                h, oc = j // 8, j % 8
                off, n = HALVES[h]
                pe.wait_ge(m1_out, c_ * 16 + j + 1)
                for c2 in range(2):
                    mm = pe.matmul(ps[j % 4][:, 0:n], w_m1[:, c2, oc * 128:(oc + 1) * 128],
                                   xnT[:, c2, bass.ds(c_ * CHUNK + off, n)], start=(c2 == 0), stop=(c2 == 1))
                mm.then_inc(m1_mm, 1)

            def output(c_, i):
                pe.wait_ge(m1_out, c_ * 16 + 4 + (8 if (i + 1) * P <= HALVES[0][1] else 16))
                pe.wait_ge(m2_out, 5 * c_ + (5 if i == 0 else i + 4))
                for c2 in range(8):
                    mm = pe.matmul(ps[6 + i % 2][0:P, 0:D], m_h[:, c2, i * P:(i + 1) * P], w_m2[:, c2, :],
                                   start=(c2 == 0), stop=(c2 == 7))
                mm.then_inc(m2_mm, 1)
            with pe.Fori(0, CHUNKS) as c_:
                for at, units, y in MLP_PLAN:
                    step(pe, MLP_AT + MLP_TURNS * c_ + at // EB, at % EB)
                    for j in units:
                        hidden(c_, j)
                    if y is not None:
                        output(c_, y)
            weave(pe, step, MLP_END, TURNS - MLP_END, {})
            phase_end(pe, 10)
            pe.wait_ge(asem["w"], 64)
            for r in range(REL):
                for ic in range(2):
                    i = 2 * r + ic
                    pe.wait_ge(asem["fold_out"], i + 1)
                    for lo, hi, b in ((0, 512, 2 * (i % 2)), (512, QW, 2 * (i % 2) + 1)):
                        for oc in range(2):
                            mm = pe.matmul(ps[b][:, 0:hi - lo], w_relT[:, oc, r * D + ic * 128:r * D + (ic + 1) * 128],
                                           w_in[:, oc, lo:hi], start=(oc == 0), stop=(oc == 1))
                    mm.then_inc(asem["fold"], 1)
            for lo, hi, b in ((0, 512, 4), (512, QW, 5)):
                for oc in range(2):
                    mm = pe.matmul(ps[b][0:REL, 0:hi - lo], b_relT[:, oc, :], w_in[:, oc, lo:hi],
                                   start=(oc == 0), stop=(oc == 1))
            mm.then_inc(asem["fold"], 1)
            phase_end(pe, 11)
            pe.sem_inc(asem["turned"], 1)

            def rel_turn(t, u, k):
                pe.wait_ge(asem["summed"], t + 1)
                for r in range(REL):
                    for c_ in range(2):
                        i = 2 * r + c_
                        pe.transpose(ps[i // 4][:, (i % 4) * P:(i % 4 + 1) * P], agsum[:, r, c_ * 128:(c_ + 1) * 128],
                                     ident[0:P, 0:P])
                pe.transpose(ps[7][0:REL + 1, 0:P], counts7, ident[0:P, 0:P]).then_inc(asem["turned"], 1)

            def rel_qkv(t, u, k):
                for r in range(REL):
                    pe.wait_ge(asem["moved"], 4 * t + 4)
                    pe.wait_ge(asem["qkv_out"], REL * t + r + REL + REL - 1)
                    b = 3 + 2 * (r % 2)
                    for lo, hi, bank in ((0, 512, b), (512, QW, b + 1)):
                        pe.matmul(ps[bank][0:P, 0:hi - lo], aT[:, 2 * r, :], w_rq[r][:, 0, lo:hi], start=True, stop=False)
                        pe.matmul(ps[bank][0:P, 0:hi - lo], aT[:, 2 * r + 1, :], w_rq[r][:, 1, lo:hi], start=False, stop=False)
                        mm = pe.matmul(ps[bank][0:P, 0:hi - lo], countT[:, r, :], b_all[:, lo:hi], start=False, stop=True)
                    mm.then_inc(asem["qkv"], 1)

            def rel_both(t, u, k):
                rel_turn(t, u, k)
                rel_qkv(t, u, k)
            tiles(pe, rel_both)
            phase_end(pe, 12)
            prj1.tensor(pe)
            phase_end(pe, 13)
            prj2.tensor(pe)
            phase_end(pe, 14)
            ln[5].tensor(pe)
            phase_end(pe, 15)
            pe.wait_ge(ffn1_loaded, 96)
            pe.sem_inc(rsem["logits"], 2)

            def ro_logits(t, u, k):
                pe.wait_ge(rsem["lt_ready"], t + 1)
                pe.wait_ge(rsem["ready"], t + 1)
                for c_ in range(2):
                    mm = pe.matmul(ps[u][0:P, 0:EXP], lt_ro[:, u, c_, :], w_ro[:, c_, :], start=(c_ == 0), stop=(c_ == 1))
                mm.then_inc(rsem["logits"], 1)

            def ro_turn(t, u, k):
                pe.wait_ge(rsem["ready"], t + 3)
                pe.wait_ge(rsem["copied"], t + 1)
                pe.transpose(ps[2 + u][0:EXP, 0:P], ro_h[:, u, :], ident[0:P, 0:P])
                pe.matmul(ps[4 + u][:, 0:P], ro_f[:, u:u + 1].broadcast_to([P, 128]), ident[0:P, 0:P],
                          start=True, stop=True).then_inc(rsem["turned"], 1)
            tiles_lagged(pe, ro_logits, ro_turn)
            phase_end(pe, 16)
            with pe.Fori(0, CHUNKS) as c_:
                for j in range(32):
                    h, pc = j // 16, j % 16
                    off, n = HALVES[h]
                    pe.wait_ge(x_relu, c_ * 32 + j + 1)
                    for c2 in range(2):
                        mm = pe.matmul(ps[j % 4][:, 0:n], w_1[:, c2, pc * 128:(pc + 1) * 128],
                                       xnT[:, c2, bass.ds(c_ * CHUNK + off, n)], start=(c2 == 0), stop=(c2 == 1))
                    mm.then_inc(x_mm, 1)
                for i in range(TPC):
                    pe.wait_ge(x_masked, c_ * 32 + (16 if (i + 1) * P <= HALVES[0][1] else 32))
                    pe.wait_ge(x_yout, 5 * c_ + (5 if i == 0 else 6 if i == 4 else i + 1))
                    for c2 in range(16):
                        pe.matmul(ps[4 + i % 4][0:P, 0:D], e_h[:, c2, i * P:(i + 1) * P], w_2[:, c2, :],
                                  start=(c2 == 0), stop=False)
                    pe.matmul(ps[4 + i % 4][0:P, 0:D], e_hot[:, i * P:(i + 1) * P], b_2, start=False, stop=True
                              ).then_inc(x_y, 1)
            phase_end(pe, 17)

        @block.vector
        def _(v):
            v.wait_ge(edge_loaded, 64)
            for a, b in ((src_f, raw_i[0]), (dst_f, raw_i[1]), (typ_f, raw_i[2])):
                v.tensor_copy(a, b)
            v.drain()
            v.scalar_tensor_tensor(out=key1_f, in0=typ_f, scalar=float(NODES), in1=dst_f, op0=ALU.mult, op1=ALU.add)
            v.drain().then_inc(edge_ready, 1)
            v.wait_ge(edge_turned, 1)
            v.tensor_copy(key_col[0][:, :], ps[0][0:P, 0:ETILES])
            v.tensor_copy(gather_col[0][:, :], ps[1][0:P, 0:ETILES])
            v.tensor_copy(key_col[1][:, :], ps[2][0:P, 0:ETILES])
            v.tensor_copy(gather_col[1][:, :], ps[0][0:P, 0:ETILES])
            v.tensor_copy(weight_col, ps[3][0:P, 0:ETILES])
            v.drain()
            for la in range(2):
                v.tensor_scalar(spare_gap[la][:, :], key_col[la][:, :], -1.0, float(SEGS[la]), ALU.mult, ALU.add)
            v.drain()
            for la in range(2):
                v.tensor_scalar(spare_gap[la][:, :], spare_gap[la][:, :], lane[0:P, 0:1], None, ALU.add)
            v.wait_ge(x_loaded, 16)
            phase_end(v, 1)
            ln[0].vector(v)
            phase_end(v, 2)
            step = msg[0].vector_step
            msg[0].vector_start(v)
            att0.woven_vector(v, step, 0, True)
            job_end(v, 1)

            def keep_mix0(t, u):
                v.wait_ge(prj0.product.sem, prj0.product.base + t + 3)
                own(v, "dve")
                v.bn_stats(out=col(m0_st, t * 6, 6), in_=prj0.out(u))
                v.tensor_copy(col(rows, t * D, D), prj0.out(u))
                v.drain().then_inc(prj0.used.sem, 1)
            prj0.woven_vector(v, step, PRJ0_AT, keep_mix0)
            v.drain()
            moments(v, as3(m0_st, 6), D // 2, m0_a, m0_b, m0_q, m0_mean, m0_var).then_inc(m0_stats, 1)
            v.wait_ge(m0_root, 1)

            def add_mix0(t):
                v.scalar_tensor_tensor(out=col(rows, t * D, D), in0=col(rows, t * D, D), scalar=col(m0_mean, t),
                                       in1=gamma0, op0=ALU.subtract, op1=ALU.mult)
                v.drain()
                v.scalar_tensor_tensor(out=col(x_cur, t * D, D), in0=col(rows, t * D, D), scalar=col(m0_rstd, t),
                                       in1=col(x_cur, t * D, D), op0=ALU.mult, op1=ALU.add)
            weave(v, step, NORM0_AT, TILES // 2, {0: [lambda k: add_mix0(2 * k)], 4: [lambda k: add_mix0(2 * k + 1)]})
            add_mix0(TILES - 1)
            weave(v, step, NORM0_AT + TILES // 2, TURNS - 1 - NORM0_AT - TILES // 2, {})
            msg[0].vector_end(v)
            phase_end(v, 3)
            v.wait_ge(gnn0_loaded, 96)
            v.sem_inc(prjg.used.sem, 2)

            def gnn0_rows(t, u, k):
                v.wait_ge(prjg.product.sem, prjg.product.base + t + 3)
                v.tensor_tensor(col(rows, t * D, D), prjg.out(u), gnn_rows[:, 0, :], ALU.add)
                v.drain().then_inc(prjg.used.sem, 1)
                for h in range(HEADS):
                    v.bn_stats(out=col(g_st, t * 24 + h * 6, 6), in_=col(rows, t * D + h * HD, HD))
            tiles(v, gnn0_rows)
            v.drain()
            moments(v, as3(g_st, 6), HD // 2, g_a, g_b, g_q, g_mean, g_var).then_inc(gvar, 1)
            gnn0_norm(v, 1, 0, DVE_TILES, HEADS)
            v.drain().then_inc(gparts, 1)
            v.wait_ge(gparts, 2)

            def row_stats(t, u, k):
                v.bn_stats(out=col(g_st, t * 6, 6), in_=col(rows, t * D, D))
            tiles(v, row_stats, 5)
            v.drain()
            moments(v, as3(g_st[:, 0:TILES * 6], 6), D // 2, *(z[:, 0:TILES] for z in (g_a, g_b, g_q, g_mean, g_var))
                    ).then_inc(gvar, 1)
            gnn0_norm(v, 2, 0, DVE_TILES, 1)
            own_x, own_y = x_cur[:, 0:DVE_TILES * D], rows[:, 0:DVE_TILES * D]
            v.tensor_tensor(own_x, own_x, own_y, ALU.add)
            phase_end(v, 4)
            ln[1].vector(v)
            phase_end(v, 5)
            v.wait_ge(ffn0_loaded, 13 * 16)
            for i in (0, 1):
                v.tensor_scalar(bns[:, 2 * i, :], bnp[:, 5 * i + 4, :], BN_EPS, None, ALU.add)
            v.drain().then_inc(bn_var, 1)
            v.wait_ge(bn_rstd, 1)
            for i in (0, 1):
                b_, g_, be_, m_, _ = (bnp[:, 5 * i + q, :] for q in range(5))
                v.tensor_tensor(bns[:, 2 * i, :], bns[:, 2 * i, :], g_, ALU.mult)
                v.tensor_tensor(bns[:, 2 * i + 1, :], b_, m_, ALU.subtract)
                v.drain()
                v.tensor_tensor(bns[:, 2 * i + 1, :], bns[:, 2 * i + 1, :], bns[:, 2 * i, :], ALU.mult)
                v.drain()
                v.tensor_tensor(bns[:, 2 * i + 1, :], bns[:, 2 * i + 1, :], be_, ALU.add)
            v.drain().then_inc(bn_ready, 1)
            v.wait_ge(gsem["logits"], TILES + 2)
            g3 = as3(gate, MOE)
            v.tensor_tensor(g3, as3(ps[0][0:P, 0:TILES * MOE], MOE), br_row.unsqueeze(1).broadcast_to([P, TILES, MOE]), ALU.add)
            v.drain()
            v.tensor_reduce(gate_sum, g3, AX.X, ALU.max)
            v.drain()
            v.tensor_tensor(g3, g3, over(gate_sum, MOE), ALU.subtract)
            v.drain().then_inc(gsem["shifted"], 1)
            v.wait_ge(gsem["exp"], 1)
            v.tensor_reduce(gate_sum, g3, AX.X, ALU.add)
            v.drain()
            v.reciprocal(gate_sum, gate_sum)
            v.drain()
            v.tensor_tensor(g3, g3, over(gate_sum, MOE), ALU.mult)
            phase_end(v, 6)
            v.sem_inc(y_out, 5)
            with v.Fori(0, MOE // 2) as k:
                for u in range(2):
                    with v.Fori(0, CHUNKS) as c_:
                        ex = 2 * k + u
                        for i in range(TPC):
                            t = c_ * TPC + i
                            v.scalar_tensor_tensor(out=col(x_cur, t * D, D), in0=bo_rows[:, bass.ds(ex, 1), :].rearrange("p a d -> p (a d)"),
                                                   scalar=col(gate, t * MOE + ex), in1=col(x_cur, t * D, D),
                                                   op0=ALU.mult, op1=ALU.add)
                        v.drain()
                        for i in range(TPC):
                            t = c_ * TPC + i
                            v.wait_ge(y_done, 5 * (ex * CHUNKS + c_) + i + 1)
                            own(v, "dve")
                            v.scalar_tensor_tensor(out=col(x_cur, t * D, D), in0=ps[4 + i % 4][0:P, 0:D],
                                                   scalar=col(gate, t * MOE + ex), in1=col(x_cur, t * D, D),
                                                   op0=ALU.mult, op1=ALU.add).then_inc(y_out, 1)
                        v.drain()
            phase_end(v, 7)
            ln[2].vector(v)
            phase_end(v, 8)
            ln[3].stats(v)
            ln[3].moments(v)
            v.wait_ge(fold_mm, 1)
            for oc in range(2):
                for q in range(3):
                    for ic in range(2):
                        v.tensor_copy(w_qkv1[:, ic, q * D + oc * 128:q * D + (oc + 1) * 128],
                                      ps[2 * oc + ic][:, q * 128:(q + 1) * 128])
                    v.tensor_copy(bias1[:, q * D + oc * 128:q * D + (oc + 1) * 128], ps[4 + oc][0:P, q * 128:(q + 1) * 128])
            phase_end(v, 9)
            step = msg[1].vector_step
            msg[1].vector_start(v)
            ln[3].woven_vector(v, step, 0)
            job_end(v, 2)
            att1.woven_vector(v, step, ATT1_AT, False)
            job_end(v, 3)

            def out3(t, u):
                v.wait_ge(prj3.product.sem, prj3.product.base + t + 3)
                v.tensor_tensor(p3_tmp[:, u, :], prj3.out(u), b_o1, ALU.add)
                v.drain().then_inc(prj3.used.sem, 1)
                v.tensor_tensor(col(rows, t * D, D), col(xn, t * D, D), p3_tmp[:, u, :], ALU.add)
                v.drain()
                v.bn_stats(out=col(ln[4].st, t * 6, 6), in_=col(rows, t * D, D))
            prj3.woven_vector(v, step, PRJ3_AT, out3)
            v.drain()
            ln[4].moments(v)
            job_end(v, 4)
            ln[4].woven_vector(v, step, LN4_AT)
            job_end(v, 5)
            v.wait_ge(mlp_loaded, 64)
            v.sem_inc(m2_out, 5)

            def add_mlp(c_, i):
                t = c_ * TPC + i
                v.wait_ge(m2_mm, 5 * c_ + i + 1)
                v.tensor_tensor(m_o[:, i % 2, :], ps[6 + i % 2][0:P, 0:D], b_m2, ALU.add)
                v.drain().then_inc(m2_out, 1)
                v.tensor_tensor(m_o[:, i % 2, :], m_o[:, i % 2, :], col(rows, t * D, D), ALU.add)
                v.drain()
                v.tensor_tensor(col(x_cur, t * D, D), col(x_cur, t * D, D), m_o[:, i % 2, :], ALU.add)
                v.drain()
            with v.Fori(0, CHUNKS) as c_:
                for n, (at, _, _) in enumerate(MLP_PLAN):
                    step(v, MLP_AT + MLP_TURNS * c_ + at // EB, at % EB)
                    if n and MLP_PLAN[n - 1][2] is not None:
                        add_mlp(c_, MLP_PLAN[n - 1][2])
            weave(v, step, MLP_END, TURNS - 1 - MLP_END, {})
            msg[1].vector_end(v)
            phase_end(v, 10)
            v.tensor_copy(row_mask, ident[0:REL + 1, 0:REL])
            v.drain()
            v.tensor_tensor(row_mask, row_mask, ident[0:REL + 1, REL:REL + 1].broadcast_to([REL + 1, REL]), ALU.add)
            phase_end(v, 11)
            v.sem_inc(asem["attended"], 2)
            v.sem_inc(asem["pool_prod_used"], 2)
            s3 = scores.rearrange("p (r s h) -> p r s h", r=REL, s=REL)
            s_in = scores.rearrange("p (r s h) -> p r h s", r=REL, s=REL)
            rh = sc24.rearrange("p (r h) -> p r h", r=REL)
            rh_over = sc24.rearrange("p (r a h) -> p r a h", r=REL, a=1).broadcast_to([P, REL, REL, HEADS])

            def rel_attend(t, u, k):
                v.wait_ge(asem["qkv_out"], REL * (t + 3))
                for r in (r for r in range(REL) if r not in POOL_RELS):
                    v.tensor_tensor(as3(prod, D), QK[:, u, r:r + 1, 0:D].broadcast_to([P, REL, D]),
                                    QK[:, u, :, D:2 * D], ALU.mult)
                    v.drain()
                    v.tensor_reduce(scores[:, r * 24:(r + 1) * 24], as3(prod, HD), AX.X, ALU.add)
                    v.drain()
                for i, r in enumerate(POOL_RELS):
                    v.wait_ge(asem["pool_prod"], len(POOL_RELS) * t + i + 1)
                    v.tensor_reduce(scores[:, r * 24:(r + 1) * 24], as3(pprod[:, i % 2, :], HD), AX.X, ALU.add)
                    v.drain().then_inc(asem["pool_prod_used"], 1)
                v.tensor_reduce(rh, s_in, AX.X, ALU.max)
                v.drain()
                v.tensor_tensor(s3, s3, rh_over, ALU.subtract)
                v.drain().then_inc(asem["shifted"], 1)
                v.wait_ge(asem["exp"], t + 1)
                v.tensor_reduce(rh, s_in, AX.X, ALU.add)
                v.drain()
                v.tensor_scalar(sc24, sc24, float(REL), None, ALU.mult)
                v.drain()
                v.reciprocal(sc24, sc24)
                v.drain()
                v.tensor_tensor(s3, s3, rh_over, ALU.mult)
                v.drain()
                v.tensor_reduce(pbar, scores.rearrange("p (r a) -> p a r", r=REL), AX.X, ALU.add)
                v.drain()
                v.tensor_tensor(as3(prod, HD), V[:, u, :, :].rearrange("p r (h c) -> p (r h) c", c=HD),
                                over(pbar, HD), ALU.mult)
                v.drain().then_inc(asem["attended"], 1)
                v.tensor_reduce(vsum, prod.rearrange("p (s d) -> p d s", s=REL), AX.X, ALU.add)
                v.drain()
                v.tensor_copy(col(rows, t * D, D), vsum)
                v.drain()
            tiles(v, rel_attend)
            phase_end(v, 12)
            v.wait_ge(prj_loaded, 64)
            v.sem_inc(prj1.used.sem, 2)

            def out1(t, u, k):
                v.wait_ge(prj1.product.sem, prj1.product.base + t + 3)
                v.tensor_tensor(prj_tmp[:, u, :], prj1.out(u), b_ao, ALU.add)
                v.drain().then_inc(prj1.used.sem, 1)
                v.tensor_tensor(col(rows, t * D, D), col(xn, t * D, D), prj_tmp[:, u, :], ALU.add)
            tiles(v, out1)
            phase_end(v, 13)
            v.sem_inc(prj2.used.sem, 2)

            def out2(t, u, k):
                v.wait_ge(prj2.product.sem, prj2.product.base + t + 3)
                v.tensor_tensor(prj_tmp[:, u, :], prj2.out(u), b_pr, ALU.add)
                v.drain().then_inc(prj2.used.sem, 1)
                v.tensor_tensor(col(x_cur, t * D, D), col(x_cur, t * D, D), prj_tmp[:, u, :], ALU.add)
            tiles(v, out2)
            phase_end(v, 14)
            ln[5].vector(v)
            phase_end(v, 15)
            v.wait_ge(ffn1_loaded, 96)
            v.wait_ge(rsem["consts"], 1)
            v.tensor_copy(e_col, e_col_i)
            v.tensor_copy(iota32, iota32_i)
            v.drain()
            v.tensor_scalar(e_col[EH:128, :], e_col[EH:128, :], 1.0, None, ALU.add)
            v.sem_inc(rsem["ready"], 2)

            def route(t, u, k):
                v.wait_ge(rsem["logits"], t + 3)
                v.wait_ge(rsem["copied"], t + 1)
                v.tensor_tensor(ro_l[:, u, :], ps[u][0:P, 0:EXP], b_ro, ALU.add)
                v.drain()
                v.max(ro_m[:, u, :], ro_l[:, u, :])
                v.drain()
                v.max_index(ro_i[:, u, :], ro_m[:, u, :], ro_l[:, u, :])
                v.drain()
                v.tensor_copy(ro_f[:, u:u + 1], ro_i[:, u, 0:1])
                v.drain()
                v.tensor_scalar(ro_h[:, u, :], iota32, ro_f[:, u:u + 1], None, ALU.is_equal)
                v.drain().then_inc(rsem["ready"], 1)
            tiles(v, route)
            phase_end(v, 16)
            v.sem_inc(x_yout, 5)
            with v.Fori(0, CHUNKS) as c_:
                v.drain()
                v.tensor_scalar(e_hot, ohT[:, bass.ds(c_ * CHUNK, CHUNK)], 1.0, None, ALU.mult)
                v.drain()
                for j in range(32):
                    h, pc = j // 16, j % 16
                    off, n = HALVES[h]
                    v.wait_ge(x_relu, c_ * 32 + 4 + j + 1)
                    v.scalar_tensor_tensor(out=e_h[:, pc, off:off + n], in0=idxT[:, bass.ds(c_ * CHUNK + off, n)],
                                           scalar=e_col[:, pc:pc + 1], in1=e_h[:, pc, off:off + n],
                                           op0=ALU.is_equal, op1=ALU.mult).then_inc(x_masked, 1)
                for i in range(TPC):
                    t = c_ * TPC + i
                    v.wait_ge(x_y, 5 * c_ + i + 1)
                    own(v, "dve")
                    v.scalar_tensor_tensor(out=col(x_cur, t * D, D), in0=ps[4 + i % 4][0:P, 0:D], scalar=0.0,
                                           in1=col(x_cur, t * D, D), op0=ALU.max, op1=ALU.add).then_inc(x_yout, 1)
            phase_end(v, 17)


def kernel(**inputs):
    import numpy as _np
    import concourse.bacc as _bacc
    from concourse import mybir as _mybir
    from concourse.bass_utils import run_bass_kernel_spmd as _run

    a = {k: _np.ascontiguousarray(v) for k, v in inputs.items()}

    def cols(v):
        return v.reshape(-1, 2, 128).transpose(2, 0, 1).reshape(128, -1)

    lay = {n: a[n] for n in ("x", "src", "dst", "edge_type_6", "edge_weight", "L0_gnn_ln2_g", "L0_gnn_ln2_b",
                             "L0_mix_Wqkv", "L0_mix_Wout", "L0_mix_gamma", "L0_ffn_Wr", "L0_ffn_br",
                             "L1_gnn_in_proj_b", "L1_gnn_attn_out_b", "L1_gnn_proj_b", "L1_mix_Wx", "L1_mix_bo",
                             "L1_mix_b2", "L1_ffn_router_b", "L1_ffn_b2")}
    for n in ("L0_gnn_bias", "L0_gnn_ln1_g", "L0_gnn_ln1_b", "L0_ffn_bo"):
        lay[n] = a[n].reshape(-1)
    for n in ("b1", "g1", "be1", "m1", "v1", "b2", "g2", "be2", "m2", "v2"):
        lay["L0_ffn_" + n] = cols(a["L0_ffn_" + n])
    for n in ("W1", "W2", "Wo"):
        lay["L0_ffn_" + n] = a["L0_ffn_" + n].reshape(-1, 256)
    lay["gnn0_W"] = a["L0_gnn_W"].transpose(1, 0, 2).reshape(256, 256)
    lay["gnn1_W_T"] = a["L1_gnn_W"].transpose(2, 0, 1).reshape(256, -1)
    lay["gnn1_b_T"] = a["L1_gnn_b"].T
    lay["gnn1_in_T"] = a["L1_gnn_in_proj_w"].T
    lay["gnn1_ao_T"] = a["L1_gnn_attn_out_w"].T
    lay["gnn1_pr_T"] = a["L1_gnn_proj_w"].T
    for n in ("ln1_w", "ln1_b", "ln2_w", "ln2_b", "bx"):
        lay["mix1_" + n] = cols(a["L1_mix_" + n])
    lay["mix1_b1"] = a["L1_mix_b1"].reshape(8, 128).T
    for n in ("Wq", "Wk", "Wv", "Wo", "W1", "W2"):
        lay[f"mix1_{n}_T"] = a["L1_mix_" + n].T
    lay["ffn1_W1"] = a["L1_ffn_W1"].transpose(1, 0, 2).reshape(256, -1)
    lay["ffn1_W2"] = a["L1_ffn_W2"].reshape(-1, 256)
    lay["ffn1_b1"] = a["L1_ffn_b1"].reshape(16, 128).T
    lay["ffn1_router_T"] = a["L1_ffn_router_w"].T

    nc = _bacc.Bacc("TRN2", target_bir_lowering=False, num_devices=1)
    arrays, aps = {}, {}
    for n, v in lay.items():
        v = _np.ascontiguousarray(v)
        arrays["in_" + n] = v
        aps[n] = nc.dram_tensor("in_" + n, v.shape, _mybir.dt.from_np(v.dtype), kind="ExternalInput").ap()
    out = nc.dram_tensor("out_rows", (3125, 256), _mybir.dt.float32, kind="ExternalOutput").ap()
    gps_two_layers(nc, aps, out)
    r = _run(nc, [arrays], core_ids=[0])
    return r.results[0]["out_rows"]
```

```python
from contextlib import ExitStack

import numpy as np
import concourse.bass as bass
from concourse import mybir

F32 = mybir.dt.float32
I32 = mybir.dt.int32
BF16 = mybir.dt.bfloat16
U32 = mybir.dt.uint32
ALU = mybir.AluOpType
ACT = mybir.ActivationFunctionType
AX = mybir.AxisListType

NODES = 3125
D = 256
P = 125
TILES = NODES // P
CHUNK = 625
CHUNKS = NODES // CHUNK
HALVES = ((0, 313), (313, 312))
TPC = CHUNK // P
EDGES = 50000
ETILES = EDGES // P
EB = 8
EROWS = 100
EBLK = ETILES // EROWS
REL = 6
HEADS = 4
HD = D // HEADS
MIX_HEADS = 8
MHD = D // MIX_HEADS
MOE = 8
EXP = 32
EH = 64
HID = 1024
BIAS_ROWS = (REL + 1) * 6
EPS = 1e-5
BN_EPS = 1e-3
TABLES = (2, 2)
AGG_ROWS = (3584, 18944)
WIDTH = (D, D + 1)
SEGS = (NODES, REL * NODES)
LOOK = 4
TURNS = ETILES // EB


def gps_two_layers(nc, A, out):
    ctx = ExitStack()
    with ctx:
        def sb(name, shape, dt=F32):
            return ctx.enter_context(nc.sbuf_tensor(name, shape, dt))

        def sem(name):
            return ctx.enter_context(nc.semaphore(name))

        def dram(name, shape, dt=F32):
            return nc.dram_tensor(name, shape, dt, kind="Internal").ap()

        ps = [ctx.enter_context(nc.psum_tensor(f"bank{i}", [128, 512], F32)) for i in range(8)]

        x_cur = sb("x_cur", [P, TILES * D])
        xn_whole = sb("xn", [128, TILES * D])
        xn = xn_whole[0:P, :]
        xnT = sb("xnT", [128, 2, NODES])
        rows = sb("rows", [P, TILES * D])
        ident = sb("ident", [128, 128])
        earlier = sb("earlier", [P, P])
        lane = sb("lane", [128, 1])
        lane_i = sb("lane_i", [128, 1], I32)
        neghalf = sb("neghalf", [128, 32])
        edge_cols = sb("edge_cols", [128, 7 * ETILES])
        key0, key1, gap0, gap1, src0, src1, weight_col = (edge_cols[0:P, i * ETILES:(i + 1) * ETILES] for i in range(7))
        key_col, spare_gap = (key0, key1), (gap0, gap1)
        gather_col = (src0.bitcast(I32), src1.bitcast(I32))
        zeros = sb("zeros", [128, D + 1])
        ARENA = 24300
        arena = sb("arena", [128, ARENA])

        xn_table = dram("xn_table", [NODES, D])
        agg = [[dram(f"agg{la}_{k}", [AGG_ROWS[la], WIDTH[la]]) for k in range(TABLES[la])] for la in range(2)]
        key_row = [dram(f"key_row{la}", [EDGES]) for la in range(2)]

        JOBS_AT = 6640
        NORM_AT = ARENA - 1600

        class Counted:

            def __init__(self, handle, base):
                self.sem, self.base = handle, base

        counts = {}

        def counted(name, total):
            if name not in counts:
                counts[name] = [sem(name), 0]
            handle, base = counts[name]
            counts[name][1] += total
            return Counted(handle, base)

        class Carver:

            def __init__(self):
                self.at = 0

            def __call__(self, parts, cols, dt=F32, **split):
                a = arena[0:parts, self.at:self.at + cols]
                self.at += cols
                assert self.at <= ARENA, self.at
                return a if dt == F32 else a.bitcast(dt)

        phase_done = sem("phase_done")
        engines = 5

        def phase_end(e, n):
            e.drain().then_inc(phase_done, 1)
            e.wait_ge(phase_done, engines * n)

        job_done = sem("job_done")

        def job_end(e, n):
            e.drain().then_inc(job_done, 1)
            e.wait_ge(job_done, 3 * n)

        def weave(e, step, first, turns, pieces):
            with e.Fori(0, turns) as k:
                for u in range(EB):
                    step(e, first + k, u)
                    for piece in pieces.get(u, ()):
                        piece(k)

        paces = {n: sem(f"pace_{n}") for n in ("act", "pool", "dve", "pe")}

        def own(e, name):
            e.sem_inc(paces[name], 1)

        def tiles(e, body, n=2):
            turns = TILES // n
            with e.Fori(0, turns) as k:
                for u in range(n):
                    body(n * k + u, u, k)
            for u in range(TILES % n):
                body(n * turns + u, u, turns)

        def tiles_lagged(e, ahead, behind, n=2):
            assert TILES % n == 1
            ahead(0, 0, 0)
            with e.Fori(0, TILES // n) as k:
                for u in range(n):
                    ahead(n * k + u + 1, (u + 1) % n, k + (u + 1) // n)
                    behind(n * k + u, u, k)
            behind(TILES - 1, 0, TILES // n)

        def col(ap, i, n=1):
            return ap[:, bass.ds(i, n)]

        def cm(v):
            return v.rearrange("(c p) n -> p c n", p=128)

        def as3(ap, b):
            return ap.rearrange("p (a b) -> p a b", b=b)

        def over(ap, n):
            return ap.unsqueeze(2).broadcast_to([ap.shape[0], ap.shape[1], n])

        def row_of(v, n, parts=128):
            return v.rearrange("(a n) -> a n", a=1).broadcast_to([parts, n])

        def moments(e, st, half, a, b, q, mean, var):
            n = 2 * half
            e.tensor_tensor(a, st[:, :, 1], st[:, :, 4], ALU.add)
            e.tensor_tensor(b, st[:, :, 1], st[:, :, 4], ALU.subtract)
            e.tensor_tensor(q, st[:, :, 2], st[:, :, 5], ALU.add)
            e.drain()
            e.tensor_scalar(mean, a, 0.5, None, ALU.mult)
            e.tensor_tensor(b, b, b, ALU.mult)
            e.tensor_scalar(q, q, 1.0 / n, EPS, ALU.mult, ALU.add)
            e.drain()
            return e.scalar_tensor_tensor(out=var, in0=b, scalar=0.25, in1=q, op0=ALU.mult, op1=ALU.add)

        class Norm:

            def __init__(s, src, dst, affine, nb=5, turned=True):
                s.src, s.dst, s.affine, s.nb, s.make_turned = src, dst, affine, nb, turned
                s.stats_ready = counted("ln_stats_ready", 1)
                s.rstd_ready = counted("ln_rstd_ready", 1)
                if turned:
                    s.stage_ready = counted("ln_stage_ready", TILES)
                    s.turned = counted("ln_turned", TILES + nb)
                    s.turned_out = counted("ln_turned_out", TILES + nb)
                c = Carver()
                c.at = NORM_AT
                s.st = c(P, TILES * 6)
                s.a, s.b, s.q, s.mean, s.var, s.rstd = [c(P, TILES) for _ in range(6)]
                s.stage = as3(c(P, nb * D), D)
                c.at += 4 * max(0, affine - 1)
                s.gcol, s.bcol = c(128, 2), c(128, 2)

            def stats(s, e):
                def stats_of(t, u, k):
                    e.bn_stats(out=col(s.st, t * 6, 6), in_=col(s.src, t * D, D))
                tiles(e, stats_of, 5)
                e.drain()

            def moments(s, e):
                moments(e, as3(s.st, 6), D // 2, s.a, s.b, s.q, s.mean, s.var).then_inc(s.stats_ready.sem, 1)

            def scale(s, e, t, u):
                e.wait_ge(s.turned.sem, s.turned.base + t + 1)
                e.tensor_scalar(s.stage[:, u, :], col(s.src, t * D, D), col(s.mean, t), col(s.rstd, t),
                                ALU.subtract, ALU.mult).then_inc(s.stage_ready.sem, 1)

            def keep(s, e, t):
                e.tensor_scalar(col(s.dst, t * D, D), col(s.src, t * D, D), col(s.mean, t), col(s.rstd, t),
                                ALU.subtract, ALU.mult)

            def turn(s, e, t, u):
                e.wait_ge(s.stage_ready.sem, s.stage_ready.base + t + 1)
                e.wait_ge(s.turned_out.sem, s.turned_out.base + t + 1)
                e.transpose(ps[u][:, 0:P], s.stage[:, u, 0:128], ident[0:P, 0:P])
                e.transpose(ps[u][:, P:2 * P], s.stage[:, u, 128:256], ident[0:P, 0:P]).then_inc(s.turned.sem, 1)

            def move(s, e, t, u):
                e.wait_ge(s.turned.sem, s.turned.base + t + s.nb + 1)
                own(e, "act")
                if s.affine:
                    e.activation(xnT[:, 0, bass.ds(t * P, P)], ps[u][:, 0:P], ACT.Identity,
                                 bias=s.bcol[:, 0:1], scale=s.gcol[:, 0:1])
                    e.activation(xnT[:, 1, bass.ds(t * P, P)], ps[u][:, P:2 * P], ACT.Identity,
                                 bias=s.bcol[:, 1:2], scale=s.gcol[:, 1:2]).then_inc(s.turned_out.sem, 1)
                else:
                    e.activation(xnT[:, :, bass.ds(t * P, P)], as3(ps[u][:, 0:2 * P], P),
                                 ACT.Copy).then_inc(s.turned_out.sem, 1)

            def vector(s, e):
                s.stats(e)
                s.moments(e)
                s.vector_rows(e)

            def vector_rows(s, e):
                e.wait_ge(s.rstd_ready.sem, s.rstd_ready.base + 1)

                def rows_of(t, u, k):
                    if s.make_turned:
                        s.scale(e, t, u)
                    if s.dst is not None:
                        s.keep(e, t)
                tiles(e, rows_of, s.nb)

            def gpsimd(s, e):
                e.wait_ge(s.stats_ready.sem, s.stats_ready.base + 1)
                e.tensor_tensor(s.rstd, s.var, neghalf[0:P, 0:TILES], ALU.pow).then_inc(s.rstd_ready.sem, 1)

            def tensor(s, e):
                e.sem_inc(s.turned.sem, s.nb)
                tiles(e, lambda t, u, k: s.turn(e, t, u), s.nb)

            def scalar(s, e):
                e.sem_inc(s.turned_out.sem, s.nb)
                tiles(e, lambda t, u, k: s.move(e, t, u), s.nb)

            def scalar_for_product(s, e, lt, used):
                e.sem_inc(s.turned_out.sem, s.nb)

                def move(t, u, k):
                    e.wait_ge(s.turned.sem, s.turned.base + t + s.nb + 1)
                    own(e, "act")
                    e.activation(xnT[:, :, bass.ds(t * P, P)], as3(ps[u][:, 0:2 * P], P), ACT.Copy)
                    e.wait_ge(used, t + 1)
                    e.activation(lt[:, u, :, :], as3(ps[u][:, 0:2 * P], P), ACT.Copy).then_inc(s.turned_out.sem, 1)
                tiles(e, move, s.nb)

            def tensor_with_product(s, e, first, last, product):
                with e.Fori(first // s.nb, last // s.nb) as k:
                    for u in range(s.nb):
                        s.turn(e, s.nb * k + u, u)
                    for u in range(s.nb):
                        e.wait_ge(s.turned_out.sem, s.turned_out.base + s.nb * (k + 1) + u + 1)
                        product(s.nb * k + u, u)

            def woven(s, e, step, first, piece):
                assert TILES % EB == 1 and EB % s.nb == 0
                weave(e, step, first, TILES // EB, {u: [lambda k, u=u: piece(e, EB * k + u, u % s.nb)] for u in range(EB)})
                piece(e, TILES - 1, 0)

            def woven_vector(s, e, step, first):
                e.wait_ge(s.rstd_ready.sem, s.rstd_ready.base + 1)
                s.woven(e, step, first, s.scale)

            def woven_tensor(s, e, step, first):
                e.sem_inc(s.turned.sem, s.nb)
                s.woven(e, step, first, s.turn)

            def woven_scalar(s, e, step, first):
                e.sem_inc(s.turned_out.sem, s.nb)
                s.woven(e, step, first, s.move)

        class Messages:

            def __init__(s, la, table):
                s.la, s.table, s.width, s.tables = la, table, WIDTH[la], TABLES[la]
                s.keys_loaded = [counted(f"msg_keys_loaded{h}", 16 * TURNS) for h in range(2)]
                s.picked = counted("msg_picked", ETILES)
                s.merged = counted("msg_merged", ETILES + EB)
                s.sums_out = counted("msg_sums_out", ETILES + 2)
                s.gathered = [counted(f"msg_gathered{u}", 16 * TURNS) for u in range(EB)]
                s.lag = EB // s.tables
                s.scattered = [counted(f"msg_scattered{k}", 16 * (s.lag + ETILES // s.tables)) for k in range(s.tables)]
                c = Carver()
                s.keys = c(128, EB * P)
                s.got = as3(c(P, EB * (D + 1)), D + 1)
                s.pick = as3(c(P, EB * P), P)
                s.sums = as3(c(P, EB * (D + 1)), D + 1)
                s.same = as3(c(P, 2 * P), P)
                s.junk = as3(c(P, 2 * P), P)
                s.count = c(P, 2)
                s.move = c(P, 2)
                s.gather_index = c(P, EB, I32)
                s.scatter_index = c(P, EB, I32)
                assert c.at <= JOBS_AT

            def sync_load(s, e, i, h):
                n = EB // 2 * P
                e.dma_start(s.keys[:, h * n:(h + 1) * n], key_row[s.la][bass.ds(i * EB * P + h * n, n)]
                            .rearrange("(a n) -> a n", a=1).broadcast_to([128, n])
                            ).then_inc(s.keys_loaded[h].sem, 16)

            def sync_turns(s, e, first, last):
                with e.Fori(first, last) as i:
                    for h in range(2):
                        e.wait_ge(s.picked.sem, s.picked.base + (i - 1) * EB + (h + 1) * (EB // 2))
                        s.sync_load(e, i, h)

            def pick_pair(s, e, i, u):
                n = i * EB + u
                if u % (EB // 2) == 0:
                    half = s.keys_loaded[u // (EB // 2)]
                    e.wait_ge(half.sem, half.base + 16 * (i + 1))
                e.wait_ge(s.merged.sem, s.merged.base + n + 2)
                own(e, "dve")
                for k in range(2):
                    keys = s.keys[0:P, (u + k) * P:(u + k + 1) * P]
                    if s.la == 0:
                        e.tensor_scalar(s.same[:, k, :], keys, col(key_col[0], n + k), None, ALU.is_equal)
                        e.tensor_scalar(s.pick[:, u + k, :], keys, col(key_col[0], n + k), col(weight_col, n + k),
                                        ALU.is_equal, ALU.mult)
                    else:
                        e.tensor_scalar(s.pick[:, u + k, :], keys, col(key_col[1], n + k), None, ALU.is_equal)
                e.drain()
                for k in range(2):
                    e.tensor_tensor_reduce(out=s.junk[:, k, :], in0=s.same[:, k, :] if s.la == 0 else s.pick[:, u + k, :],
                                           in1=earlier[:, :], scale=1.0, scalar=0.0,
                                           op0=ALU.mult, op1=ALU.add, accum_out=s.count[:, k:k + 1])
                for k in range(2):
                    s.buffer_landed(e, i, u + k)
                own(e, "dve")
                e.tensor_copy(s.gather_index[:, u:u + 2], col(gather_col[s.la], n, 2))
                e.drain()
                e.scalar_tensor_tensor(out=s.move, in0=s.count, scalar=1.0, in1=col(spare_gap[s.la], n, 2),
                                       op0=ALU.min, op1=ALU.mult)
                e.drain()
                e.tensor_tensor(s.scatter_index[:, u:u + 2], s.move, col(key_col[s.la], n, 2), ALU.add)
                e.drain().then_inc(s.picked.sem, 2)

            def vector_start(s, e):
                s.cleared(e)
                for u in range(0, LOOK, 2):
                    s.pick_pair(e, 0, u)

            def vector_step(s, e, i, u):
                if u % 2 == 0:
                    s.pick_pair(e, i + (u + LOOK) // EB, (u + LOOK) % EB)

            def vector_end(s, e):
                for u in range(EB - LOOK):
                    s.vector_step(e, TURNS - 1, u)

            def clear(s, e, tables):
                part = AGG_ROWS[s.la] // s.lag
                for k in tables:
                    for h in range(s.lag):
                        e.dma_start(agg[s.la][k][h * part:(h + 1) * part, :].rearrange("(p a) d -> p a d", p=128),
                                    zeros[:, 0:s.width].unsqueeze(1).broadcast_to([128, part // 128, s.width])
                                    ).then_inc(s.scattered[k].sem, 16)

            def cleared(s, e):
                for k in range(s.tables):
                    e.wait_ge(s.scattered[k].sem, s.scattered[k].base + 16 * s.lag)

            def buffer_landed(s, e, i, u):
                table = s.scattered[u % s.tables]
                e.wait_ge(table.sem, table.base + 16 * (i * s.lag + u // s.tables + 1))

            def gather(s, e, i, u):
                e.wait_ge(s.picked.sem, s.picked.base + i * EB + u + 1)
                own(e, "pool")
                e.indirect_dma_start(out=s.got[:, u, 0:D], out_offset=None, in_=s.table[:, :],
                                     in_offset=bass.IndirectOffsetOnAxis(ap=s.gather_index[:, u:u + 1], axis=0)
                                     ).then_inc(s.gathered[u].sem, 16)

            def scatter(s, e, i, u):
                table = s.scattered[u % s.tables]
                e.wait_ge(s.sums_out.sem, s.sums_out.base + i * EB + u + 3)
                e.wait_ge(table.sem, table.base + 16 * (i * s.lag + u // s.tables + s.lag))
                own(e, "pool")
                e.indirect_dma_start(out=agg[s.la][u % s.tables][:, :], in_=s.sums[:, u, 0:s.width], in_offset=None,
                                     out_offset=bass.IndirectOffsetOnAxis(ap=s.scatter_index[:, u:u + 1], axis=0),
                                     compute_op=ALU.add).then_inc(table.sem, 16)

            def gpsimd_start(s, e):
                e.memset(s.got[:, :, D:D + 1], 1.0)
                e.drain()
                s.cleared(e)
                e.wait_ge(table_written, 16 * (s.la + 1))
                for u in range(LOOK):
                    s.gather(e, 0, u)

            def gpsimd_step(s, e, i, u):
                s.scatter(e, i, u)
                s.gather(e, i + (u + LOOK) // EB, (u + LOOK) % EB)

            def gpsimd_end(s, e):
                for u in range(EB):
                    s.scatter(e, TURNS - 1, u)
                    if u < EB - LOOK:
                        s.gather(e, TURNS - 1, u + LOOK)
                for k in range(s.tables):
                    e.wait_ge(s.scattered[k].sem, s.scattered[k].base + 16 * (s.lag + ETILES // s.tables))

            def tensor_start(s, e):
                e.sem_inc(s.merged.sem, EB)

            def tensor_step(s, e, i, u):
                n = i * EB + u
                e.wait_ge(s.picked.sem, s.picked.base + n + 1)
                e.wait_ge(s.gathered[u].sem, s.gathered[u].base + 16 * (i + 1))
                e.wait_ge(s.sums_out.sem, s.sums_out.base + n + 1)
                e.matmul(ps[4 + u % 2][0:P, 0:s.width], s.pick[:, u, :], s.got[:, u, 0:s.width],
                         start=True, stop=True).then_inc(s.merged.sem, 1)

            def scalar_start(s, e):
                s.cleared(e)
                e.sem_inc(s.sums_out.sem, 2)

            def scalar_step(s, e, i, u):
                n = i * EB + u
                e.wait_ge(s.merged.sem, s.merged.base + n + EB + 1)
                s.buffer_landed(e, i, u)
                e.activation(s.sums[:, u, 0:s.width], ps[4 + u % 2][0:P, 0:s.width], ACT.Copy).then_inc(s.sums_out.sem, 1)

        class Project:

            def __init__(s, weights, at=0, staged=True):
                s.staged = counted("prj_staged", TILES if staged else 0)
                s.turned = counted("prj_turned", TILES + 2)
                s.moved = counted("prj_moved", TILES + 2)
                s.product = counted("prj_product", TILES + 2)
                s.used = counted("prj_used", TILES + 2)
                s.w = weights
                c = Carver()
                c.at = at
                s.stage = as3(c(P, 2 * D), D)
                s.lt = c(128, 2 * 2 * P).rearrange("p (u c n) -> p u c n", u=2, c=2)
                s.end = c.at

            def gpsimd(s, e, src):
                def fill(t, u, k):
                    e.wait_ge(s.turned.sem, s.turned.base + t + 1)
                    own(e, "pool")
                    e.tensor_copy(s.stage[:, u, :], col(src, t * D, D)).then_inc(s.staged.sem, 1)
                tiles(e, fill)

            def fill(s, e, t, u):
                e.wait_ge(s.turned.sem, s.turned.base + t + 1)
                own(e, "act")
                e.activation(s.stage[:, u, :], col(rows, t * D, D), ACT.Copy).then_inc(s.staged.sem, 1)

            def turn(s, e, t, u):
                e.wait_ge(s.staged.sem, s.staged.base + t + 1)
                e.wait_ge(s.moved.sem, s.moved.base + t + 1)
                e.transpose(ps[u][:, 0:P], s.stage[:, u, 0:128], ident[0:P, 0:P])
                e.transpose(ps[u][:, P:2 * P], s.stage[:, u, 128:256], ident[0:P, 0:P]).then_inc(s.turned.sem, 1)

            def multiply(s, e, t, u):
                e.wait_ge(s.moved.sem, s.moved.base + t + 3)
                e.wait_ge(s.used.sem, s.used.base + t + 1)
                for c in range(2):
                    mm = e.matmul(ps[2 + u][0:P, 0:D], s.lt[:, u, c, :], s.w[:, c, :],
                                  start=(c == 0), stop=(c == 1))
                mm.then_inc(s.product.sem, 1)

            def move(s, e, t, u):
                e.wait_ge(s.turned.sem, s.turned.base + t + 3)
                e.wait_ge(s.product.sem, s.product.base + t + 1)
                e.activation(s.lt[:, u, :, :], as3(ps[u][:, 0:2 * P], P), ACT.Copy).then_inc(s.moved.sem, 1)

            def tensor(s, e, turn=None, n=2):
                e.sem_inc(s.turned.sem, 2)
                e.sem_inc(s.product.sem, 2)
                tiles_lagged(e, turn or (lambda t, u, k: s.turn(e, t, u)), lambda t, u, k: s.multiply(e, t, u % 2), n)

            def scalar(s, e):
                e.sem_inc(s.moved.sem, 2)
                tiles(e, lambda t, u, k: s.move(e, t, u))

            def out(s, u):
                return ps[2 + u][0:P, 0:D]

            def woven_tensor(s, e, step, first):
                e.sem_inc(s.turned.sem, 2)
                e.sem_inc(s.product.sem, 2)
                s.turn(e, 0, 0)
                weave(e, step, first, TILES // 4, {2 * b: [
                    lambda k, b=b: s.turn(e, 4 * k + b + 1, (b + 1) % 2),
                    lambda k, b=b: s.multiply(e, 4 * k + b, b % 2)] for b in range(4)})
                s.multiply(e, TILES - 1, 0)

            def woven_scalar(s, e, step, first):
                e.sem_inc(s.moved.sem, 2)
                s.fill(e, 0, 0)
                s.move(e, 0, 0)
                weave(e, step, first, TILES // 4, {
                    **{2 * b: [lambda k, b=b: s.fill(e, 4 * k + b + 1, (b + 1) % 2)] for b in range(4)},
                    **{2 * b + 1: [lambda k, b=b: s.move(e, 4 * k + b + 1, (b + 1) % 2)] for b in range(4)}})

            def woven_vector(s, e, step, first, use):
                e.sem_inc(s.used.sem, 2)
                weave(e, step, first, TILES // 4, {2 * b + 1: [lambda k, b=b: use(4 * k + b, b % 2)] for b in range(4)})
                use(TILES - 1, 0)

        class Attend:
            def __init__(s, at, scale, wqkv, bias, w_out):
                s.scale, s.wqkv, s.bias, s.w_out = scale, wqkv, bias, w_out
                s.k_product = counted("mix_k_product", 4 * CHUNKS)
                s.k_reduced = counted("mix_k_reduced", 4 * CHUNKS + 4)
                s.k_max = counted("mix_k_max", 1)
                s.k_row = counted("mix_k_row", 1)
                s.shift = counted("mix_shift", 1)
                s.lt_ready = counted("mix_lt_ready", TILES)
                s.qkv = counted("mix_qkv", TILES + 2)
                s.qkv_out = counted("mix_qkv_out", TILES + 2)
                s.q_shifted = counted("mix_q_shifted", TILES)
                s.k_exp = counted("mix_k_exp", TILES)
                s.q_exp = counted("mix_q_exp", TILES)
                s.ctx_sum = counted("mix_ctx_sum", TILES + 2)
                s.ctx_closed = counted("mix_ctx_closed", 1)
                s.blocks = counted("mix_blocks", 1)
                s.blocks_turned = counted("mix_blocks_turned", 1)
                s.blocks_out = counted("mix_blocks_out", 1)
                s.folded = counted("mix_folded", 1)
                s.v_out = counted("mix_v_out", TILES + 2 if bias is None else 0)
                c = Carver()
                c.at = at
                s.lt_at = c.at
                s.lt = c(128, 4 * P).rearrange("p (u c n) -> p u c n", u=2, c=2)
                s.part = c(128, 4)
                s.part_new = c(128, 4)
                s.kmax = c(128, 2)
                s.shift_row = c(P, D)
                s.tmp = c(P, D)
                s.ks = as3(c(P, 2 * D), D)
                s.ke = as3(c(P, 2 * D), D)
                s.qb = as3(c(P, 2 * D), D)
                s.qe = as3(c(P, 2 * D), D)
                s.v1 = as3(c(P, 2 * (D + 1)), D + 1)
                s.q8 = as3(c(P, 2 * MIX_HEADS), MIX_HEADS)
                s.zero = c(P, D + 1)
                s.rs = c(128, 2)
                s.bd = as3(c(128, 2 * D), D)
                s.bdT = as3(c(128, 2 * 128), 128)
                s.m_at = c.at
                s.m = as3(c(128, 2 * D), D)
                s.end = c.at

            def woven_tensor(s, e, step, first):
                def keys_product(c, j):
                    oc, (off, n) = j // 2, HALVES[j % 2]
                    e.wait_ge(s.k_reduced.sem, s.k_reduced.base + 4 * c + j + 1)
                    for k in range(2):
                        mm = e.matmul(ps[j][:, 0:n], s.wqkv[:, k, D + oc * 128:D + (oc + 1) * 128],
                                      xnT[:, k, bass.ds(c * CHUNK + off, n)], start=(k == 0), stop=(k == 1))
                    mm.then_inc(s.k_product.sem, 1)
                weave(e, step, first, CHUNKS, {2 * j: [lambda c, j=j: keys_product(c, j)] for j in range(4)})
                first += CHUNKS
                e.wait_ge(s.k_max.sem, s.k_max.base + 1)
                for oc in range(2):
                    mm = e.matmul(ps[0][0:P, oc * 128:(oc + 1) * 128], s.kmax[:, oc:oc + 1].broadcast_to([128, P]),
                                  ident[:, :], start=True, stop=True, skip_group_check=True)
                mm.then_inc(s.k_row.sem, 1)
                e.wait_ge(s.shift.sem, s.shift.base + 1)
                for c in range(2):
                    e.matmul(ps[6 + c][:, 0:D + 1], s.zero[:, 0:128], s.zero, start=True, stop=False)
                e.sem_inc(s.qkv.sem, 2)
                e.sem_inc(s.ctx_sum.sem, 2)

                def project(t, u, k):
                    e.wait_ge(s.lt_ready.sem, s.lt_ready.base + t + 1)
                    e.wait_ge(s.qkv_out.sem, s.qkv_out.base + t + 1)
                    if s.bias is None:
                        e.wait_ge(s.v_out.sem, s.v_out.base + t + 1)
                    for c in range(2):
                        e.matmul(ps[u][0:P, 0:512], s.lt[:, u, c, :], s.wqkv[:, c, 0:512],
                                 start=(c == 0), stop=(c == 1))
                    for c in range(2):
                        mm = e.matmul(ps[2 + u][0:P, 0:D], s.lt[:, u, c, :], s.wqkv[:, c, 512:768],
                                      start=(c == 0), stop=(c == 1))
                    mm.then_inc(s.qkv.sem, 1)

                def context(t, u, k):
                    e.wait_ge(s.k_exp.sem, s.k_exp.base + t + 1)
                    if s.bias is None:
                        e.wait_ge(s.v_out.sem, s.v_out.base + t + 3)
                    for c in range(2):
                        mm = e.matmul(ps[6 + c][:, 0:D + 1], s.ke[:, u, c * 128:(c + 1) * 128], s.v1[:, u, :],
                                      start=False, stop=False)
                    mm.then_inc(s.ctx_sum.sem, 1)
                project(0, 0, 0)
                weave(e, step, first, TILES // 2, {4 * b + 1: [
                    lambda k, b=b: project(2 * k + b + 1, 1 - b, 0), lambda k, b=b: context(2 * k + b, b, 0)] for b in range(2)})
                context(TILES - 1, 0, 0)
                for c in range(2):
                    mm = e.matmul(ps[6 + c][:, 0:D + 1], s.zero[:, 0:128], s.zero, start=False, stop=True)
                mm.then_inc(s.ctx_closed.sem, 1)
                e.wait_ge(s.blocks.sem, s.blocks.base + 1)
                for c in range(2):
                    mm = e.transpose(ps[0][:, c * 128:(c + 1) * 128], s.bd[:, c, c * 128:(c + 1) * 128], ident[:, :])
                mm.then_inc(s.blocks_turned.sem, 1)
                e.wait_ge(s.blocks_out.sem, s.blocks_out.base + 1)
                for c in range(2):
                    mm = e.matmul(ps[1][:, c * D:(c + 1) * D], s.bdT[:, c, :], s.w_out[:, c, :],
                                  start=True, stop=True, skip_group_check=True)
                mm.then_inc(s.folded.sem, 1)

            def woven_scalar(s, e, step, first):
                weave(e, step, first, CHUNKS, {})
                first += CHUNKS

                def fill(t, u):
                    e.wait_ge(s.qkv.sem, s.qkv.base + t + 1)
                    own(e, "act")
                    e.activation(s.lt[:, u, :, :], xnT[:, :, bass.ds(t * P, P)], ACT.Copy).then_inc(s.lt_ready.sem, 1)

                def exps(t, u):
                    e.wait_ge(s.qkv_out.sem, s.qkv_out.base + t + 3)
                    e.wait_ge(s.ctx_sum.sem, s.ctx_sum.base + t + 1)
                    e.activation(s.ke[:, u, :], s.ks[:, u, :], ACT.Exp).then_inc(s.k_exp.sem, 1)
                    e.wait_ge(s.q_shifted.sem, s.q_shifted.base + t + 1)
                    e.activation(s.qe[:, u, :], s.qb[:, u, :], ACT.Exp).then_inc(s.q_exp.sem, 1)

                def values(t, u):
                    e.wait_ge(s.qkv.sem, s.qkv.base + t + 3)
                    e.wait_ge(s.ctx_sum.sem, s.ctx_sum.base + t + 1)
                    e.activation(s.v1[:, u, 0:D], ps[2 + u][0:P, 0:D], ACT.Copy).then_inc(s.v_out.sem, 1)
                fill(0, 0)
                pieces = {4 * b: [lambda k, b=b: fill(2 * k + b + 1, 1 - b),
                                  lambda k, b=b: exps(2 * k + b, b)] for b in range(2)}
                if s.bias is None:
                    e.sem_inc(s.v_out.sem, 2)
                    values(0, 0)
                    pieces.update({4 * b + 2: [lambda k, b=b: values(2 * k + b + 1, 1 - b)] for b in range(2)})
                weave(e, step, first, TILES // 2, pieces)
                exps(TILES - 1, 0)

            def woven_vector(s, e, step, first):
                e.sem_inc(s.k_reduced.sem, 4)
                e.memset(s.part, -3.0e38)
                e.memset(s.zero, 0.0)
                e.memset(s.bd[:, :, :], 0.0)
                e.memset(s.v1[:, :, D:D + 1], 1.0)

                def keys_max(c, j):
                    n = HALVES[j % 2][1]
                    e.wait_ge(s.k_product.sem, s.k_product.base + 4 * c + j + 1)
                    e.tensor_reduce(s.part_new[:, j:j + 1], ps[j][:, 0:n], AX.X, ALU.max).then_inc(s.k_reduced.sem, 1)
                    if j == 3:
                        e.drain()
                        e.tensor_tensor(s.part, s.part, s.part_new, ALU.max)
                        e.drain()
                weave(e, step, first, CHUNKS, {2 * j + 1: [lambda c, j=j: keys_max(c, j)] for j in range(4)})
                first += CHUNKS
                p2 = as3(s.part, 2)
                e.tensor_tensor(s.kmax, p2[:, :, 0], p2[:, :, 1], ALU.max)
                e.drain().then_inc(s.k_max.sem, 1)
                e.wait_ge(s.k_row.sem, s.k_row.base + 1)
                if s.bias is None:
                    e.tensor_scalar(s.shift_row, ps[0][0:P, 0:D], -1.0, None, ALU.mult)
                else:
                    e.tensor_tensor(s.tmp, ps[0][0:P, 0:D], s.bias[:, D:2 * D], ALU.add)
                    e.drain()
                    e.tensor_tensor(s.shift_row, s.bias[:, D:2 * D], s.tmp, ALU.subtract)
                e.drain().then_inc(s.shift.sem, 1)
                e.sem_inc(s.qkv_out.sem, 2)

                def spread(t, u, k):
                    e.wait_ge(s.qkv.sem, s.qkv.base + t + 3)
                    e.wait_ge(s.ctx_sum.sem, s.ctx_sum.base + t + 1)
                    e.tensor_tensor(s.ks[:, u, :], ps[u][0:P, D:2 * D], s.shift_row, ALU.add)
                    q_out = q3 = as3(s.qb[:, u, :], MHD)
                    if s.bias is None:
                        q3 = as3(ps[u][0:P, 0:D], MHD)
                    else:
                        e.tensor_tensor(s.v1[:, u, 0:D], ps[2 + u][0:P, 0:D], s.bias[:, 2 * D:3 * D], ALU.add)
                        e.tensor_tensor(s.qb[:, u, :], ps[u][0:P, 0:D], s.bias[:, 0:D], ALU.add)
                        e.drain().then_inc(s.qkv_out.sem, 1)
                    e.tensor_reduce(s.q8[:, u, :], q3, AX.X, ALU.max)
                    e.drain()
                    e.tensor_tensor(q_out, q3, over(s.q8[:, u, :], MHD), ALU.subtract)
                    e.drain().then_inc(s.q_shifted.sem, 1)
                    if s.bias is None:
                        e.sem_inc(s.qkv_out.sem, 1)

                def finish(t, u, k):
                    e.wait_ge(s.q_exp.sem, s.q_exp.base + t + 1)
                    q3 = as3(s.qe[:, u, :], MHD)
                    e.tensor_reduce(s.q8[:, u, :], q3, AX.X, ALU.add)
                    e.drain()
                    e.reciprocal(s.q8[:, u, :], s.q8[:, u, :])
                    e.drain()
                    e.tensor_tensor(as3(col(rows, t * D, D), MHD), q3, over(s.q8[:, u, :], MHD), ALU.mult)
                    e.drain()
                spread(0, 0, 0)
                weave(e, step, first, TILES // 2, {
                    2: [lambda k: finish(2 * k, 0, 0)], 3: [lambda k: spread(2 * k + 1, 1, 0)],
                    6: [lambda k: finish(2 * k + 1, 1, 0)], 7: [lambda k: spread(2 * k + 2, 0, 0)]})
                finish(TILES - 1, 0, 0)
                e.wait_ge(s.ctx_closed.sem, s.ctx_closed.base + 1)
                for c in range(2):
                    e.reciprocal(s.rs[:, c:c + 1], ps[6 + c][:, D:D + 1])
                e.drain()
                for h in range(MIX_HEADS):
                    c, p0 = h // 4, (h % 4) * MHD
                    e.tensor_scalar(s.bd[p0:p0 + MHD, c, h * MHD:(h + 1) * MHD],
                                    ps[6 + c][p0:p0 + MHD, h * MHD:(h + 1) * MHD],
                                    s.rs[p0:p0 + MHD, c:c + 1], s.scale, ALU.mult, ALU.mult)
                e.drain().then_inc(s.blocks.sem, 1)
                e.wait_ge(s.blocks_turned.sem, s.blocks_turned.base + 1)
                e.tensor_copy(s.bdT[:, :, :], as3(ps[0][:, 0:256], 128))
                e.drain().then_inc(s.blocks_out.sem, 1)
                e.wait_ge(s.folded.sem, s.folded.base + 1)
                e.tensor_copy(s.m[:, :, :], as3(ps[1][:, 0:512], D))

        edge_loaded, edge_ready, edge_turned, consts_ready = (sem(n) for n in (
            "edge_loaded", "edge_ready", "edge_turned", "consts_ready"))
        x_loaded, rows_written, table_written, out_written = (sem(n) for n in (
            "x_loaded", "rows_written", "table_written", "out_written"))
        c = Carver()
        raw_i = [c(EROWS, EBLK * P, I32) for _ in range(3)]
        raw_w = c(EROWS, EBLK * P)
        src_f, dst_f, typ_f, key1_f = [c(EROWS, EBLK * P) for _ in range(4)]
        ones_c = c(128, 128)

        ln = [Norm(x_cur, xn, 0), Norm(x_cur, None, 0), Norm(x_cur, xn, 0, nb=4, turned=False),
              Norm(xn, None, 1, nb=4), Norm(rows, None, 2, nb=4), Norm(x_cur, None, 0)]

        c = Carver()
        c.at = JOBS_AT
        w_qkv0 = as3(c(128, 2 * 768), 768)
        w_out0 = as3(c(128, 2 * D), D)
        gamma0 = c(P, D)
        mix0_loaded = sem("mix0_loaded")
        att0 = Attend(c.at, MHD ** -0.5, w_qkv0, None, w_out0)
        prj0 = Project(att0.m, att0.end)
        c.at = prj0.end
        m0_st = c(P, TILES * 6)
        m0_a, m0_b, m0_q, m0_mean, m0_var, m0_rstd = [c(P, TILES) for _ in range(6)]
        m0_stats, m0_root = sem("mix0_stats"), sem("mix0_root")
        mix0_end = c.at
        assert c.at <= NORM_AT

        msg = [Messages(0, xn_table), Messages(1, xn_table)]

        prjg = Project(None, 0, staged=False)
        c = Carver()
        c.at = mix0_end
        w_gnn0 = as3(c(128, 2 * D), D)
        prjg.w = w_gnn0
        gnn_rows = as3(c(P, 5 * D), D)
        assert c.at <= NORM_AT
        c.at = prjg.end
        AG0_BUFFERS = 4
        ag0 = c(P, AG0_BUFFERS * TABLES[0] * D).rearrange("p (u k d) -> p u k d", u=AG0_BUFFERS, k=TABLES[0])
        NG = TILES * HEADS
        g_st = c(P, NG * 6)
        g_a, g_b, g_q, g_mean, g_var, g_rs = [c(P, NG) for _ in range(6)]
        g_half = c(P, NG)
        assert c.at <= mix0_end
        DVE_TILES = 17
        gnn0_loaded = sem("gnn0_loaded")
        agg0_loaded = [sem(f"agg0_loaded{u}") for u in range(AG0_BUFFERS)]
        gvar, grstd, gparts = sem("gnn0_var"), sem("gnn0_rstd"), sem("gnn0_parts")

        def gnn0_norm(e, which, lo, hi, heads):
            w = D // heads
            y = rows[:, lo * D:hi * D]
            mean, rs = (over(z[:, lo * heads:hi * heads], w) for z in (g_mean, g_rs))
            g, b = (gnn_rows[:, i:i + 1, :].broadcast_to([P, hi - lo, D]) for i in (2 * which - 1, 2 * which))
            e.wait_ge(grstd, which)
            e.tensor_tensor(as3(y, w), as3(y, w), mean, ALU.subtract)
            e.drain()
            e.tensor_tensor(as3(y, w), as3(y, w), rs, ALU.mult)
            e.drain()
            e.tensor_tensor(as3(y, D), as3(y, D), g, ALU.mult)
            e.drain()
            e.tensor_tensor(as3(y, D), as3(y, D), b, ALU.add)
            e.drain()

        c = Carver()
        w_e = c(128, 2 * 3 * 2 * D).rearrange("p (u w c d) -> p u w c d", u=2, w=3, c=2)
        bnp = c(128, 10 * 16).rearrange("p (a b) -> p a b", b=16)
        bns = as3(c(128, 4 * 16), 16)
        w_r = as3(c(128, 2 * MOE), MOE)
        br_row = c(P, MOE)
        bo_rows = as3(c(P, MOE * D), D)
        gate = c(P, TILES * MOE)
        gate_sum = c(P, TILES)
        ltg = c(128, 10 * P).rearrange("p (u c n) -> p u c n", u=5, c=2)
        assert c.at <= NORM_AT
        h1 = as3(c(128, 2 * CHUNK), CHUNK)
        h2 = as3(c(128, 2 * CHUNK), CHUNK)
        ffn0_loaded = sem("ffn0_loaded")
        gsem = {x: sem(f"gate_{x}") for x in ("logits", "shifted", "exp")}
        bn_var, bn_rstd, bn_ready = sem("bn_var"), sem("bn_rstd"), sem("bn_ready")
        we_loaded = [sem(f"expert_loaded{u}") for u in range(2)]
        we_used, unit_done, unit_out, y_done, y_out = (sem(f"moe_{n}") for n in (
            "weights_used", "unit_done", "unit_out", "y_done", "y_out"))

        RD = REL * D
        RW = REL * (D + 1)
        QW = 3 * D
        c = Carver()
        xnT_flat = xnT[:, :, :].rearrange("p c n -> p (c n)")
        c.at = ARENA - 2 * 2 * QW
        w_rq = [as3(xnT_flat[:, r * 2 * QW:(r + 1) * 2 * QW] if r < 4 else c(128, 2 * QW), QW) for r in range(REL)]
        c.at = 0
        BR = REL * 6
        b_all = edge_cols[0:BIAS_ROWS, 0:QW]
        b_parts = edge_cols[0:BIAS_ROWS, QW:QW + QW // 2].bitcast(BF16)
        b_part = edge_cols[0:BIAS_ROWS, 3 * QW // 2:2 * QW].bitcast(BF16)
        countT = edge_cols[0:BIAS_ROWS, 2 * QW:2 * QW + REL * P].bitcast(BF16).rearrange("p (u r n) -> p u r n", u=2, r=REL)
        masks = edge_cols[0:BIAS_ROWS, 2 * QW + REL * P:2 * QW + REL * P + REL + 3]
        row_mask, part_mask = masks[:, 0:REL], masks[:, REL:REL + 3]
        at = c.at
        c.at = JOBS_AT
        w_relT = as3(c(128, 2 * RD), RD)
        w_in = as3(c(128, 2 * QW), QW)
        b_relT = as3(c(128, 2 * BR), BR)
        c.at = at
        ag1 = c(P, 2 * RW).rearrange("p (k r d) -> p k r d", k=2, d=D + 1)
        rel_counts = c(P, REL)
        counts_hi = c(P, REL // 2).bitcast(BF16)
        count_parts = c(P, BIAS_ROWS)
        aT = c(128, 2 * 12 * P).rearrange("p (u c n) -> p u c n", u=2, c=12)
        QK = c(P, 2 * REL * 2 * D).rearrange("p (u r d) -> p u r d", u=2, d=2 * D)
        V = c(P, 2 * RD).rearrange("p (u r d) -> p u r d", u=2, d=D)
        prod = c(P, RD)
        pprod = as3(c(P, 2 * RD), RD)
        scores = c(P, REL * REL * HEADS)
        sc24 = c(P, REL * HEADS)
        pbar = c(P, REL * HEADS)
        assert c.at <= ARENA - 2 * 2 * QW
        POOL_RELS = (2, 3, 4, 5)
        rel_agg_loaded = sem("rel_agg_loaded")
        asem = {x: sem(f"relatt_{x}") for x in ("w", "b", "fold", "fold_out", "summed", "turned", "moved",
                                                "qkv", "qkv_out", "attended", "pool_prod", "pool_prod_used", "shifted", "exp")}

        c = Carver()
        c.at = JOBS_AT
        w_qkv1 = as3(c(128, 2 * 768), 768)
        bias1 = c(P, 768)
        w_out1 = as3(c(128, 2 * D), D)
        b_o1 = c(P, D)
        att1 = Attend(c.at, 1.0, w_qkv1, bias1, w_out1)
        prj3 = Project(att1.m, att1.end)
        mlp_weights_at = att1.lt_at
        c.at = prj3.end
        w_x = as3(c(128, 2 * D), D)
        b_x = c(128, 2)
        blk = c(128, 3 * 128)
        p3_tmp = as3(c(P, 2 * D), D)
        mlp_hidden_at = c.at
        attended1 = sem("attended1")
        mix1_loaded, blk_cleared, blk_loaded, fold_mm, fold_out, bias_mm = (sem(f"mix1_{n}") for n in (
            "loaded", "blk_cleared", "blk_loaded", "fold_mm", "fold_out", "bias_mm"))

        prj1 = Project(None, NORM_AT - 5000)
        prj2 = Project(None, prj1.end)
        c = Carver()
        c.at = prj2.end
        w_ao = as3(c(128, 2 * D), D)
        w_pr = as3(c(128, 2 * D), D)
        prj1.w, prj2.w = w_ao, w_pr
        b_ao = c(P, D)
        b_pr = c(P, D)
        prj_tmp = as3(c(P, 2 * D), D)
        prj_loaded = sem("prj_loaded")

        c = Carver()
        c.at = mlp_weights_at
        w_m1 = as3(c(128, 2 * HID), HID)
        w_m2 = as3(c(128, 8 * D), D)
        b_m1 = c(128, 8)
        b_m2 = c(P, D)
        assert c.at <= att1.m_at
        c.at = mlp_hidden_at
        m_h = as3(c(128, 8 * CHUNK), CHUNK)
        m_o = p3_tmp
        assert c.at <= NORM_AT
        mlp_loaded, mlp_ended, m1_mm, m1_out, m2_mm, m2_out = (sem(f"mlp_{n}") for n in ("loaded", "ended", "m1_mm", "m1_out", "m2_mm", "m2_out"))

        c = Carver()
        w_1 = as3(c(128, 2 * EXP * EH), EXP * EH)
        w_2 = as3(c(128, 16 * D), D)
        b_1 = c(128, 16)
        w_ro = as3(c(128, 2 * EXP), EXP)
        b_ro = c(P, EXP)
        b_2 = c(EXP, D)
        assert c.at <= NORM_AT - 5000
        e_col = c(128, 16)
        e_col_i = c(128, 16, I32)
        iota32 = c(P, EXP)
        iota32_i = c(P, EXP, I32)
        ro_l, ro_c = [c(P, TILES * EXP) for _ in range(2)]
        ro_m, ro_f = [c(P, TILES) for _ in range(2)]
        e_number, e_number_i = c(EXP, 1), c(EXP, 1, I32)
        ones_ro = c(P, 128)
        lt_ro = c(128, 10 * P).rearrange("p (u c n) -> p u c n", u=5, c=2)
        assert c.at <= NORM_AT
        e_h = as3(c(128, 16 * CHUNK), CHUNK)
        ffn1_loaded = sem("ffn1_loaded")
        rsem = {x: sem(f"route_{x}") for x in ("consts", "logits", "diagonal", "spread", "numbers")}
        RO_BANK = 15
        ro_diag = rows[:, NODES:2 * NODES]
        RO_PIECES = [(at, min(512, NODES - at)) for at in range(0, NODES, 512)]
        x_mm, x_relu, x_masked, x_y, x_yout = (sem(f"moe1_{n}") for n in ("unit", "relu", "masked", "y", "y_out"))
        e_hot = c(EXP, CHUNK)
        idxT = xn_whole[:, 0:NODES]
        ohT = rows[0:EXP, 0:NODES]

        PRJ0_AT = CHUNKS + TILES // 2
        NORM0_AT = PRJ0_AT + TILES // 4
        assert NORM0_AT + TILES // 2 < TURNS
        ATT1_AT = TILES // EB
        PRJ3_AT = ATT1_AT + CHUNKS + TILES // 2
        LN4_AT = PRJ3_AT + TILES // 4
        MLP_AT = LN4_AT + TILES // EB
        MLP_TURNS = 3
        MLP_END = MLP_AT + MLP_TURNS * CHUNKS
        FOLD_AT = MLP_END + 1
        FOLD_TURNS = 2 * 2 * REL // EB
        assert FOLD_AT + FOLD_TURNS < TURNS
        MLP_OUTPUT = {9: 0, 12: 1, 17: 2, 19: 3, 21: 4}
        MLP_PLAN = [(n, (n,) if n < 16 else (), MLP_OUTPUT.get(n)) for n in range(MLP_TURNS * EB)]

        block = ctx.enter_context(nc.Block())

        @block.sync
        def _(sp):
            sp.dma_start(as3(x_cur[:, :], D), A["x"].rearrange("(t p) d -> p t d", p=P)).then_inc(x_loaded, 16)
            for r, n in enumerate(("src", "dst", "edge_type_6")):
                sp.dma_start(as3(raw_i[r], P), A[n].rearrange("(a q j) -> q a j", q=EROWS, j=P)).then_inc(edge_loaded, 16)
            sp.dma_start(as3(raw_w, P), A["edge_weight"].rearrange("(a q j) -> q a j", q=EROWS, j=P)).then_inc(edge_loaded, 16)
            sp.wait_ge(edge_ready, 1)
            for la, k in enumerate((src_f, key1_f)):
                sp.dma_start(key_row[la].rearrange("(a q j) -> q a j", q=EROWS, j=P), as3(k, P)).then_inc(rows_written, 16)
            sp.dma_start(w_qkv0[:, :, :], cm(A["L0_mix_Wqkv"])).then_inc(mix0_loaded, 16)
            sp.dma_start(w_out0[:, :, :], cm(A["L0_mix_Wout"])).then_inc(mix0_loaded, 16)
            sp.dma_start(gamma0, row_of(A["L0_mix_gamma"], D, P)).then_inc(mix0_loaded, 16)
            sp.dma_start(w_gnn0[:, :, :], cm(A["gnn0_W"])).then_inc(gnn0_loaded, 16)
            for i, n in enumerate(("L0_gnn_bias", "L0_gnn_ln1_g", "L0_gnn_ln1_b", "L0_gnn_ln2_g", "L0_gnn_ln2_b")):
                sp.dma_start(gnn_rows[:, i, :], row_of(A[n], D, P)).then_inc(gnn0_loaded, 16)
            sp.wait_ge(rows_written, 32)
            sp.wait_ge(mix0_loaded, 48)
            sp.wait_ge(gnn0_loaded, 96)
            phase_end(sp, 1)
            sp.dma_start(xn_table.rearrange("(t p) d -> p t d", p=P), as3(xn[:, :], D)).then_inc(table_written, 16)
            for h in range(2):
                msg[0].sync_load(sp, 0, h)
            msg[0].sync_turns(sp, 1, TURNS)
            sp.wait_ge(table_written, 16)
            phase_end(sp, 2)

            def load_agg(t, u, k):
                sp.wait_ge(prjg.turned.sem, prjg.turned.base + t + 3 - AG0_BUFFERS)
                for tb in range(TABLES[0]):
                    sp.dma_start(ag0[:, u, tb, :], agg[0][tb][bass.ds(t * P, P), :]).then_inc(agg0_loaded[u], 16)
            assert prjg.turned.base >= AG0_BUFFERS
            tiles(sp, load_agg, AG0_BUFFERS)
            phase_end(sp, 3)
            for i, n in enumerate(("L0_ffn_b1", "L0_ffn_g1", "L0_ffn_be1", "L0_ffn_m1", "L0_ffn_v1",
                                   "L0_ffn_b2", "L0_ffn_g2", "L0_ffn_be2", "L0_ffn_m2", "L0_ffn_v2")):
                sp.dma_start(bnp[:, i, :], A[n]).then_inc(ffn0_loaded, 16)
            sp.dma_start(w_r[:, :, :], cm(A["L0_ffn_Wr"])).then_inc(ffn0_loaded, 16)
            sp.dma_start(br_row, row_of(A["L0_ffn_br"], MOE, P)).then_inc(ffn0_loaded, 16)
            sp.dma_start(bo_rows.rearrange("p e d -> p (e d)"), row_of(A["L0_ffn_bo"], MOE * D, P)).then_inc(ffn0_loaded, 16)
            sp.wait_ge(ffn0_loaded, 13 * 16)
            phase_end(sp, 4)
            with sp.Fori(0, MOE // 2) as k:
                for u in range(2):
                    sp.wait_ge(we_used, 2 * k + u + 1)
                    for i, n in enumerate(("L0_ffn_W1", "L0_ffn_W2", "L0_ffn_Wo")):
                        sp.dma_start(w_e[:, u, i, :, :], A[n][bass.ds((2 * k + u) * D, D), :]
                                     .rearrange("(c p) n -> p c n", p=128)).then_inc(we_loaded[u], 16)
            phase_end(sp, 5)
            sp.dma_start(ln[3].gcol, A["mix1_ln1_w"]).then_inc(mix1_loaded, 16)
            sp.dma_start(ln[3].bcol, A["mix1_ln1_b"]).then_inc(mix1_loaded, 16)
            sp.dma_start(ln[4].gcol, A["mix1_ln2_w"]).then_inc(mix1_loaded, 16)
            sp.dma_start(ln[4].bcol, A["mix1_ln2_b"]).then_inc(mix1_loaded, 16)
            sp.dma_start(w_x[:, :, :], cm(A["L1_mix_Wx"])).then_inc(mix1_loaded, 16)
            sp.dma_start(b_x, A["mix1_bx"]).then_inc(mix1_loaded, 16)
            sp.dma_start(w_out1[:, :, :], cm(A["mix1_Wo_T"])).then_inc(mix1_loaded, 16)
            sp.dma_start(b_o1, row_of(A["L1_mix_bo"], D, P)).then_inc(mix1_loaded, 16)
            sp.wait_ge(blk_cleared, 1)
            for i, n in enumerate(("mix1_Wq_T", "mix1_Wk_T", "mix1_Wv_T")):
                for h in range(4):
                    sp.dma_start(blk[h * MHD:(h + 1) * MHD, i * 128 + h * MHD:i * 128 + (h + 1) * MHD],
                                 A[n]).then_inc(blk_loaded, 16)
            sp.wait_ge(mix1_loaded, 128)
            sp.wait_ge(blk_loaded, 16 * 12)
            sp.wait_ge(ln[3].stats_ready.sem, ln[3].stats_ready.base + 1)
            sp.dma_start(xn_table.rearrange("(t p) d -> p t d", p=P), as3(xn[:, :], D)).then_inc(table_written, 16)
            phase_end(sp, 6)
            for h in range(2):
                msg[1].sync_load(sp, 0, h)
            msg[1].sync_turns(sp, 1, PRJ3_AT + 1)
            sp.wait_ge(attended1, 1)
            sp.dma_start(w_m1[:, :, :], cm(A["mix1_W1_T"])).then_inc(mlp_loaded, 16)
            sp.dma_start(w_m2[:, :, :], A["mix1_W2_T"].rearrange("(c p) n -> p c n", p=128)).then_inc(mlp_loaded, 16)
            sp.dma_start(b_m1, A["mix1_b1"]).then_inc(mlp_loaded, 16)
            sp.dma_start(b_m2, row_of(A["L1_mix_b2"], D, P)).then_inc(mlp_loaded, 16)
            msg[1].sync_turns(sp, PRJ3_AT + 1, MLP_END + 1)
            sp.wait_ge(mlp_ended, 1)
            sp.dma_start(w_relT[:, :, :], cm(A["gnn1_W_T"])).then_inc(asem["w"], 16)
            sp.dma_start(w_in[:, :, :], cm(A["gnn1_in_T"])).then_inc(asem["w"], 16)
            sp.dma_start(b_relT[:, :, :], cm(A["gnn1_b_T"])).then_inc(asem["w"], 16)
            msg[1].sync_turns(sp, MLP_END + 1, TURNS)
            phase_end(sp, 7)
            sp.dma_start(b_all[BR:BIAS_ROWS, :], row_of(A["L1_gnn_in_proj_b"], QW, 6)).then_inc(asem["b"], 16)
            sp.dma_start(masks, A["rel_masks"]).then_inc(asem["b"], 16)
            phase_end(sp, 8)

            def load_rel(t, u, k):
                sp.wait_ge(asem["turned"], t + 1)
                for tb in range(TABLES[1]):
                    sp.dma_start(ag1[:, tb, :, :], agg[1][tb][0:REL * NODES, :]
                                 .rearrange("(r n) d -> n r d", r=REL)[bass.ds(t * P, P), :, :]
                                 ).then_inc(rel_agg_loaded, 16)
            tiles(sp, load_rel)
            phase_end(sp, 9)
            sp.dma_start(w_ao[:, :, :], cm(A["gnn1_ao_T"])).then_inc(prj_loaded, 16)
            sp.dma_start(w_pr[:, :, :], cm(A["gnn1_pr_T"])).then_inc(prj_loaded, 16)
            sp.dma_start(b_ao, row_of(A["L1_gnn_attn_out_b"], D, P)).then_inc(prj_loaded, 16)
            sp.dma_start(b_pr, row_of(A["L1_gnn_proj_b"], D, P)).then_inc(prj_loaded, 16)
            sp.wait_ge(prj_loaded, 64)
            for d_, n in ((w_1, cm(A["ffn1_W1"])), (w_2, A["ffn1_W2"].rearrange("(c p) n -> p c n", p=128)), (w_ro, cm(A["ffn1_router_T"]))):
                sp.dma_start(d_[:, :, :], n).then_inc(ffn1_loaded, 16)
            sp.dma_start(b_1, A["ffn1_b1"]).then_inc(ffn1_loaded, 16)
            sp.dma_start(b_ro, row_of(A["L1_ffn_router_b"], EXP, P)).then_inc(ffn1_loaded, 16)
            sp.dma_start(b_2, A["L1_ffn_b2"]).then_inc(ffn1_loaded, 16)
            phase_end(sp, 10)
            phase_end(sp, 11)
            sp.wait_ge(ffn1_loaded, 96)
            phase_end(sp, 12)
            for c_ in range(CHUNKS):
                sp.wait_ge(x_yout, 5 + TPC * (c_ + 1))
                sp.dma_start(out[c_ * CHUNK:(c_ + 1) * CHUNK, :].rearrange("(t p) d -> p t d", p=P),
                             as3(x_cur[:, c_ * TPC * D:(c_ + 1) * TPC * D], D)).then_inc(out_written, 16)
            phase_end(sp, 13)
            sp.wait_ge(out_written, 16 * CHUNKS)

        @block.gpsimd
        def _(pool):
            pool.memset(ones_c, 1.0)
            pool.memset(neghalf[:, :], -0.5)
            pool.memset(zeros[:, :], 0.0)
            pool.iota(lane_i[:, :], [[0, 1]], base=0, channel_multiplier=1)
            pool.drain()
            pool.affine_select(out=ident[:, :], in_=ones_c, compare_op=ALU.is_equal, fill=0.0, base=0,
                               pattern=[[-1, 128]], channel_multiplier=1)
            pool.affine_select(out=earlier[:, :], in_=ones_c[0:P, 0:P], compare_op=ALU.is_gt, fill=0.0, base=0,
                               pattern=[[-1, P]], channel_multiplier=1)
            pool.tensor_copy(lane[:, :], lane_i[:, :])
            pool.drain().then_inc(consts_ready, 1)
            msg[0].clear(pool, (0,))
            ln[0].gpsimd(pool)
            msg[0].clear(pool, (1,))
            phase_end(pool, 1)
            msg[0].gpsimd_start(pool)
            weave(pool, msg[0].gpsimd_step, 0, NORM0_AT, {})
            pool.wait_ge(m0_stats, 1)
            pool.tensor_tensor(m0_rstd, m0_var, neghalf[0:P, 0:TILES], ALU.pow).then_inc(m0_root, 1)
            weave(pool, msg[0].gpsimd_step, NORM0_AT, TURNS - 1 - NORM0_AT, {})
            msg[0].gpsimd_end(pool)
            phase_end(pool, 2)
            pool.memset(g_half, -0.5)
            pool.drain()
            pool.wait_ge(gvar, 1)
            pool.tensor_tensor(g_rs, g_var, g_half, ALU.pow).then_inc(grstd, 1)
            gnn0_norm(pool, 1, DVE_TILES, TILES, HEADS)
            pool.drain().then_inc(gparts, 1)
            pool.wait_ge(gvar, 2)
            pool.tensor_tensor(g_rs[:, 0:TILES], g_var[:, 0:TILES], g_half[:, 0:TILES], ALU.pow).then_inc(grstd, 1)
            gnn0_norm(pool, 2, DVE_TILES, TILES, 1)
            own_x, own_y = x_cur[:, DVE_TILES * D:], rows[:, DVE_TILES * D:]
            pool.tensor_tensor(own_x, own_x, own_y, ALU.add)
            phase_end(pool, 3)
            ln[1].gpsimd(pool)
            pool.wait_ge(bn_var, 1)
            for i in (0, 2):
                pool.tensor_tensor(bns[:, i, :], bns[:, i, :], neghalf[:, 0:16], ALU.pow)
            pool.drain().then_inc(bn_rstd, 1)
            phase_end(pool, 4)
            msg[1].clear(pool, (0, 1))
            phase_end(pool, 5)
            pool.memset(blk, 0.0)
            pool.drain().then_inc(blk_cleared, 1)
            ln[2].gpsimd(pool)
            ln[3].gpsimd(pool)
            phase_end(pool, 6)
            msg[1].gpsimd_start(pool)
            weave(pool, msg[1].gpsimd_step, 0, LN4_AT, {})
            ln[4].gpsimd(pool)
            weave(pool, msg[1].gpsimd_step, LN4_AT, TURNS - 1 - LN4_AT, {})
            msg[1].gpsimd_end(pool)
            phase_end(pool, 7)
            phase_end(pool, 8)
            pool.memset(count_parts[:, BR:BR + 3], 1.0)
            pool.memset(count_parts[:, BR + 3:], 0.0)

            def rel_sum(t):
                pool.wait_ge(rel_agg_loaded, 32 * (t + 1))
                pool.tensor_tensor(rel_counts.unsqueeze(2), ag1[:, 0, :, D:D + 1], ag1[:, 1, :, D:D + 1], ALU.add)
                pool.tensor_tensor(ag1[:, 0, :, 0:D], ag1[:, 0, :, 0:D], ag1[:, 1, :, 0:D], ALU.add)
                pool.drain()
                pool.tensor_copy(counts_hi, rel_counts)
                pool.drain()
                hi = counts_hi.unsqueeze(1).broadcast_to([P, 3, REL])
                pool.tensor_copy(as3(count_parts[:, 0:BR // 2], REL), hi)
                pool.tensor_tensor(as3(count_parts[:, BR // 2:BR], REL), rel_counts.unsqueeze(1).broadcast_to([P, 3, REL]), hi,
                                   ALU.subtract)
                pool.drain().then_inc(asem["summed"], 1)

            def rel_prod(t, u, some):
                pool.wait_ge(asem["qkv_out"], REL * (t + 3))
                for i in some:
                    r = POOL_RELS[i]
                    pool.wait_ge(asem["pool_prod_used"], len(POOL_RELS) * t + i + 1)
                    pool.tensor_tensor(as3(pprod[:, i % 2, :], D), QK[:, u, r:r + 1, 0:D].broadcast_to([P, REL, D]),
                                       QK[:, u, :, D:2 * D], ALU.mult).then_inc(asem["pool_prod"], 1)
            rel_sum(0)
            rel_sum(1)
            with pool.Fori(0, TILES // 2 - 1) as k:
                for u in range(2):
                    rel_prod(2 * k + u, u, (0, 1))
                    rel_sum(2 * k + u + 2)
                    rel_prod(2 * k + u, u, (2, 3))
            rel_prod(TILES - 3, 0, (0, 1))
            rel_sum(TILES - 1)
            rel_prod(TILES - 3, 0, (2, 3))
            for t in range(TILES - 2, TILES):
                rel_prod(t, t % 2, range(4))
            phase_end(pool, 9)
            prj1.gpsimd(pool, rows[:, :])
            phase_end(pool, 10)
            prj2.gpsimd(pool, rows[:, :])
            phase_end(pool, 11)
            ln[5].gpsimd(pool)
            pool.iota(e_col_i, [[2, 16]], base=0, channel_multiplier=0)
            pool.iota(iota32_i, [[1, EXP]], base=0, channel_multiplier=0)
            pool.iota(e_number_i, [[0, 1]], base=0, channel_multiplier=1)
            pool.memset(ones_ro, 1.0)
            pool.drain().then_inc(rsem["consts"], 1)
            phase_end(pool, 12)
            phase_end(pool, 13)

        @block.scalar
        def _(act):
            act.preload_act_table(ACT.Exp)
            ln[0].scalar(act)
            phase_end(act, 1)
            msg[0].scalar_start(act)
            att0.woven_scalar(act, msg[0].scalar_step, 0)
            job_end(act, 1)
            prj0.woven_scalar(act, msg[0].scalar_step, PRJ0_AT)
            weave(act, msg[0].scalar_step, NORM0_AT, TURNS - NORM0_AT, {})
            phase_end(act, 2)
            prjg.scalar(act)
            phase_end(act, 3)
            ln[1].scalar_for_product(act, ltg, gsem["logits"])
            act.wait_ge(gsem["shifted"], 1)
            act.activation(gate, gate, ACT.Exp).then_inc(gsem["exp"], 1)
            phase_end(act, 4)
            act.sem_inc(unit_out, 8)
            with act.Fori(0, MOE // 2) as k:
                for u in range(2):
                    with act.Fori(0, CHUNKS) as c_:
                        ex = 2 * k + u
                        g = ex * CHUNKS + c_
                        for layer in range(2):
                            dst = (h1, h2)[layer]
                            for j in range(4):
                                h, oc = j // 2, j % 2
                                off, n = HALVES[h]
                                act.wait_ge(unit_done, g * 8 + 4 * layer + j + 1)
                                own(act, "act")
                                act.activation(dst[:, oc, off:off + n], ps[j][:, 0:n], ACT.Relu,
                                               scale=bns[:, 2 * layer, bass.ds(ex * 2 + oc, 1)],
                                               bias=bns[:, 2 * layer + 1, bass.ds(ex * 2 + oc, 1)]).then_inc(unit_out, 1)
            phase_end(act, 5)
            phase_end(act, 6)
            step = msg[1].scalar_step
            msg[1].scalar_start(act)
            ln[3].woven_scalar(act, step, 0)
            job_end(act, 2)
            att1.woven_scalar(act, step, ATT1_AT)
            job_end(act, 3)
            prj3.woven_scalar(act, step, PRJ3_AT)
            job_end(act, 4)
            ln[4].woven_scalar(act, step, LN4_AT)
            act.preload_act_table(ACT.Gelu)
            job_end(act, 5)
            act.wait_ge(mlp_loaded, 64)
            act.sem_inc(m1_out, 4)

            def gelu(c_, j):
                h, oc = j // 8, j % 8
                off, n = HALVES[h]
                act.wait_ge(m1_mm, c_ * 16 + j + 1)
                act.activation(m_h[:, oc, off:off + n], ps[j % 4][:, 0:n], ACT.Gelu,
                               bias=b_m1[:, oc:oc + 1]).then_inc(m1_out, 1)
            with act.Fori(0, CHUNKS) as c_:
                for at, units, _ in MLP_PLAN:
                    step(act, MLP_AT + MLP_TURNS * c_ + at // EB, at % EB)
                    for j in units:
                        gelu(c_, j)
            job_end(act, 6)
            weave(act, step, MLP_END, 1, {})
            act.sem_inc(asem["fold_out"], 2)
            for n in range(FOLD_TURNS * EB):
                step(act, FOLD_AT + n // EB, n % EB)
                if n % 2:
                    continue
                i = n // 2
                r, ic = i // 2, i % 2
                act.wait_ge(asem["fold"], i + 1)
                act.activation(w_rq[r][:, ic, 0:512], ps[2 * (i % 2)][:, :], ACT.Copy)
                act.activation(w_rq[r][:, ic, 512:QW], ps[2 * (i % 2) + 1][:, 0:D], ACT.Copy).then_inc(asem["fold_out"], 1)
            weave(act, step, FOLD_AT + FOLD_TURNS, TURNS - FOLD_AT - FOLD_TURNS, {})
            act.preload_act_table(ACT.Exp)
            phase_end(act, 7)
            act.wait_ge(asem["fold"], 2 * REL + 1)
            act.activation(b_all[0:BR, 0:512], ps[4][0:BR, :], ACT.Copy)
            act.activation(b_all[0:BR, 512:QW], ps[5][0:BR, 0:D], ACT.Copy)
            act.drain().then_inc(asem["fold_out"], 1)
            phase_end(act, 8)
            act.sem_inc(asem["qkv_out"], 2 * REL)
            act.sem_inc(asem["moved"], 1)

            def rel_move(t, u):
                act.wait_ge(asem["turned"], t + 2)
                for b in range(3):
                    act.activation(aT[:, u, 4 * b:4 * b + 4, :], as3(ps[b][:, 0:4 * P], P), ACT.Copy)
                for r in range(REL):
                    act.activation(countT[:, u, r, :], ps[7][0:BIAS_ROWS, 0:P], ACT.Copy, scale=row_mask[:, r:r + 1])
                act.drain().then_inc(asem["moved"], 1)

            def rel_out(t, u, rs):
                act.wait_ge(asem["attended"], t + 1)
                for r in rs:
                    b = 3 + 2 * (r % 2)
                    act.wait_ge(asem["qkv"], REL * t + r + 1)
                    act.activation(QK[:, u, r, :], ps[b][0:P, :], ACT.Copy)
                    act.activation(V[:, u, r, :], ps[b + 1][0:P, 0:D], ACT.Copy).then_inc(asem["qkv_out"], 1)

            def rel_exp(t):
                act.wait_ge(asem["shifted"], t + 1)
                act.activation(scores, scores, ACT.Exp, scale=HD ** -0.5).then_inc(asem["exp"], 1)

            def rel_step(t, u, first=False):
                rel_out(t, u, range(0, 3))
                rel_move(t + 1, 1 - u)
                rel_out(t, u, range(3, 4))
                if not first:
                    rel_exp(t - 1)
                rel_out(t, u, range(4, REL))
            rel_move(0, 0)
            rel_step(0, 0, first=True)
            with act.Fori(0, TILES // 2 - 1) as k:
                rel_step(2 * k + 1, 1)
                rel_step(2 * k + 2, 0)
            rel_step(TILES - 2, 1)
            rel_out(TILES - 1, 0, range(0, 4))
            rel_exp(TILES - 2)
            rel_out(TILES - 1, 0, range(4, REL))
            rel_exp(TILES - 1)
            phase_end(act, 9)
            prj1.scalar(act)
            phase_end(act, 10)
            prj2.scalar(act)
            phase_end(act, 11)
            ln[5].scalar_for_product(act, lt_ro, rsem["logits"])
            for i, (at, n) in enumerate(RO_PIECES):
                act.wait_ge(rsem["spread"], i + 1)
                act.activation(idxT[:, at:at + n], ps[i][:, 0:n], ACT.Copy)
            act.drain().then_inc(rsem["numbers"], 1)
            phase_end(act, 12)
            act.sem_inc(x_relu, 4)
            with act.Fori(0, CHUNKS) as c_:
                for j in range(32):
                    h, pc = j // 16, j % 16
                    off, n = HALVES[h]
                    act.wait_ge(x_mm, c_ * 32 + j + 1)
                    act.activation(e_h[:, pc, off:off + n], ps[j % 4][:, 0:n], ACT.Relu,
                                   bias=b_1[:, pc:pc + 1]).then_inc(x_relu, 1)
            phase_end(act, 13)

        @block.tensor
        def _(pe):
            pe.wait_ge(edge_ready, 1)
            pe.wait_ge(consts_ready, 1)
            for i, a in enumerate((src_f, dst_f, key1_f, raw_w)):
                for b in range(EBLK):
                    mm = pe.transpose(ps[i][0:P, b * EROWS:(b + 1) * EROWS], as3(a, P)[:, b, :], ident[0:EROWS, 0:EROWS])
            mm.then_inc(edge_turned, 1)
            ln[0].tensor(pe)
            phase_end(pe, 1)
            msg[0].tensor_start(pe)
            att0.woven_tensor(pe, msg[0].tensor_step, 0)
            job_end(pe, 1)
            prj0.woven_tensor(pe, msg[0].tensor_step, PRJ0_AT)
            weave(pe, msg[0].tensor_step, NORM0_AT, TURNS - NORM0_AT, {})
            phase_end(pe, 2)

            def turn_tables(t, u, k):
                pe.wait_ge(agg0_loaded[u], 16 * TABLES[0] * (k + 1))
                pe.wait_ge(prjg.moved.sem, prjg.moved.base + t + 1)
                for c_ in range(2):
                    for tb in range(TABLES[0]):
                        mm = pe.matmul(ps[u % 2][:, c_ * P:(c_ + 1) * P], ag0[:, u, tb, c_ * 128:(c_ + 1) * 128],
                                       ident[0:P, 0:P], start=(tb == 0), stop=(tb == TABLES[0] - 1), skip_group_check=True)
                mm.then_inc(prjg.turned.sem, 1)
            prjg.tensor(pe, turn_tables, AG0_BUFFERS)
            phase_end(pe, 3)
            pe.wait_ge(ffn0_loaded, 13 * 16)
            pe.sem_inc(gsem["logits"], 5)
            pe.sem_inc(ln[1].turned.sem, ln[1].nb)

            def logits(t, u):
                for c_ in range(2):
                    mm = pe.matmul(col(ps[5][0:P, :], t * MOE, MOE), ltg[:, u, c_, :], w_r[:, c_, :],
                                   start=(c_ == 0), stop=(c_ == 1), skip_group_check=True)
                mm.then_inc(gsem["logits"], 1)
            ln[1].tensor_with_product(pe, 0, TILES, logits)
            phase_end(pe, 4)
            pe.sem_inc(we_used, 2)
            with pe.Fori(0, MOE // 2) as k:
                for u in range(2):
                    pe.wait_ge(we_loaded[u], 48 * (k + 1))
                    own(pe, "pe")
                    with pe.Fori(0, CHUNKS) as c_:
                        g = (2 * k + u) * CHUNKS + c_
                        for layer in range(2):
                            for j in range(4):
                                h, oc = j // 2, j % 2
                                off, n = HALVES[h]
                                if layer == 0:
                                    pe.wait_ge(unit_out, 8 * g + j + 5)
                                else:
                                    pe.wait_ge(unit_out, 8 * g + 8 + (2 if j < 2 else 4))
                                for c2 in range(2):
                                    rhs = xnT[:, c2, bass.ds(c_ * CHUNK + off, n)] if layer == 0 else h1[:, c2, off:off + n]
                                    mm = pe.matmul(ps[j][:, 0:n], w_e[:, u, layer, c2, oc * 128:(oc + 1) * 128], rhs,
                                                   start=(c2 == 0), stop=(c2 == 1))
                                mm.then_inc(unit_done, 1)
                        for i in range(TPC):
                            pe.wait_ge(unit_out, 8 * g + 8 + (6 if (i + 1) * P <= HALVES[0][1] else 8))
                            pe.wait_ge(y_out, 5 * g + (5 if i == 0 else 6 if i == 4 else i + 1))
                            for c2 in range(2):
                                mm = pe.matmul(ps[4 + i % 4][0:P, 0:D], h2[:, c2, i * P:(i + 1) * P], w_e[:, u, 2, c2, :],
                                               start=(c2 == 0), stop=(c2 == 1))
                            mm.then_inc(y_done, 1)
                    pe.drain().then_inc(we_used, 1)
            phase_end(pe, 5)
            pe.wait_ge(mix1_loaded, 128)
            pe.wait_ge(blk_loaded, 16 * 12)
            for oc in range(2):
                for ic in range(2):
                    mm = pe.matmul(ps[2 * oc + ic][:, 0:384], w_x[:, oc, ic * 128:(ic + 1) * 128], blk,
                                   start=True, stop=True)
                mm = pe.matmul(ps[4 + oc][0:P, 0:384], b_x[:, oc:oc + 1].broadcast_to([128, P]), blk, start=True, stop=True)
            mm.then_inc(fold_mm, 1)
            phase_end(pe, 6)
            step = msg[1].tensor_step
            msg[1].tensor_start(pe)
            ln[3].woven_tensor(pe, step, 0)
            job_end(pe, 2)
            att1.woven_tensor(pe, step, ATT1_AT)
            job_end(pe, 3)
            pe.sem_inc(attended1, 1)
            prj3.woven_tensor(pe, step, PRJ3_AT)
            job_end(pe, 4)
            ln[4].woven_tensor(pe, step, LN4_AT)
            job_end(pe, 5)
            pe.wait_ge(mlp_loaded, 64)

            def hidden(c_, j):
                h, oc = j // 8, j % 8
                off, n = HALVES[h]
                pe.wait_ge(m1_out, c_ * 16 + j + 1)
                for c2 in range(2):
                    mm = pe.matmul(ps[j % 4][:, 0:n], w_m1[:, c2, oc * 128:(oc + 1) * 128],
                                   xnT[:, c2, bass.ds(c_ * CHUNK + off, n)], start=(c2 == 0), stop=(c2 == 1))
                mm.then_inc(m1_mm, 1)

            def output(c_, i):
                pe.wait_ge(m1_out, c_ * 16 + 4 + (8 if (i + 1) * P <= HALVES[0][1] else 16))
                pe.wait_ge(m2_out, 5 * c_ + (5 if i == 0 else i + 4))
                for c2 in range(8):
                    mm = pe.matmul(ps[6 + i % 2][0:P, 0:D], m_h[:, c2, i * P:(i + 1) * P], w_m2[:, c2, :],
                                   start=(c2 == 0), stop=(c2 == 7))
                mm.then_inc(m2_mm, 1)
            with pe.Fori(0, CHUNKS) as c_:
                for at, units, y in MLP_PLAN:
                    step(pe, MLP_AT + MLP_TURNS * c_ + at // EB, at % EB)
                    for j in units:
                        hidden(c_, j)
                    if y is not None:
                        output(c_, y)
            job_end(pe, 6)
            pe.sem_inc(mlp_ended, 1)
            weave(pe, step, MLP_END, 1, {})
            pe.wait_ge(asem["w"], 48)
            for n in range(FOLD_TURNS * EB):
                step(pe, FOLD_AT + n // EB, n % EB)
                if n % 2:
                    continue
                i = n // 2
                r, ic = i // 2, i % 2
                pe.wait_ge(asem["fold_out"], i + 1)
                for lo, hi, b in ((0, 512, 2 * (i % 2)), (512, QW, 2 * (i % 2) + 1)):
                    for oc in range(2):
                        mm = pe.matmul(ps[b][:, 0:hi - lo], w_relT[:, oc, r * D + ic * 128:r * D + (ic + 1) * 128],
                                       w_in[:, oc, lo:hi], start=(oc == 0), stop=(oc == 1))
                mm.then_inc(asem["fold"], 1)
            weave(pe, step, FOLD_AT + FOLD_TURNS, TURNS - FOLD_AT - FOLD_TURNS, {})
            phase_end(pe, 7)
            for lo, hi, b in ((0, 512, 4), (512, QW, 5)):
                for oc in range(2):
                    mm = pe.matmul(ps[b][0:BR, 0:hi - lo], b_relT[:, oc, :],
                                   w_in[:, oc, lo:hi], start=(oc == 0), stop=(oc == 1))
            mm.then_inc(asem["fold"], 1)
            phase_end(pe, 8)
            pe.sem_inc(asem["turned"], 1)

            def rel_turn(t):
                pe.wait_ge(asem["summed"], t + 1)
                pe.wait_ge(asem["moved"], t + 1)
                for r in range(REL):
                    for c_ in range(2):
                        i = 2 * r + c_
                        pe.transpose(ps[i // 4][:, (i % 4) * P:(i % 4 + 1) * P], ag1[:, 0, r, c_ * 128:(c_ + 1) * 128],
                                     ident[0:P, 0:P])
                pe.transpose(ps[7][0:BIAS_ROWS, 0:P], count_parts, ident[0:P, 0:P]).then_inc(asem["turned"], 1)

            def rel_qkv(t, u, rels):
                for r in rels:
                    pe.wait_ge(asem["moved"], t + 2)
                    pe.wait_ge(asem["qkv_out"], REL * t + r + REL + REL - 1)
                    b = 3 + 2 * (r % 2)
                    for lo, hi, bank in ((0, 512, b), (512, QW, b + 1)):
                        pe.matmul(ps[bank][0:P, 0:hi - lo], aT[:, u, 2 * r, :], w_rq[r][:, 0, lo:hi], start=True, stop=False)
                        pe.matmul(ps[bank][0:P, 0:hi - lo], aT[:, u, 2 * r + 1, :], w_rq[r][:, 1, lo:hi], start=False, stop=False)
                        mm = pe.matmul(ps[bank][0:P, 0:hi - lo], countT[:, u, r, :], b_parts[:, lo:hi], start=False, stop=True)
                    mm.then_inc(asem["qkv"], 1)

            def rel_tile(t, u):
                rel_qkv(t, u, range(0, 3))
                rel_turn(t + 1)
                rel_qkv(t, u, range(3, REL))
            rel_turn(0)
            with pe.Fori(0, TILES // 2) as k:
                for u in range(2):
                    rel_tile(2 * k + u, u)
            rel_qkv(TILES - 1, 0, range(REL))
            phase_end(pe, 9)
            prj1.tensor(pe)
            phase_end(pe, 10)
            prj2.tensor(pe)
            phase_end(pe, 11)
            pe.wait_ge(ffn1_loaded, 96)
            pe.sem_inc(rsem["logits"], 5)
            pe.sem_inc(ln[5].turned.sem, ln[5].nb)

            def ro_logits(bank, t, u):
                for c_ in range(2):
                    mm = pe.matmul(col(ps[5 + bank][0:P, :], (t - bank * RO_BANK) * EXP, EXP), lt_ro[:, u, c_, :], w_ro[:, c_, :],
                                   start=(c_ == 0), stop=(c_ == 1), skip_group_check=True)
                mm.then_inc(rsem["logits"], 1)
            for bank, first, last in ((0, 0, RO_BANK), (1, RO_BANK, TILES)):
                ln[5].tensor_with_product(pe, first, last, lambda t, u, bank=bank: ro_logits(bank, t, u))
            pe.wait_ge(rsem["diagonal"], 1)
            for i, (at, n) in enumerate(RO_PIECES):
                pe.matmul(ps[i][:, 0:n], ones_ro, ro_diag[:, at:at + n], start=True, stop=True).then_inc(rsem["spread"], 1)
            phase_end(pe, 12)
            with pe.Fori(0, CHUNKS) as c_:
                for j in range(32):
                    h, pc = j // 16, j % 16
                    off, n = HALVES[h]
                    pe.wait_ge(x_relu, c_ * 32 + j + 1)
                    for c2 in range(2):
                        mm = pe.matmul(ps[j % 4][:, 0:n], w_1[:, c2, pc * 128:(pc + 1) * 128],
                                       xnT[:, c2, bass.ds(c_ * CHUNK + off, n)], start=(c2 == 0), stop=(c2 == 1))
                    mm.then_inc(x_mm, 1)
                for i in range(TPC):
                    pe.wait_ge(x_masked, c_ * 32 + (16 if (i + 1) * P <= HALVES[0][1] else 32))
                    pe.wait_ge(x_yout, 5 * c_ + (5 if i == 0 else 6 if i == 4 else i + 1))
                    for c2 in range(16):
                        pe.matmul(ps[4 + i % 4][0:P, 0:D], e_h[:, c2, i * P:(i + 1) * P], w_2[:, c2, :],
                                  start=(c2 == 0), stop=False)
                    pe.matmul(ps[4 + i % 4][0:P, 0:D], e_hot[:, i * P:(i + 1) * P], b_2, start=False, stop=True
                              ).then_inc(x_y, 1)
            phase_end(pe, 13)

        @block.vector
        def _(v):
            v.wait_ge(x_loaded, 16)
            ln[0].stats(v)
            ln[0].moments(v)
            v.wait_ge(edge_loaded, 64)
            for a, b in ((src_f, raw_i[0]), (dst_f, raw_i[1]), (typ_f, raw_i[2])):
                v.tensor_copy(a, b)
            v.drain()
            v.scalar_tensor_tensor(out=key1_f, in0=typ_f, scalar=float(NODES), in1=dst_f, op0=ALU.mult, op1=ALU.add)
            v.drain().then_inc(edge_ready, 1)
            v.wait_ge(edge_turned, 1)
            v.tensor_copy(key_col[0][:, :], ps[0][0:P, 0:ETILES])
            v.tensor_copy(gather_col[0][:, :], ps[1][0:P, 0:ETILES])
            v.tensor_copy(key_col[1][:, :], ps[2][0:P, 0:ETILES])
            v.tensor_copy(gather_col[1][:, :], ps[0][0:P, 0:ETILES])
            v.tensor_copy(weight_col, ps[3][0:P, 0:ETILES])
            v.drain()
            for la in range(2):
                v.tensor_scalar(spare_gap[la][:, :], key_col[la][:, :], -1.0, float(SEGS[la]), ALU.mult, ALU.add)
            v.drain()
            for la in range(2):
                v.tensor_scalar(spare_gap[la][:, :], spare_gap[la][:, :], lane[0:P, 0:1], None, ALU.add)
            ln[0].vector_rows(v)
            phase_end(v, 1)
            step = msg[0].vector_step
            msg[0].vector_start(v)
            att0.woven_vector(v, step, 0)
            job_end(v, 1)

            def keep_mix0(t, u):
                v.wait_ge(prj0.product.sem, prj0.product.base + t + 3)
                own(v, "dve")
                v.bn_stats(out=col(m0_st, t * 6, 6), in_=prj0.out(u))
                v.tensor_copy(col(rows, t * D, D), prj0.out(u))
                v.drain().then_inc(prj0.used.sem, 1)
            prj0.woven_vector(v, step, PRJ0_AT, keep_mix0)
            v.drain()
            moments(v, as3(m0_st, 6), D // 2, m0_a, m0_b, m0_q, m0_mean, m0_var).then_inc(m0_stats, 1)
            v.wait_ge(m0_root, 1)

            def add_mix0(t):
                v.scalar_tensor_tensor(out=col(rows, t * D, D), in0=col(rows, t * D, D), scalar=col(m0_mean, t),
                                       in1=gamma0, op0=ALU.subtract, op1=ALU.mult)
                v.drain()
                v.scalar_tensor_tensor(out=col(x_cur, t * D, D), in0=col(rows, t * D, D), scalar=col(m0_rstd, t),
                                       in1=col(x_cur, t * D, D), op0=ALU.mult, op1=ALU.add)
            weave(v, step, NORM0_AT, TILES // 2, {0: [lambda k: add_mix0(2 * k)], 4: [lambda k: add_mix0(2 * k + 1)]})
            add_mix0(TILES - 1)
            weave(v, step, NORM0_AT + TILES // 2, TURNS - 1 - NORM0_AT - TILES // 2, {})
            msg[0].vector_end(v)
            phase_end(v, 2)
            v.sem_inc(prjg.used.sem, 2)

            def gnn0_rows(t, u, k):
                v.wait_ge(prjg.product.sem, prjg.product.base + t + 3)
                v.tensor_tensor(col(rows, t * D, D), prjg.out(u), gnn_rows[:, 0, :], ALU.add)
                v.drain().then_inc(prjg.used.sem, 1)
                for h in range(HEADS):
                    v.bn_stats(out=col(g_st, t * 24 + h * 6, 6), in_=col(rows, t * D + h * HD, HD))
            tiles(v, gnn0_rows)
            v.drain()
            moments(v, as3(g_st, 6), HD // 2, g_a, g_b, g_q, g_mean, g_var).then_inc(gvar, 1)
            gnn0_norm(v, 1, 0, DVE_TILES, HEADS)
            v.drain().then_inc(gparts, 1)
            v.wait_ge(gparts, 2)

            def row_stats(t, u, k):
                v.bn_stats(out=col(g_st, t * 6, 6), in_=col(rows, t * D, D))
            tiles(v, row_stats, 5)
            v.drain()
            moments(v, as3(g_st[:, 0:TILES * 6], 6), D // 2, *(z[:, 0:TILES] for z in (g_a, g_b, g_q, g_mean, g_var))
                    ).then_inc(gvar, 1)
            gnn0_norm(v, 2, 0, DVE_TILES, 1)
            own_x, own_y = x_cur[:, 0:DVE_TILES * D], rows[:, 0:DVE_TILES * D]
            v.tensor_tensor(own_x, own_x, own_y, ALU.add)
            phase_end(v, 3)
            ln[1].vector(v)
            v.wait_ge(ffn0_loaded, 13 * 16)
            for i in (0, 1):
                v.tensor_scalar(bns[:, 2 * i, :], bnp[:, 5 * i + 4, :], BN_EPS, None, ALU.add)
            v.drain().then_inc(bn_var, 1)
            v.wait_ge(bn_rstd, 1)
            for i in (0, 1):
                b_, g_, be_, m_, _ = (bnp[:, 5 * i + q, :] for q in range(5))
                v.tensor_tensor(bns[:, 2 * i, :], bns[:, 2 * i, :], g_, ALU.mult)
                v.tensor_tensor(bns[:, 2 * i + 1, :], b_, m_, ALU.subtract)
                v.drain()
                v.tensor_tensor(bns[:, 2 * i + 1, :], bns[:, 2 * i + 1, :], bns[:, 2 * i, :], ALU.mult)
                v.drain()
                v.tensor_tensor(bns[:, 2 * i + 1, :], bns[:, 2 * i + 1, :], be_, ALU.add)
            v.drain().then_inc(bn_ready, 1)
            v.wait_ge(gsem["logits"], TILES + 5)
            g3 = as3(gate, MOE)
            v.tensor_tensor(g3, as3(ps[5][0:P, 0:TILES * MOE], MOE), br_row.unsqueeze(1).broadcast_to([P, TILES, MOE]), ALU.add)
            v.drain()
            v.tensor_reduce(gate_sum, g3, AX.X, ALU.max)
            v.drain()
            v.tensor_tensor(g3, g3, over(gate_sum, MOE), ALU.subtract)
            v.drain().then_inc(gsem["shifted"], 1)
            v.wait_ge(gsem["exp"], 1)
            v.tensor_reduce(gate_sum, g3, AX.X, ALU.add)
            v.drain()
            v.reciprocal(gate_sum, gate_sum)
            v.drain()
            v.tensor_tensor(g3, g3, over(gate_sum, MOE), ALU.mult)
            phase_end(v, 4)
            v.sem_inc(y_out, 5)
            with v.Fori(0, MOE // 2) as k:
                for u in range(2):
                    with v.Fori(0, CHUNKS) as c_:
                        ex = 2 * k + u
                        for i in range(TPC):
                            t = c_ * TPC + i
                            v.scalar_tensor_tensor(out=col(x_cur, t * D, D), in0=bo_rows[:, bass.ds(ex, 1), :].rearrange("p a d -> p (a d)"),
                                                   scalar=col(gate, t * MOE + ex), in1=col(x_cur, t * D, D),
                                                   op0=ALU.mult, op1=ALU.add)
                        v.drain()
                        for i in range(TPC):
                            t = c_ * TPC + i
                            v.wait_ge(y_done, 5 * (ex * CHUNKS + c_) + i + 1)
                            own(v, "dve")
                            v.scalar_tensor_tensor(out=col(x_cur, t * D, D), in0=ps[4 + i % 4][0:P, 0:D],
                                                   scalar=col(gate, t * MOE + ex), in1=col(x_cur, t * D, D),
                                                   op0=ALU.mult, op1=ALU.add).then_inc(y_out, 1)
                        v.drain()
            phase_end(v, 5)
            ln[2].vector(v)
            v.drain()
            ln[3].stats(v)
            ln[3].moments(v)
            v.wait_ge(fold_mm, 1)
            for oc in range(2):
                for q in range(3):
                    for ic in range(2):
                        v.tensor_copy(w_qkv1[:, ic, q * D + oc * 128:q * D + (oc + 1) * 128],
                                      ps[2 * oc + ic][:, q * 128:(q + 1) * 128])
                    v.tensor_copy(bias1[:, q * D + oc * 128:q * D + (oc + 1) * 128], ps[4 + oc][0:P, q * 128:(q + 1) * 128])
            phase_end(v, 6)
            step = msg[1].vector_step
            msg[1].vector_start(v)
            ln[3].woven_vector(v, step, 0)
            job_end(v, 2)
            att1.woven_vector(v, step, ATT1_AT)
            job_end(v, 3)

            def out3(t, u):
                v.wait_ge(prj3.product.sem, prj3.product.base + t + 3)
                v.tensor_tensor(p3_tmp[:, u, :], prj3.out(u), b_o1, ALU.add)
                v.drain().then_inc(prj3.used.sem, 1)
                v.tensor_tensor(col(rows, t * D, D), col(xn, t * D, D), p3_tmp[:, u, :], ALU.add)
                v.drain()
                v.bn_stats(out=col(ln[4].st, t * 6, 6), in_=col(rows, t * D, D))
            prj3.woven_vector(v, step, PRJ3_AT, out3)
            v.drain()
            ln[4].moments(v)
            job_end(v, 4)
            ln[4].woven_vector(v, step, LN4_AT)
            job_end(v, 5)
            v.wait_ge(mlp_loaded, 64)
            v.sem_inc(m2_out, 5)

            def add_mlp(c_, i):
                t = c_ * TPC + i
                v.wait_ge(m2_mm, 5 * c_ + i + 1)
                v.tensor_tensor(m_o[:, i % 2, :], ps[6 + i % 2][0:P, 0:D], b_m2, ALU.add)
                v.drain().then_inc(m2_out, 1)
                v.tensor_tensor(m_o[:, i % 2, :], m_o[:, i % 2, :], col(rows, t * D, D), ALU.add)
                v.drain()
                v.tensor_tensor(col(x_cur, t * D, D), col(x_cur, t * D, D), m_o[:, i % 2, :], ALU.add)
                v.drain()
            with v.Fori(0, CHUNKS) as c_:
                for n, (at, _, _) in enumerate(MLP_PLAN):
                    step(v, MLP_AT + MLP_TURNS * c_ + at // EB, at % EB)
                    if n and MLP_PLAN[n - 1][2] is not None:
                        add_mlp(c_, MLP_PLAN[n - 1][2])
            job_end(v, 6)
            weave(v, step, MLP_END, TURNS - 1 - MLP_END, {})
            msg[1].vector_end(v)
            phase_end(v, 7)
            v.wait_ge(asem["b"], 32)
            v.wait_ge(asem["fold_out"], 2 * REL + 3)
            for i in range(3):
                v.tensor_copy(b_part, b_all)
                v.drain()
                if i == 0:
                    v.tensor_scalar(b_parts, b_part, part_mask[:, i:i + 1], None, ALU.mult)
                else:
                    v.scalar_tensor_tensor(out=b_parts, in0=b_part, scalar=part_mask[:, i:i + 1], in1=b_parts,
                                           op0=ALU.mult, op1=ALU.add)
                v.tensor_tensor(b_all, b_all, b_part, ALU.subtract)
                v.drain()
            phase_end(v, 8)
            v.sem_inc(asem["attended"], 2)
            v.sem_inc(asem["pool_prod_used"], 2)
            s3 = scores.rearrange("p (r s h) -> p r s h", r=REL, s=REL)
            s_in = scores.rearrange("p (r s h) -> p r h s", r=REL, s=REL)
            rh = sc24.rearrange("p (r h) -> p r h", r=REL)
            rh_over = sc24.rearrange("p (r a h) -> p r a h", r=REL, a=1).broadcast_to([P, REL, REL, HEADS])

            def rel_attend(t, u, k):
                v.wait_ge(asem["qkv_out"], REL * (t + 3))
                own_rels = [r for r in range(REL) if r not in POOL_RELS]
                for i, r in enumerate(POOL_RELS):
                    v.wait_ge(asem["pool_prod"], len(POOL_RELS) * t + i + 1)
                    v.tensor_reduce(scores[:, r * 24:(r + 1) * 24], as3(pprod[:, i % 2, :], HD), AX.X, ALU.add
                                    ).then_inc(asem["pool_prod_used"], 1)
                    if i < len(own_rels):
                        r = own_rels[i]
                        v.tensor_tensor(as3(prod, D), QK[:, u, r:r + 1, 0:D].broadcast_to([P, REL, D]),
                                        QK[:, u, :, D:2 * D], ALU.mult)
                        v.drain()
                        v.tensor_reduce(scores[:, r * 24:(r + 1) * 24], as3(prod, HD), AX.X, ALU.add)
                        v.drain()
                v.drain()
                v.tensor_reduce(rh, s_in, AX.X, ALU.max)
                v.drain()
                v.tensor_tensor(s3, s3, rh_over, ALU.subtract)
                v.drain().then_inc(asem["shifted"], 1)
                v.wait_ge(asem["exp"], t + 1)
                v.tensor_reduce(rh, s_in, AX.X, ALU.add)
                v.drain()
                v.tensor_scalar(sc24, sc24, float(REL), None, ALU.mult)
                v.drain()
                v.reciprocal(sc24, sc24)
                v.drain()
                v.tensor_tensor(s3, s3, rh_over, ALU.mult)
                v.drain()
                v.tensor_reduce(pbar, scores.rearrange("p (r a) -> p a r", r=REL), AX.X, ALU.add)
                v.drain()
                v.tensor_tensor(as3(prod, HD), V[:, u, :, :].rearrange("p r (h c) -> p (r h) c", c=HD),
                                over(pbar, HD), ALU.mult)
                v.drain().then_inc(asem["attended"], 1)
                v.tensor_reduce(col(rows, t * D, D), prod.rearrange("p (s d) -> p d s", s=REL), AX.X, ALU.add)
                v.drain()
            tiles(v, rel_attend)
            phase_end(v, 9)
            v.wait_ge(prj_loaded, 64)
            v.sem_inc(prj1.used.sem, 2)

            def out1(t, u, k):
                v.wait_ge(prj1.product.sem, prj1.product.base + t + 3)
                v.tensor_tensor(prj_tmp[:, u, :], prj1.out(u), b_ao, ALU.add)
                v.drain().then_inc(prj1.used.sem, 1)
                v.tensor_tensor(col(rows, t * D, D), col(xn, t * D, D), prj_tmp[:, u, :], ALU.add)
            tiles(v, out1)
            phase_end(v, 10)
            v.sem_inc(prj2.used.sem, 2)

            def out2(t, u, k):
                v.wait_ge(prj2.product.sem, prj2.product.base + t + 3)
                v.tensor_tensor(prj_tmp[:, u, :], prj2.out(u), b_pr, ALU.add)
                v.drain().then_inc(prj2.used.sem, 1)
                v.tensor_tensor(col(x_cur, t * D, D), col(x_cur, t * D, D), prj_tmp[:, u, :], ALU.add)
            tiles(v, out2)
            phase_end(v, 11)
            ln[5].vector(v)
            v.wait_ge(ffn1_loaded, 96)
            v.wait_ge(rsem["consts"], 1)
            v.tensor_copy(e_col, e_col_i)
            v.tensor_copy(iota32, iota32_i)
            v.tensor_copy(e_number, e_number_i)
            v.drain()
            v.tensor_scalar(e_col[EH:128, :], e_col[EH:128, :], 1.0, None, ALU.add)
            v.tensor_scalar(iota32, iota32, -1.0, float(EXP), ALU.mult, ALU.add)
            v.drain()
            v.wait_ge(rsem["logits"], TILES + 5)
            l3, c3 = as3(ro_l, EXP), as3(ro_c, EXP)
            for bank, first, last in ((0, 0, RO_BANK), (1, RO_BANK, TILES)):
                n = last - first
                v.tensor_tensor(l3[:, first:last, :], as3(ps[5 + bank][0:P, 0:n * EXP], EXP),
                                b_ro.unsqueeze(1).broadcast_to([P, n, EXP]), ALU.add)
            v.drain()
            v.tensor_reduce(ro_m, l3, AX.X, ALU.max)
            v.drain()
            v.tensor_tensor(c3, l3, over(ro_m, EXP), ALU.is_equal)
            v.drain()
            v.tensor_tensor(c3, c3, iota32.unsqueeze(1).broadcast_to([P, TILES, EXP]), ALU.mult)
            v.drain()
            v.tensor_reduce(ro_f, c3, AX.X, ALU.max)
            v.drain()
            v.tensor_scalar(ro_f, ro_f, -1.0, float(EXP), ALU.mult, ALU.add)
            v.drain()
            v.tensor_tensor(as3(ro_diag, P), ident[0:P, 0:P].unsqueeze(1).broadcast_to([P, TILES, P]), over(ro_f, P), ALU.mult)
            v.drain().then_inc(rsem["diagonal"], 1)
            v.wait_ge(rsem["numbers"], 1)
            v.tensor_scalar(ohT, idxT[0:EXP, :], e_number, None, ALU.is_equal)
            phase_end(v, 12)
            v.sem_inc(x_yout, 5)
            with v.Fori(0, CHUNKS) as c_:
                v.drain()
                v.tensor_scalar(e_hot, ohT[:, bass.ds(c_ * CHUNK, CHUNK)], 1.0, None, ALU.mult)
                v.drain()
                for j in range(32):
                    h, pc = j // 16, j % 16
                    off, n = HALVES[h]
                    v.wait_ge(x_relu, c_ * 32 + 4 + j + 1)
                    v.scalar_tensor_tensor(out=e_h[:, pc, off:off + n], in0=idxT[:, bass.ds(c_ * CHUNK + off, n)],
                                           scalar=e_col[:, pc:pc + 1], in1=e_h[:, pc, off:off + n],
                                           op0=ALU.is_equal, op1=ALU.mult).then_inc(x_masked, 1)
                for i in range(TPC):
                    t = c_ * TPC + i
                    v.wait_ge(x_y, 5 * c_ + i + 1)
                    own(v, "dve")
                    v.scalar_tensor_tensor(out=col(x_cur, t * D, D), in0=ps[4 + i % 4][0:P, 0:D], scalar=0.0,
                                           in1=col(x_cur, t * D, D), op0=ALU.max, op1=ALU.add).then_inc(x_yout, 1)
            phase_end(v, 13)


def kernel(**inputs):
    import numpy as _np
    import concourse.bacc as _bacc
    from concourse import mybir as _mybir
    from concourse.bass_utils import run_bass_kernel_spmd as _run

    a = {k: _np.ascontiguousarray(v) for k, v in inputs.items()}

    def cols(v):
        return v.reshape(-1, 2, 128).transpose(2, 0, 1).reshape(128, -1)

    lay = {n: a[n] for n in ("x", "src", "dst", "edge_type_6", "edge_weight", "L0_gnn_ln2_g", "L0_gnn_ln2_b",
                             "L0_mix_Wqkv", "L0_mix_Wout", "L0_mix_gamma", "L0_ffn_Wr", "L0_ffn_br",
                             "L1_gnn_in_proj_b", "L1_gnn_attn_out_b", "L1_gnn_proj_b", "L1_mix_Wx", "L1_mix_bo",
                             "L1_mix_b2", "L1_ffn_router_b", "L1_ffn_b2")}
    for n in ("L0_gnn_bias", "L0_gnn_ln1_g", "L0_gnn_ln1_b", "L0_ffn_bo"):
        lay[n] = a[n].reshape(-1)
    for n in ("b1", "g1", "be1", "m1", "v1", "b2", "g2", "be2", "m2", "v2"):
        lay["L0_ffn_" + n] = cols(a["L0_ffn_" + n])
    for n in ("W1", "W2", "Wo"):
        lay["L0_ffn_" + n] = a["L0_ffn_" + n].reshape(-1, 256)
    lay["gnn0_W"] = a["L0_gnn_W"].transpose(1, 0, 2).reshape(256, 256)
    lay["gnn1_W_T"] = a["L1_gnn_W"].transpose(2, 0, 1).reshape(256, -1)
    lay["gnn1_b_T"] = _np.tile(a["L1_gnn_b"].T, (1, 6))
    product = _np.concatenate([_np.arange(36) // 6, _np.arange(6)])
    relation = _np.concatenate([_np.arange(36) % 6, _np.full(6, -1)])
    lay["rel_masks"] = _np.concatenate([(relation[:, None] == _np.arange(6)) | (relation[:, None] < 0),
                                        product[:, None] % 3 == _np.arange(3)], axis=1).astype(_np.float32)
    lay["gnn1_in_T"] = a["L1_gnn_in_proj_w"].T
    lay["gnn1_ao_T"] = a["L1_gnn_attn_out_w"].T
    lay["gnn1_pr_T"] = a["L1_gnn_proj_w"].T
    for n in ("ln1_w", "ln1_b", "ln2_w", "ln2_b", "bx"):
        lay["mix1_" + n] = cols(a["L1_mix_" + n])
    lay["mix1_b1"] = a["L1_mix_b1"].reshape(8, 128).T
    for n in ("Wq", "Wk", "Wv", "Wo", "W1", "W2"):
        lay[f"mix1_{n}_T"] = a["L1_mix_" + n].T
    lay["ffn1_W1"] = a["L1_ffn_W1"].transpose(1, 0, 2).reshape(256, -1)
    lay["ffn1_W2"] = a["L1_ffn_W2"].reshape(-1, 256)
    lay["ffn1_b1"] = a["L1_ffn_b1"].reshape(16, 128).T
    lay["ffn1_router_T"] = a["L1_ffn_router_w"].T

    nc = _bacc.Bacc("TRN2", target_bir_lowering=False, num_devices=1)
    arrays, aps = {}, {}
    for n, v in lay.items():
        v = _np.ascontiguousarray(v)
        arrays["in_" + n] = v
        aps[n] = nc.dram_tensor("in_" + n, v.shape, _mybir.dt.from_np(v.dtype), kind="ExternalInput").ap()
    out = nc.dram_tensor("out_rows", (3125, 256), _mybir.dt.float32, kind="ExternalOutput").ap()
    gps_two_layers(nc, aps, out)
    r = _run(nc, [arrays], core_ids=[0])
    return r.results[0]["out_rows"]
```
